# Optimizing a Trainium2 kernel written in Bass

```python
import numpy as np
import jax
import jax.numpy as jnp

def _softmax(x, axis=-1):
    return jax.nn.softmax(x, axis=axis)

def _gelu(x):
    return jax.nn.gelu(x, approximate=True)

def _silu(x):
    return jax.nn.silu(x)

def _sigmoid(x):
    return jax.nn.sigmoid(x)

def _layernorm(x, axis=-1, eps=1e-05):
    m = jnp.mean(x, axis=axis, keepdims=True)
    v = jnp.var(x, axis=axis, keepdims=True)
    return (x - m) / jnp.sqrt(v + eps)

def _scatter_add(tgt, idx, src, axis=0):
    return tgt.at[idx].add(src)

def _segment_sum(src, seg, n):
    return jax.ops.segment_sum(src, seg, n)
kernel_name = 'mk_sandwich_d1_jaxref_r8_c08c96'

def setup_inputs(seed: int=0):
    np.random.seed(seed)
    _w = jnp.asarray

    def _L0_attn_setup():
        import jax, jax.numpy as jnp
        import numpy as np
        B, L, D = (2, 256, 128)
        H, HD = (16, 64)
        LD = 32
        key = jax.random.key(seed)
        ks = jax.random.split(key, 6)
        s = lambda fan_in: 1.0 / np.sqrt(fan_in)
        x_bld = jax.random.normal(ks[0], (B, L, D), dtype=jnp.float32)
        Wq = jax.random.normal(ks[1], (D, H, HD), dtype=jnp.float32) * s(D)
        Wkv_down = jax.random.normal(ks[2], (D, LD), dtype=jnp.float32) * s(D)
        Wk_up = jax.random.normal(ks[3], (LD, H, HD), dtype=jnp.float32) * s(LD)
        Wv_up = jax.random.normal(ks[4], (LD, H, HD), dtype=jnp.float32) * s(LD)
        Wout = jax.random.normal(ks[5], (H, HD, D), dtype=jnp.float32) * s(H * HD)
        return {'x_bld': x_bld, 'Wq': Wq, 'Wkv_down': Wkv_down, 'Wk_up': Wk_up, 'Wv_up': Wv_up, 'Wout': Wout}
    _L0_attn_in = _L0_attn_setup()

    def _L0_ffn_setup():
        import jax, jax.numpy as jnp
        import numpy as np
        from math import sqrt
        B, S, D, H, E, K, FF = (2, 128, 128, 16, 8, 2, 512)
        HD = D // H
        EPS = 1e-05

        def _rope_cache(seq_len, hd):
            inv_freq = 1.0 / 10000.0 ** (jnp.arange(0, hd, 2, dtype=jnp.float32) / hd)
            t = jnp.arange(seq_len, dtype=jnp.float32)
            freqs = t[:, None] * inv_freq[None, :]
            emb = jnp.concatenate([freqs, freqs], axis=-1)
            return (jnp.cos(emb), jnp.sin(emb))

        def _rotate_half(x):
            x1, x2 = jnp.split(x, 2, axis=-1)
            return jnp.concatenate([-x2, x1], axis=-1)

        def _layernorm(x, g, b):
            m = jnp.mean(x, axis=-1, keepdims=True)
            v = jnp.var(x, axis=-1, keepdims=True)
            return (x - m) * jax.lax.rsqrt(v + EPS) * g + b

        def _forward(x, Wq, bq, Wk, bk, Wv, bv, Wo, bo, Wg, bg, W1, b1, W2, b2, g1, be1, g2, be2):
            bsz, seq, d = x.shape
            q = (x @ Wq + bq).reshape(bsz, seq, H, HD).transpose(0, 2, 1, 3)
            k = (x @ Wk + bk).reshape(bsz, seq, H, HD).transpose(0, 2, 1, 3)
            v = (x @ Wv + bv).reshape(bsz, seq, H, HD).transpose(0, 2, 1, 3)
            cos, sin = _rope_cache(seq, HD)
            cos = cos[None, None]
            sin = sin[None, None]
            q = q * cos + _rotate_half(q) * sin
            k = k * cos + _rotate_half(k) * sin
            scores = jnp.einsum('bhqd,bhkd->bhqk', q, k) / sqrt(HD)
            attn = jax.nn.softmax(scores, axis=-1)
            ao = jnp.einsum('bhqk,bhkd->bhqd', attn, v)
            ao = ao.transpose(0, 2, 1, 3).reshape(bsz, seq, d)
            attn_out = ao @ Wo + bo
            x1 = _layernorm(x + attn_out, g1, be1)
            gate_logits = x1 @ Wg + bg
            gate_probs = jax.nn.softmax(gate_logits, axis=-1)
            topk_p, topk_i = jax.lax.top_k(gate_probs, K)
            topk_p = topk_p / jnp.sum(topk_p, axis=-1, keepdims=True)
            comb = jnp.sum(jax.nn.one_hot(topk_i, E, dtype=x.dtype) * topk_p[..., None], axis=-2)
            h = jax.nn.gelu(jnp.einsum('bsd,edf->bsef', x1, W1) + b1, approximate=False)
            y = jnp.einsum('bsef,efd->bsed', h, W2) + b2
            moe_out = jnp.einsum('bse,bsed->bsd', comb, y)
            return _layernorm(x1 + moe_out, g2, be2)
        key = jax.random.key(seed)
        ks = jax.random.split(key, 20)
        std = 0.02
        p = lambda k, sh: jax.random.normal(k, sh, dtype=jnp.float32) * std
        return {'x': jax.random.normal(ks[0], (B, S, D), dtype=jnp.float32), 'Wq': p(ks[1], (D, D)), 'bq': jnp.zeros((D,), jnp.float32), 'Wk': p(ks[2], (D, D)), 'bk': jnp.zeros((D,), jnp.float32), 'Wv': p(ks[3], (D, D)), 'bv': jnp.zeros((D,), jnp.float32), 'Wo': p(ks[4], (D, D)), 'bo': jnp.zeros((D,), jnp.float32), 'Wg': p(ks[5], (D, E)), 'bg': jnp.zeros((E,), jnp.float32), 'W1': p(ks[6], (E, D, FF)), 'b1': jnp.zeros((E, FF), jnp.float32), 'W2': p(ks[7], (E, FF, D)), 'b2': jnp.zeros((E, D), jnp.float32), 'g1': jnp.ones((D,), jnp.float32), 'be1': jnp.zeros((D,), jnp.float32), 'g2': jnp.ones((D,), jnp.float32), 'be2': jnp.zeros((D,), jnp.float32)}
    _L0_ffn_in = _L0_ffn_setup()
    _d = {'L0_attn_x_bld': _L0_attn_in['x_bld'], 'L0_attn_Wq': _L0_attn_in['Wq'], 'L0_attn_Wkv_down': _L0_attn_in['Wkv_down'], 'L0_attn_Wk_up': _L0_attn_in['Wk_up'], 'L0_attn_Wv_up': _L0_attn_in['Wv_up'], 'L0_attn_Wout': _L0_attn_in['Wout'], 'L0_ffn_Wq': _L0_ffn_in['Wq'], 'L0_ffn_bq': _L0_ffn_in['bq'], 'L0_ffn_Wk': _L0_ffn_in['Wk'], 'L0_ffn_bk': _L0_ffn_in['bk'], 'L0_ffn_Wv': _L0_ffn_in['Wv'], 'L0_ffn_bv': _L0_ffn_in['bv'], 'L0_ffn_Wo': _L0_ffn_in['Wo'], 'L0_ffn_bo': _L0_ffn_in['bo'], 'L0_ffn_Wg': _L0_ffn_in['Wg'], 'L0_ffn_bg': _L0_ffn_in['bg'], 'L0_ffn_W1': _L0_ffn_in['W1'], 'L0_ffn_b1': _L0_ffn_in['b1'], 'L0_ffn_W2': _L0_ffn_in['W2'], 'L0_ffn_b2': _L0_ffn_in['b2'], 'L0_ffn_g1': _L0_ffn_in['g1'], 'L0_ffn_be1': _L0_ffn_in['be1'], 'L0_ffn_g2': _L0_ffn_in['g2'], 'L0_ffn_be2': _L0_ffn_in['be2']}
    _x0 = _d['L0_attn_x_bld']
    _d['L0_attn_x_bld'] = jax.random.normal(jax.random.fold_in(jax.random.key(seed), 1), (4, 1024, 128), dtype=_x0.dtype)
    del _x0
    return _d

def reference(L0_attn_x_bld, L0_attn_Wq, L0_attn_Wkv_down, L0_attn_Wk_up, L0_attn_Wv_up, L0_attn_Wout, L0_ffn_Wq, L0_ffn_bq, L0_ffn_Wk, L0_ffn_bk, L0_ffn_Wv, L0_ffn_bv, L0_ffn_Wo, L0_ffn_bo, L0_ffn_Wg, L0_ffn_bg, L0_ffn_W1, L0_ffn_b1, L0_ffn_W2, L0_ffn_b2, L0_ffn_g1, L0_ffn_be1, L0_ffn_g2, L0_ffn_be2):

    def _L0_attn_ref(x_bld, Wq, Wkv_down, Wk_up, Wv_up, Wout):
        import jax, jax.numpy as jnp
        import numpy as np
        B, L, D = (2, 256, 128)
        H, HD = (16, 64)
        LD = 32
        q_blhd = jnp.einsum('bld,dhk->blhk', x_bld, Wq)
        latent_bll = jnp.einsum('bld,dc->blc', x_bld, Wkv_down)
        k_blhd = jnp.einsum('blc,chk->blhk', latent_bll, Wk_up)
        v_blhd = jnp.einsum('blc,chk->blhk', latent_bll, Wv_up)
        attn = jnp.einsum('bqhd,bkhd->bhqk', q_blhd, k_blhd) / jnp.sqrt(jnp.asarray(HD, dtype=x_bld.dtype))
        l = x_bld.shape[1]
        mask = (jnp.arange(l)[None, :] <= jnp.arange(l)[:, None])[None, None]
        neg_inf = jnp.finfo(attn.dtype).min
        attn = jax.nn.softmax(jnp.where(mask, attn, neg_inf), axis=-1)
        y_blhd = jnp.einsum('bhqk,bkhd->bqhd', attn, v_blhd)
        return jnp.einsum('bqhd,hdo->bqo', y_blhd, Wout)

    def _L0_ffn_ref(x, Wq, bq, Wk, bk, Wv, bv, Wo, bo, Wg, bg, W1, b1, W2, b2, g1, be1, g2, be2):
        import jax, jax.numpy as jnp
        import numpy as np
        from math import sqrt
        B, S, D, H, E, K, FF = (2, 128, 128, 16, 8, 2, 512)
        HD = D // H
        EPS = 1e-05

        def _rope_cache(seq_len, hd):
            inv_freq = 1.0 / 10000.0 ** (jnp.arange(0, hd, 2, dtype=jnp.float32) / hd)
            t = jnp.arange(seq_len, dtype=jnp.float32)
            freqs = t[:, None] * inv_freq[None, :]
            emb = jnp.concatenate([freqs, freqs], axis=-1)
            return (jnp.cos(emb), jnp.sin(emb))

        def _rotate_half(x):
            x1, x2 = jnp.split(x, 2, axis=-1)
            return jnp.concatenate([-x2, x1], axis=-1)

        def _layernorm(x, g, b):
            m = jnp.mean(x, axis=-1, keepdims=True)
            v = jnp.var(x, axis=-1, keepdims=True)
            return (x - m) * jax.lax.rsqrt(v + EPS) * g + b

        def _forward(x, Wq, bq, Wk, bk, Wv, bv, Wo, bo, Wg, bg, W1, b1, W2, b2, g1, be1, g2, be2):
            bsz, seq, d = x.shape
            q = (x @ Wq + bq).reshape(bsz, seq, H, HD).transpose(0, 2, 1, 3)
            k = (x @ Wk + bk).reshape(bsz, seq, H, HD).transpose(0, 2, 1, 3)
            v = (x @ Wv + bv).reshape(bsz, seq, H, HD).transpose(0, 2, 1, 3)
            cos, sin = _rope_cache(seq, HD)
            cos = cos[None, None]
            sin = sin[None, None]
            q = q * cos + _rotate_half(q) * sin
            k = k * cos + _rotate_half(k) * sin
            scores = jnp.einsum('bhqd,bhkd->bhqk', q, k) / sqrt(HD)
            attn = jax.nn.softmax(scores, axis=-1)
            ao = jnp.einsum('bhqk,bhkd->bhqd', attn, v)
            ao = ao.transpose(0, 2, 1, 3).reshape(bsz, seq, d)
            attn_out = ao @ Wo + bo
            x1 = _layernorm(x + attn_out, g1, be1)
            gate_logits = x1 @ Wg + bg
            gate_probs = jax.nn.softmax(gate_logits, axis=-1)
            topk_p, topk_i = jax.lax.top_k(gate_probs, K)
            topk_p = topk_p / jnp.sum(topk_p, axis=-1, keepdims=True)
            comb = jnp.sum(jax.nn.one_hot(topk_i, E, dtype=x.dtype) * topk_p[..., None], axis=-2)
            h = jax.nn.gelu(jnp.einsum('bsd,edf->bsef', x1, W1) + b1, approximate=False)
            y = jnp.einsum('bsef,efd->bsed', h, W2) + b2
            moe_out = jnp.einsum('bse,bsed->bsd', comb, y)
            return _layernorm(x1 + moe_out, g2, be2)
        return _forward(x, Wq, bq, Wk, bk, Wv, bv, Wo, bo, Wg, bg, W1, b1, W2, b2, g1, be1, g2, be2)
    x = L0_attn_x_bld
    x = x + _layernorm(_L0_attn_ref(_layernorm(x, axis=-1), L0_attn_Wq, L0_attn_Wkv_down, L0_attn_Wk_up, L0_attn_Wv_up, L0_attn_Wout), axis=-1)
    x = x + _layernorm(_L0_ffn_ref(_layernorm(x, axis=-1), L0_ffn_Wq, L0_ffn_bq, L0_ffn_Wk, L0_ffn_bk, L0_ffn_Wv, L0_ffn_bv, L0_ffn_Wo, L0_ffn_bo, L0_ffn_Wg, L0_ffn_bg, L0_ffn_W1, L0_ffn_b1, L0_ffn_W2, L0_ffn_b2, L0_ffn_g1, L0_ffn_be1, L0_ffn_g2, L0_ffn_be2), axis=-1)
    return x

_drawn_inputs = setup_inputs


def setup_inputs(seed=0):
    import zlib

    import numpy as np

    out = dict(_drawn_inputs(seed))
    spreads = {'L0_ffn_bq': (0.0, 0.8),
     'L0_ffn_bk': (0.0, 0.8),
     'L0_ffn_bv': (0.0, 0.741),
     'L0_ffn_bo': (0.0, 0.1),
     'L0_ffn_bg': (0.0, 0.443),
     'L0_ffn_b1': (0.0, 0.8),
     'L0_ffn_b2': (0.0, 0.291),
     'L0_ffn_g1': (1.0, 0.2),
     'L0_ffn_be1': (0.0, 0.1),
     'L0_ffn_g2': (1.0, 0.2),
     'L0_ffn_be2': (0.0, 0.1)}
    factors = {'L0_ffn_Wq': 8.0,
     'L0_ffn_Wk': 8.0,
     'L0_ffn_Wv': 8.0,
     'L0_ffn_Wo': 5.352,
     'L0_ffn_W1': 3.622,
     'L0_ffn_W2': 3.234}
    for name, (base, spread) in spreads.items():
        noise = np.random.default_rng([zlib.crc32(name.encode()), seed]).standard_normal(out[name].shape)
        drawn = base * np.exp(spread * noise) if base else spread * noise
        out[name] = jnp.asarray(drawn.astype(out[name].dtype))
    for name, factor in factors.items():
        out[name] = (out[name] * factor).astype(out[name].dtype)
    return out
```

```python
from contextlib import ExitStack

import numpy as np

import concourse.bass as bass
from concourse import mybir

F32 = mybir.dt.float32
F32R = mybir.dt.float32r
BF16 = mybir.dt.bfloat16
ALU = mybir.AluOpType
ACT = mybir.ActivationFunctionType
AX = mybir.AxisListType

P = 128
B, L, D = 4, 1024, 128
NT = L // P
HALF = 512
NC = L // HALF
H = 16
HD1 = 64
LAT = 32
HD2 = D // H
GH = 4
NG = H // GH
GROUPS = B * NG
R = 32
E, FF = 8, 512
NF = FF // P
EPS = 1e-5
MASKED = -1e30
ROW_H0, ROW_H1, ROW_L, ROW_M = 0, 32, 64, 96


class Chain:

    def __init__(self, eng, sem, base, per_body):
        self.eng, self.sem, self.base, self.n, self.per_body = eng, sem, base, 0, per_body

    def did(self, instruction):
        instruction.then_inc(self.sem, 1)
        self.n += 1

    def settle(self):
        self.eng.wait_ge(self.sem, self.base + self.n)

    def close(self):
        assert self.n == self.per_body, (self.n, self.per_body)


def wait_from(eng, sem, value):
    if isinstance(value, int) and value <= 0:
        return
    eng.wait_ge(sem, value)


def wait_past(eng, sem, value):
    eng.wait_ge(sem, value + 1)


def hold(sp, sem, value, steady, steady_value, given=1):
    wait_from(sp, sem, value + given)
    sp.wait_ge(steady, steady_value)


LN_STEPS = 3 * NT + 1


def normalise(dve, chain, tiles, out_tiles, st, mv, var, std, rstd, var_ready, std_ready, nth):
    for t in range(NT):
        chain.did(dve.bn_stats(st[:, t, :], tiles(t)))
    chain.settle()
    dve.memset(rstd[:, :], 1.0)
    for t in range(NT):
        chain.did(dve.bn_aggr(mv[:, t, :], st[:, t, :]))
    chain.settle()
    dve.tensor_scalar(var[:, :], mv[:, :, 1], EPS, None, ALU.add).then_inc(var_ready, 1)
    wait_past(dve, std_ready, nth + 1)
    chain.did(dve.reciprocal(rstd[:, :], std[:, :]))
    chain.settle()
    for t in range(NT):
        chain.did(dve.tensor_scalar(out_tiles(t), tiles(t), mv[:, t, 0:1], rstd[:, t:t + 1],
                                    ALU.subtract, ALU.mult))
    chain.settle()


def build(nc, t):
    with ExitStack() as outer:
        def sb(ctx, name, shape, dt=F32):
            return ctx.enter_context(nc.sbuf_tensor(name, shape, dt))

        def dram(name, shape):
            return nc.dram_tensor(name, shape, F32, kind="Internal").ap()

        s = {
            "q1h": dram("q1h", (GROUPS, P, L)), "q1l": dram("q1l", (GROUPS, P, L)),
            "k1h": dram("k1h", (GROUPS, LAT, L)), "k1l": dram("k1l", (GROUPS, LAT, L)),
            "v1": dram("v1", (GROUPS, P, NT, LAT)),
            "y1": dram("y1", (GROUPS, P, L)),
            "q2h": dram("q2h", (GROUPS, R, L)), "q2l": dram("q2l", (GROUPS, R, L)),
            "k2h": dram("k2h", (GROUPS, R, L)), "k2l": dram("k2l", (GROUPS, R, L)),
            "v2": dram("v2", (GROUPS, P, NT, GH, R)),
            "y2": dram("y2", (GROUPS, P, L)),
            "xmid": dram("xmid", (B, P, NT, D)), "xn2": dram("xn2", (B, P, NT, D)),
        }
        c = {
            "ident": sb(outer, "ident", [P, P]), "sel": sb(outer, "sel", [P, P]),
            "ident_b": sb(outer, "ident_b", [P, P], BF16),
            "mask_q": sb(outer, "mask_q", [P, P], BF16), "mask_k": sb(outer, "mask_k", [P, P], BF16),
            "wy1": sb(outer, "wy1", [P, NG, D]),
            "ones": sb(outer, "ones", [P, R]),
        }
        prepare_first(nc, t, s, c)
        attend(nc, "a", True, s["q1h"], s["q1l"], s["k1h"], s["k1l"], s["v1"], s["y1"],
               float(HD1) ** -0.5, t, c)
        prepare_second(nc, t, s, c)
        attend(nc, "f", False, s["q2h"], s["q2l"], s["k2h"], s["k2l"], s["v2"], s["y2"],
               float(HD2) ** -0.5, t, c)
        experts(nc, t, s, c)


def prepare_first(nc, t, s, c):
    with ExitStack() as ctx:
        def sb(name, shape, dt=F32):
            return ctx.enter_context(nc.sbuf_tensor(name, shape, dt))

        def sem(name):
            return ctx.enter_context(nc.semaphore(name))

        wq_t = sb("wq_t", [HD1, H, D])
        wk_t = sb("wk_t", [HD1, H, LAT])
        wv_t = sb("wv_t", [HD1, H, LAT])
        wout = sb("wout", [HD1, H, D])
        wkv = sb("wkv", [D, LAT])
        masks = sb("masks", [P, 2, P])
        wqk = sb("wqk", [D, H, LAT])
        x = sb("x1_in", [P, NT, D])
        xn = sb("x1_n", [P, NT, D])
        x_t = sb("x1_t", [D, L])
        st = sb("st1", [P, NT, 6])
        mv = sb("mv1", [P, NT, 2])
        var = sb("var1", [P, NT])
        std = sb("std1", [P, NT])
        rstd = sb("rstd1", [P, NT])
        q_hi = sb("q1_hi", [P, 2, L], F32R)
        q_lo = sb("q1_lo", [P, 2, L], F32R)
        k_hi = sb("k1_hi", [LAT, L], F32R)
        k_lo = sb("k1_lo", [LAT, L], F32R)
        lat = sb("lat1", [P, NT, LAT])
        ps_t = ctx.enter_context(nc.psum_tensor("ps1_t", [P, 2, HALF], F32))
        ps_q = ctx.enter_context(nc.psum_tensor("ps1_q", [P, 2, HALF], F32))
        ps_k = ctx.enter_context(nc.psum_tensor("ps1_k", [P, 2, HALF], F32))
        ps_v = ctx.enter_context(nc.psum_tensor("ps1_v", [P, HALF], F32))
        ps_w = ctx.enter_context(nc.psum_tensor("ps1_w", [P, HALF], F32))

        weights_in = sem("a1_weights_in")
        consts_made = sem("a1_consts_made")
        wqk_made = sem("a1_wqk_made")
        wqk_copied = sem("a1_wqk_copied")
        wy_made = sem("a1_wy_made")
        wy_copied = sem("a1_wy_copied")
        x_in = sem("a1_x_in")
        steps = sem("a1_steps")
        var_ready = sem("a1_var_ready")
        std_ready = sem("a1_std_ready")
        xn_ready = sem("a1_xn_ready")
        turned = sem("a1_turned")
        xt_ready = sem("a1_xt_ready")
        q_made = sem("a1_q_made")
        q_hi_ready = sem("a1_q_hi_ready")
        q_lo_ready = sem("a1_q_lo_ready")
        k_made = sem("a1_k_made")
        k_hi_ready = sem("a1_k_hi_ready")
        k_lo_ready = sem("a1_k_lo_ready")
        v_made = sem("a1_v_made")
        lat_ready = sem("a1_lat_ready")
        q_out = [sem(f"a1_q_out{i}") for i in range(2)]
        kv_out = sem("a1_kv_out")
        given = sem("a1_given")
        block = ctx.enter_context(nc.Block())
        NW = 9
        NQ = NG * NC

        @block.sync
        def _(sp):
            sp.wait_ge(given, 1)
            sp.dma_start(wq_t[:, :, :], t["wq_t"]).then_inc(weights_in, 16)
            sp.dma_start(wk_t[:, :, :], t["wk_t"]).then_inc(weights_in, 16)
            sp.dma_start(wv_t[:, :, :], t["wv_t"]).then_inc(weights_in, 16)
            sp.dma_start(wout[:, :, :], t["wout"]).then_inc(weights_in, 16)
            sp.dma_start(wkv[:, :], t["wkv"]).then_inc(weights_in, 16)
            sp.dma_start(c["ident"][:, :], t["ident"]).then_inc(weights_in, 16)
            sp.dma_start(c["sel"][:, :], t["sel"]).then_inc(weights_in, 16)
            sp.dma_start(masks[:, 0, :], t["mask_q"]).then_inc(weights_in, 16)
            sp.dma_start(masks[:, 1, :], t["mask_k"]).then_inc(weights_in, 16)
            with sp.Fori(0, B) as b:
                hold(sp, xn_ready, b, weights_in, 16 * NW)
                sp.dma_start(x[:, :, :], t["x"][b].rearrange("(t p) d -> p t d", p=P)).then_inc(x_in, 16)
                hold(sp, k_lo_ready, NC * b + NC, weights_in, 16 * NW)
                for g in range(NG):
                    sp.dma_start(s["k1h"][b * NG + g], k_hi[:, :].bitcast(F32)).then_inc(kv_out, 16)
                    sp.dma_start(s["k1l"][b * NG + g], k_lo[:, :].bitcast(F32)).then_inc(kv_out, 16)
                hold(sp, lat_ready, b + 1, weights_in, 16 * NW)
                for g in range(NG):
                    sp.dma_start(s["v1"][b * NG + g], lat[:, :, :]).then_inc(kv_out, 16)
                for g in range(NG):
                    hold(sp, q_lo_ready, NQ * b + NC * (g + 1), weights_in, 16 * NW)
                    sp.dma_start(s["q1h"][b * NG + g], q_hi[:, g % 2, :].bitcast(F32)).then_inc(q_out[g % 2], 16)
                    sp.dma_start(s["q1l"][b * NG + g], q_lo[:, g % 2, :].bitcast(F32)).then_inc(q_out[g % 2], 16)
            hold(sp, kv_out, 16 * 3 * GROUPS, weights_in, 16 * NW)
            for i in range(2):
                hold(sp, q_out[i], 16 * GROUPS, weights_in, 16 * NW)

        @block.vector
        def _(dve):
            dve.wait_ge(given, 1)
            dve.memset(c["ones"][:, :], 1.0).then_inc(consts_made, 1)
            dve.wait_ge(weights_in, 16 * NW)
            dve.tensor_copy(c["ident_b"][:, :], c["ident"][:, :]).then_inc(consts_made, 1)
            dve.tensor_copy(c["mask_q"][:, :], masks[:, 0, :]).then_inc(consts_made, 1)
            dve.tensor_copy(c["mask_k"][:, :], masks[:, 1, :]).then_inc(consts_made, 1)
            dve.wait_ge(consts_made, 4)
            with dve.Fori(0, B) as b:
                chain = Chain(dve, steps, b * LN_STEPS, LN_STEPS)
                wait_past(dve, x_in, 16 * b + 16)
                wait_past(dve, turned, 2 * b)
                normalise(dve, chain, lambda i: x[:, i, :], lambda i: xn[:, i, :],
                          st, mv, var, std, rstd, var_ready, std_ready, b)
                chain.close()
                dve.sem_inc(xn_ready, 1)
                wait_past(dve, kv_out, 16 * 3 * NG * b)
                for i in range(NC):
                    wait_past(dve, k_hi_ready, NC * b + i + 1)
                    sl = slice(i * HALF, (i + 1) * HALF)
                    dve.tensor_tensor(k_lo[:, sl], ps_k[0:LAT, i, :], k_hi[:, sl].bitcast(F32),
                                      ALU.subtract).then_inc(k_lo_ready, 1)
                for n in range(NQ):
                    g, i = n // NC, n % NC
                    wait_past(dve, q_hi_ready, NQ * b + n + 1)
                    sl = slice(i * HALF, (i + 1) * HALF)
                    dve.tensor_tensor(q_lo[:, g % 2, sl], ps_q[:, i, :], q_hi[:, g % 2, sl].bitcast(F32),
                                      ALU.subtract).then_inc(q_lo_ready, 1)

        @block.gpsimd
        def _(pool):
            for count in (x_in, var_ready, std_ready, xn_ready, turned, xt_ready, q_made, q_hi_ready,
                          q_lo_ready, k_made, k_hi_ready, k_lo_ready, v_made,
                          lat_ready, kv_out, *q_out):
                pool.sem_inc(count, 1)
            pool.sem_inc(given, 1)
            pool.wait_ge(given, 1)

        @block.scalar
        def _(act):
            act.wait_ge(given, 1)
            act.wait_ge(wqk_made, 1)
            nc.scalar.copy(wqk[:, :, :], ps_w[:, :].rearrange("d (h c) -> d h c", h=H)).then_inc(wqk_copied, 1)
            act.wait_ge(wy_made, 1)
            nc.scalar.copy(c["wy1"][:, :, :], ps_w[:, :].rearrange("r (g d) -> r g d", g=NG)).then_inc(wy_copied, 1)
            with act.Fori(0, B) as b:
                wait_past(act, var_ready, b + 1)
                nc.scalar.activation(std[:, :], var[:, :], ACT.Sqrt).then_inc(std_ready, 1)
                for i in range(2):
                    wait_past(act, turned, 2 * b + i + 1)
                    if i == 0:
                        wait_past(act, q_made, NQ * b)
                    nc.scalar.copy(x_t[:, i * HALF:(i + 1) * HALF], ps_t[:, i, :]).then_inc(xt_ready, 1)
                wait_past(act, kv_out, 16 * 3 * NG * b)
                for i in range(NC):
                    wait_past(act, k_made, NC * b + i + 1)
                    nc.scalar.copy(k_hi[:, i * HALF:(i + 1) * HALF], ps_k[0:LAT, i, :]).then_inc(k_hi_ready, 1)
                wait_past(act, v_made, b + 1)
                nc.scalar.copy(lat[:, :, :], ps_v[:, 0:NT * LAT].rearrange("p (t c) -> p t c", t=NT))\
                    .then_inc(lat_ready, 1)
                for n in range(NQ):
                    g, i = n // NC, n % NC
                    if i == 0:
                        wait_past(act, q_out[g % 2], 16 * 2 * (2 * b + g // 2))
                    wait_past(act, q_made, NQ * b + n + 1)
                    nc.scalar.copy(q_hi[:, g % 2, i * HALF:(i + 1) * HALF], ps_q[:, i, :]).then_inc(q_hi_ready, 1)

        @block.tensor
        def _(pe):
            pe.wait_ge(given, 1)
            pe.wait_ge(weights_in, 16 * NW)
            for h in range(H):
                last = pe.matmul(ps_w[:, h * LAT:(h + 1) * LAT], wq_t[:, h, :], wk_t[:, h, :],
                                 start=True, stop=True)
            last.then_inc(wqk_made, 1)
            pe.wait_ge(wqk_copied, 1)
            for h in range(H):
                j, g = h % GH, h // GH
                last = pe.matmul(ps_w[R * j:R * j + R, g * D:(g + 1) * D], wv_t[:, h, :], wout[:, h, :],
                                 start=True, stop=True)
            last.then_inc(wy_made, 1)
            with pe.Fori(0, B) as b:
                wait_past(pe, xn_ready, b + 1)
                wait_past(pe, xt_ready, 2 * b)
                for i in range(NT):
                    tr = pe.transpose(ps_t[:, i // 4, (i % 4) * P:(i % 4 + 1) * P], xn[:, i, :], c["ident"][:, :])
                    if i % 4 == 3:
                        tr.then_inc(turned, 1)
                wait_past(pe, xt_ready, 2 * b + 2)
                wait_past(pe, k_lo_ready, NC * b)
                for i in range(NC):
                    pe.matmul(ps_k[0:LAT, i, :], wkv[:, :], x_t[:, i * HALF:(i + 1) * HALF],
                              start=True, stop=True).then_inc(k_made, 1)
                wait_past(pe, lat_ready, b)
                for i in range(NT):
                    last = pe.matmul(ps_v[:, i * LAT:(i + 1) * LAT], x_t[:, i * P:(i + 1) * P], wkv[:, :],
                                     start=True, stop=True)
                last.then_inc(v_made, 1)
                for n in range(NQ):
                    g, i = n // NC, n % NC
                    if n >= 2:
                        wait_past(pe, q_lo_ready, NQ * b + n - 1)
                    else:
                        wait_past(pe, q_lo_ready, NQ * b)
                    pe.matmul(ps_q[:, i, :], wqk[:, g * GH:(g + 1) * GH, :], x_t[:, i * HALF:(i + 1) * HALF],
                              start=True, stop=True).then_inc(q_made, 1)
            pe.wait_ge(wy_copied, 1)


def attend(nc, tag, causal, q_hi_d, q_lo_d, k_hi_d, k_lo_d, v_d, y_d, scale, t, c):
    TILES = [(ch, k) for ch in range(NC) for k in range((ch + 1) * NT // NC if causal else NT)]
    NCT = len(TILES)
    ENDS = [max(n for n, x in enumerate(TILES) if x[0] == ch) for ch in range(NC)]
    UNITS = [(i, j, kk) for i in range(NT) for kk in range(i // 4 + 1 if causal else NC) for j in range(GH)]
    NU = len(UNITS)
    NWK = NU + 2
    FIRST = 2
    SPAN = 8 if causal else 11
    PER = -(-NU // SPAN)
    LASTU = FIRST + SPAN - 1
    NP = 4
    NLOAD = 6 if causal else 3 + 3 * GH
    KROWS = ROW_M + (1 if causal else GH)
    assert NCT % NP == 0 and NWK % 2 == 0 and LASTU + 1 < NCT

    with ExitStack() as ctx:
        def sb(name, shape, dt=F32):
            return ctx.enter_context(nc.sbuf_tensor(f"{tag}_{name}", shape, dt))

        def sem(name):
            return ctx.enter_context(nc.semaphore(f"{tag}_{name}"))

        many = [sb(f"many{i}", [P, GH, L], F32R) for i in range(2)]
        one = [sb(f"one{i}", [P, L], F32R) for i in range(2)]
        v = [sb(f"v{i}", [P, NT, R if causal else GH * R]) for i in range(2)]
        rows = sb("rows", [P, L if causal else GH * L])
        probs = sb("probs", [P, NP, GH, HALF])
        y = sb("y", [P, NC, HALF])
        rec = sb("rec", [P, HALF])
        raw = sb("raw", [P, HALF])
        part_max = sb("part_max", [P, NT, GH, NC])
        neg_max = sb("neg_max", [P, NT, ROW_M + GH])
        ps_s = ctx.enter_context(nc.psum_tensor(f"{tag}_ps_s", [P, 2, 2, HALF], F32))
        ps_w = ctx.enter_context(nc.psum_tensor(f"{tag}_ps_w", [P, 2, HALF], F32))
        ps_o = ctx.enter_context(nc.psum_tensor(f"{tag}_ps_o", [P, HALF], F32))
        ps_d = ctx.enter_context(nc.psum_tensor(f"{tag}_ps_d", [P, HALF], F32))

        filled = sem("filled")
        rows_in = sem("rows_in")
        operands_in = [sem(f"operands_in{i}") for i in range(2)]
        v_in = [sem(f"v_in{i}") for i in range(2)]
        work_full = sem("work_full")
        work_free = sem("work_free")
        neg_ready = sem("neg_ready")
        max_in = sem("max_in")
        scores_ready = sem("scores_ready")
        exp_done = sem("exp_done")
        pv_done = sem("pv_done")
        raw_ready = sem("raw_ready")
        den_ready = sem("den_ready")
        rec_ready = sem("rec_ready")
        y_ready = sem("y_ready")
        y_out = [sem(f"y_out{i}") for i in range(NC)]
        block = ctx.enter_context(nc.Block())
        NFILL = 4 if causal else 6

        def units_at(k):
            n0 = (k - FIRST) * PER
            return range(max(n0, 0), min(max(n0 + PER, 0), NU))

        def first_col(ch, k):
            return max(0, (k - ch * 4) * P) if causal else 0

        def run_steps(eng, step):
            step(0, 0, 0, False, True)
            step(1, 0, 1, True, True)
            with eng.Fori(1, GROUPS // 2 - 1) as it:
                step(it * 2, it, 0, True, True)
                step(it * 2 + 1, it, 1, True, True)
            step(GROUPS - 2, GROUPS // 2 - 1, 0, True, True)
            step(GROUPS - 1, GROUPS // 2 - 1, 1, True, False)

        @block.sync
        def _(sp):
            def load_operands(g, par):
                if causal:
                    heads = q_hi_d[g].rearrange("(j r) n -> r j n", j=GH)
                    lows = q_lo_d[g].rearrange("(j r) n -> r j n", j=GH)
                    pairs = [(many[par][ROW_H0:ROW_H0 + R, :, :], heads), (many[par][ROW_H1:ROW_H1 + R, :, :], heads),
                             (many[par][ROW_L:ROW_L + R, :, :], lows),
                             (one[par][ROW_H0:ROW_H0 + R, :], k_hi_d[g]), (one[par][ROW_H1:ROW_H1 + R, :], k_lo_d[g]),
                             (one[par][ROW_L:ROW_L + R, :], k_hi_d[g])]
                else:
                    pairs = [(one[par][ROW_H0:ROW_H0 + R, :], q_hi_d[g]), (one[par][ROW_H1:ROW_H1 + R, :], q_hi_d[g]),
                             (one[par][ROW_L:ROW_L + R, :], q_lo_d[g])]
                    for j in range(GH):
                        own = slice(j * HD2, (j + 1) * HD2)
                        for row, src in ((ROW_H0, k_hi_d), (ROW_H1, k_lo_d), (ROW_L, k_hi_d)):
                            pairs.append((many[par][row + j * HD2:row + (j + 1) * HD2, j, :], src[g, own, :]))
                assert len(pairs) == NLOAD
                for dst, src in pairs:
                    sp.dma_start(dst.bitcast(F32), src).then_inc(operands_in[par], 16)

            def load_v(g, par):
                src = v_d[g] if causal else v_d[g].rearrange("p t j r -> p t (j r)")
                sp.dma_start(v[par][:, :, :], src).then_inc(v_in[par], 16)

            def place_max(g, par):
                hold(sp, work_free, g * NWK + NWK, filled, NFILL, 0)
                for j in range(GH):
                    sp.dma_start(many[par][ROW_M:ROW_M + 1, j, :].bitcast(F32),
                                 rows[ROW_M + j:ROW_M + j + 1, :]).then_inc(max_in, 16)

            def store(s, ch):
                hold(sp, y_ready, s * NC + ch + 1, filled, NFILL, 0)
                sp.dma_start(y_d[s][:, ch * HALF:(ch + 1) * HALF], y[:, ch, :]).then_inc(y_out[ch], 16)

            def step(s, half, par, has_prev, has_next):
                if has_next:
                    hold(sp, pv_done, s * NCT, filled, NFILL, 0)
                    load_v(s + 1, 1 - par)
                if has_prev:
                    store(s - 1, 1)
                store(s, 0)
                if has_next and causal:
                    place_max(s + 1, 1 - par)
                if not (isinstance(s, int) and s >= GROUPS - 2):
                    hold(sp, scores_ready, (s + 1) * 2 * NCT, filled, NFILL, 0)
                    load_operands(s + 2, par)

            if not causal:
                sp.dma_start(rows[ROW_M:ROW_M + GH, :], t["head_rows"]).then_inc(rows_in, 16)
            sp.wait_ge(filled, NFILL)
            load_operands(0, 0)
            load_v(0, 0)
            load_operands(1, 1)
            if causal:
                place_max(0, 0)
            run_steps(sp, step)
            store(GROUPS - 1, 1)
            for ch in range(NC):
                hold(sp, y_out[ch], 16 * GROUPS, filled, NFILL, 0)

        @block.tensor
        def _(pe):
            def max_unit(g, half_g, par, n):
                i, j, kk = UNITS[n]
                diag = causal and kk == i // 4
                off = (i % 4) * P
                width = off + P if diag else HALF
                wait_from(pe, work_free, g * NWK + n - 1)
                q = many[par][0:ROW_M, j, i * P:(i + 1) * P] if causal else one[par][0:ROW_M, i * P:(i + 1) * P]
                k = one[par][0:ROW_M, kk * HALF:kk * HALF + width] if causal \
                    else many[par][0:ROW_M, j, kk * HALF:kk * HALF + width]
                last = pe.matmul(ps_w[:, n % 2, 0:width], q, k, start=True, stop=not diag)
                if diag:
                    last = pe.matmul(ps_w[:, n % 2, off:width], c["ident_b"][:, :], c["mask_q"][:, :],
                                     start=False, stop=True)
                last.then_inc(work_full, 1)

            def max_start(g, half_g, par):
                pe.wait_ge(operands_in[par], (half_g + 1) * 16 * NLOAD)

            def turn_max(g):
                pe.wait_ge(neg_ready, g + 1)
                for hb in range(2):
                    wait_from(pe, work_free, g * NWK + NU + hb - 1)
                    for ii in range(4):
                        last = pe.transpose(ps_w[0:ROW_M + GH, (NU + hb) % 2, ii * P:(ii + 1) * P],
                                            neg_max[:, hb * 4 + ii, :], c["ident"][:, :])
                    last.then_inc(work_full, 1)

            def scores(s, par, k, pair):
                ch, kt = TILES[k]
                lo = first_col(ch, kt)
                diag = causal and kt >= 4 * ch
                wait_from(pe, exp_done, s * 2 * NCT + 2 * k + pair - 1)
                for jj in range(2):
                    j = 2 * pair + jj
                    cols = slice(ch * HALF + lo, (ch + 1) * HALF)
                    keys = slice(kt * P, (kt + 1) * P)
                    lhs = one[par][0:KROWS, keys] if causal else many[par][0:KROWS, j, keys]
                    rhs = many[par][0:KROWS, j, cols] if causal else one[par][0:KROWS, cols]
                    last = pe.matmul(ps_s[:, pair, jj, lo:HALF], lhs, rhs, start=True, stop=not diag)
                    if diag:
                        last = pe.matmul(ps_s[:, pair, jj, lo:lo + P], c["ident_b"][:, :], c["mask_k"][:, :],
                                         start=False, stop=True)
                last.then_inc(scores_ready, 1)

            def values(s, half, par, k):
                ch, kt = TILES[k]
                lo = first_col(ch, kt)
                stop = k in ENDS
                pe.wait_ge(exp_done, s * 2 * NCT + 2 * k + 2)
                if k == 0:
                    pe.wait_ge(v_in[par], (half + 1) * 16)
                if kt == 0:
                    wait_from(pe, y_ready if causal else raw_ready, s * NC + ch)
                for j in range(GH):
                    lhs = v[par][:, kt, :] if causal else v[par][:, kt, j * R:(j + 1) * R]
                    last = pe.matmul(ps_o[R * j:R * j + R, lo:HALF], lhs, probs[:, k % NP, j, lo:HALF],
                                     start=kt == 0, stop=stop)
                if causal:
                    for j in range(GH):
                        last = pe.matmul(ps_d[R * j:R * j + R, lo:HALF], c["ones"][:, :],
                                         probs[:, k % NP, j, lo:HALF], start=kt == 0, stop=stop)
                last.then_inc(pv_done, 1)

            def spread_den(s, ch):
                pe.wait_ge(raw_ready, s * NC + ch + 1)
                wait_from(pe, rec_ready, s * NC + ch)
                pe.matmul(ps_d[:, :], c["sel"][:, :], raw[:, :], start=True, stop=True).then_inc(den_ready, 1)

            def carried(s, half, par, k, has_prev):
                if k > 0:
                    values(s, half, par, k - 1)
                elif has_prev:
                    values(s - 1, half - 1 if par == 0 else half, 1 - par, NCT - 1)
                if not causal:
                    if k == 1 and has_prev:
                        spread_den(s - 1, 1)
                    if k == ENDS[0] + 2:
                        spread_den(s, 0)

            def step(s, half, par, has_prev, has_next):
                if causal:
                    pe.wait_ge(max_in, (s + 1) * 16 * GH)
                else:
                    pe.wait_ge(work_free, (s + 1) * NWK)
                for k in range(NCT):
                    scores(s, par, k, 0)
                    scores(s, par, k, 1)
                    if has_next:
                        half_n = half if par == 0 else half + 1
                        if k == FIRST:
                            max_start(s + 1, half_n, 1 - par)
                        for n in units_at(k):
                            max_unit(s + 1, half_n, 1 - par, n)
                        if k == LASTU + 1:
                            turn_max(s + 1)
                    carried(s, half, par, k, has_prev)

            pe.wait_ge(filled, NFILL)
            max_start(0, 0, 0)
            for n in range(NU):
                max_unit(0, 0, 0, n)
            turn_max(0)
            run_steps(pe, step)
            values(GROUPS - 1, GROUPS // 2 - 1, 1, NCT - 1)
            if not causal:
                spread_den(GROUPS - 1, 1)

        @block.scalar
        def _(act):
            def step(s, half, par, has_prev, has_next):
                for k in range(NCT):
                    ch, kt = TILES[k]
                    lo = first_col(ch, kt)
                    wait_from(act, pv_done, s * NCT + k - NP + 1)
                    for pair in range(2):
                        act.wait_ge(scores_ready, s * 2 * NCT + 2 * k + pair + 1)
                        nc.scalar.activation(probs[:, k % NP, 2 * pair:2 * pair + 2, lo:HALF],
                                             ps_s[:, pair, :, lo:HALF], ACT.Exp, scale=scale).then_inc(exp_done, 1)

            run_steps(act, step)

        @block.vector
        def _(dve):
            def max_unit(g, n):
                i, j, kk = UNITS[n]
                width = (i % 4) * P + P if causal and kk == i // 4 else HALF
                dve.wait_ge(work_full, g * NWK + n + 1)
                dve.reduce_max(part_max[:, i, j, kk:kk + 1], ps_w[:, n % 2, 0:width], AX.X).then_inc(work_free, 1)

            def negate_max(g):
                dve.wait_ge(work_free, g * NWK + NU)
                wait_from(dve, work_full, g * NWK)
                dve.tensor_reduce(neg_max[:, :, ROW_M:ROW_M + GH], part_max[:, :, :, :], AX.X, ALU.max,
                                  negate=True).then_inc(neg_ready, 1)

            def take_turned(g, par):
                if causal:
                    wait_from(dve, max_in, g * 16 * GH)
                for hb in range(2):
                    dve.wait_ge(work_full, g * NWK + NU + hb + 1)
                    sl = slice(hb * HALF, (hb + 1) * HALF)
                    src = ps_w[ROW_M:ROW_M + GH, (NU + hb) % 2, :]
                    dst = (rows[ROW_M:ROW_M + GH, sl].bitcast(F32R) if causal else one[par][ROW_M:ROW_M + GH, sl])
                    dve.tensor_copy(dst, src).then_inc(work_free, 1)

            def outputs(s, half, ch):
                dve.wait_ge(pv_done, s * NCT + ENDS[ch] + 1)
                if causal:
                    dve.reciprocal(rec[:, :], ps_d[:, :]).then_inc(rec_ready, 1)
                    dve.wait_ge(rec_ready, s * NC + ch + 1)
                    wait_from(dve, y_out[ch], s * 16)
                    dve.tensor_tensor(y[:, ch, :], ps_o[:, :], rec[:, :], ALU.mult).then_inc(y_ready, 1)
                else:
                    wait_from(dve, y_ready, s * NC + ch)
                    dve.tensor_copy(raw[:, :], ps_o[:, :]).then_inc(raw_ready, 1)

            def divide(s, half, ch):
                dve.wait_ge(den_ready, s * NC + ch + 1)
                dve.reciprocal(rec[:, :], ps_d[:, :]).then_inc(rec_ready, 1)
                dve.wait_ge(rec_ready, s * NC + ch + 1)
                wait_from(dve, y_out[ch], s * 16)
                dve.tensor_tensor(y[:, ch, :], raw[:, :], rec[:, :], ALU.mult).then_inc(y_ready, 1)

            def carried(s, half, k, has_prev):
                if k == 0 and has_prev:
                    outputs(s - 1, half, 1)
                if k == ENDS[0] + 1:
                    outputs(s, half, 0)
                if not causal:
                    if k == 1 and has_prev:
                        divide(s - 1, half, 1)
                    if k == ENDS[0] + 2:
                        divide(s, half, 0)

            def step(s, half, par, has_prev, has_next):
                for k in range(NCT):
                    if has_next:
                        for n in units_at(k):
                            max_unit(s + 1, n)
                        if k == LASTU:
                            negate_max(s + 1)
                        if k == LASTU + 1:
                            take_turned(s + 1, 1 - par)
                    carried(s, half, k, has_prev)

            dve.memset(part_max[:, :, :, :], -3e38).then_inc(filled, 1)
            dve.memset(neg_max[:, :, :], 0.0).then_inc(filled, 1)
            for i in range(2):
                if causal:
                    dve.memset(one[i][ROW_M:ROW_M + 1, :].bitcast(F32), 1.0).then_inc(filled, 1)
                else:
                    dve.memset(many[i][0:ROW_M, :, :].bitcast(F32), 0.0).then_inc(filled, 1)
                    if i == 0:
                        dve.wait_ge(rows_in, 16)
                    dve.tensor_copy(many[i][ROW_M:ROW_M + GH, :, :],
                                    rows[ROW_M:ROW_M + GH, :].rearrange("r (j n) -> r j n", j=GH)).then_inc(filled, 1)
            dve.wait_ge(filled, NFILL)
            for n in range(NU):
                max_unit(0, n)
            negate_max(0)
            take_turned(0, 0)
            run_steps(dve, step)
            outputs(GROUPS - 1, 0, 1)
            if not causal:
                divide(GROUPS - 1, 0, 1)


def prepare_second(nc, t, s, c):
    with ExitStack() as ctx:
        def sb(name, shape, dt=F32):
            return ctx.enter_context(nc.sbuf_tensor(f"m_{name}", shape, dt))

        def sem(name):
            return ctx.enter_context(nc.semaphore(f"m_{name}"))

        def bank(name, n=2):
            return ctx.enter_context(nc.psum_tensor(f"m_{name}", [P, n, HALF], F32))

        wq, wk, wv = (sb(n, [D, D]) for n in ("wq", "wk", "wv"))
        wqs, wks = (sb(n, [D, D]) for n in ("wqs", "wks"))
        bqk = sb("bqk", [D, 2, 2])
        rope = sb("rope", [D, 2, L])
        turn_a, turn_b = sb("turn_a", [D, 2, HALF]), sb("turn_b", [D, 2, HALF])
        qk = sb("qk", [D, 2, L])
        bv = sb("bv", [P, D])
        y = sb("y", [P, NG, L])
        x = sb("x", [P, NT, D])
        an = sb("an", [P, NT, D])
        xmid = sb("xmid", [P, NT, D])
        xn = sb("xn", [P, NT, D])
        x_t = sb("x_t", [D, L])
        st, mv = sb("st", [P, NT, 6]), sb("mv", [P, NT, 2])
        var, std, rstd = sb("var", [P, NT]), sb("std", [P, NT]), sb("rstd", [P, NT])
        hi = sb("hi", [P, 2, L], F32R)
        lo = sb("lo", [P, 2, L], F32R)
        v_ext = sb("v_ext", [P, NG, NT, GH, R])
        ps_a, ps_t, ps_q, ps_v = bank("ps_a"), bank("ps_t"), bank("ps_q"), bank("ps_v")

        weights_in = sem("weights_in")
        v_filled = sem("v_filled")
        y_in = sem("y_in")
        x_in = sem("x_in")
        a_made = sem("a_made")
        steps = sem("steps")
        var_ready = sem("var_ready")
        std_ready = sem("std_ready")
        xmid_ready = sem("xmid_ready")
        xn_ready = sem("xn_ready")
        turned = sem("turned")
        xt_ready = sem("xt_ready")
        q_made = sem("q_made")
        turned_by = sem("turned_by")
        roped = sem("roped")
        hi_ready = sem("hi_ready")
        lo_ready = sem("lo_ready")
        v_made = sem("v_made")
        v_ready = sem("v_ready")
        mid_out = sem("mid_out")
        qk_out = sem("qk_out")
        v_out = sem("v_out")
        given = sem("given")
        block = ctx.enter_context(nc.Block())
        NQ = 2 * NC
        NWT = 8
        STEPS = 2 * LN_STEPS + 1

        @block.sync
        def _(sp):
            sp.wait_ge(given, 1)
            sp.dma_start(wq[:, :], t["wq"]).then_inc(weights_in, 16)
            sp.dma_start(wk[:, :], t["wk"]).then_inc(weights_in, 16)
            sp.dma_start(wv[:, :], t["wv"]).then_inc(weights_in, 16)
            sp.dma_start(wqs[:, :], t["wqs"]).then_inc(weights_in, 16)
            sp.dma_start(wks[:, :], t["wks"]).then_inc(weights_in, 16)
            sp.dma_start(rope[:, :, :], t["rope"]).then_inc(weights_in, 16)
            sp.dma_start(bqk[:, :, :], t["bqk"]).then_inc(weights_in, 16)
            sp.dma_start(bv[:, :], t["bv"]).then_inc(weights_in, 16)
            with sp.Fori(0, B) as b:
                hold(sp, a_made, 2 * b, weights_in, 16 * NWT)
                for g in range(NG):
                    sp.dma_start(y[:, g, :], s["y1"][b * NG + g]).then_inc(y_in, 16)
                hold(sp, xmid_ready, b, weights_in, 16 * NWT)
                sp.dma_start(x[:, :, :], t["x"][b].rearrange("(t p) d -> p t d", p=P)).then_inc(x_in, 16)
                hold(sp, xmid_ready, b + 1, weights_in, 16 * NWT)
                sp.dma_start(s["xmid"][b], xmid[:, :, :]).then_inc(mid_out, 16)
                hold(sp, xn_ready, b + 1, weights_in, 16 * NWT)
                sp.dma_start(s["xn2"][b], xn[:, :, :]).then_inc(mid_out, 16)
                for i, (dh, dl) in enumerate((("q2h", "q2l"), ("k2h", "k2l"))):
                    hold(sp, lo_ready, NQ * b + NC * (i + 1), weights_in, 16 * NWT)
                    for g in range(NG):
                        sp.dma_start(s[dh][b * NG + g], hi[g * R:(g + 1) * R, i, :].bitcast(F32)).then_inc(qk_out, 16)
                        sp.dma_start(s[dl][b * NG + g], lo[g * R:(g + 1) * R, i, :].bitcast(F32)).then_inc(qk_out, 16)
                hold(sp, v_ready, NT * (b + 1), weights_in, 16 * NWT)
                for g in range(NG):
                    sp.dma_start(s["v2"][b * NG + g], v_ext[:, g, :, :, :]).then_inc(v_out, 16)
            hold(sp, mid_out, 16 * 2 * B, weights_in, 16 * NWT)
            hold(sp, qk_out, 16 * 4 * GROUPS, weights_in, 16 * NWT)
            hold(sp, v_out, 16 * GROUPS, weights_in, 16 * NWT)

        @block.vector
        def _(dve):
            dve.wait_ge(given, 1)
            dve.memset(v_ext[:, :, :, :, :], 0.0).then_inc(v_filled, 1)
            dve.wait_ge(v_filled, 1)
            for g in range(NG):
                dve.memset(v_ext[:, g, :, :, HD2:HD2 + 1], 1.0).then_inc(v_filled, 1)
            dve.wait_ge(v_filled, 1 + NG)
            dve.wait_ge(weights_in, 16 * NWT)
            with dve.Fori(0, B) as b:
                chain = Chain(dve, steps, b * STEPS, STEPS)
                wait_past(dve, a_made, 2 * b + 2)
                normalise(dve, chain, lambda i: ps_a[:, i // 4, (i % 4) * D:(i % 4 + 1) * D], lambda i: an[:, i, :],
                          st, mv, var, std, rstd, var_ready, std_ready, b * 2)
                wait_past(dve, x_in, 16 * b + 16)
                wait_past(dve, mid_out, 32 * b)
                chain.did(dve.tensor_tensor(xmid[:, :, :], an[:, :, :], x[:, :, :], ALU.add))
                chain.settle()
                dve.sem_inc(xmid_ready, 1)
                wait_past(dve, turned, 2 * b)
                normalise(dve, chain, lambda i: xmid[:, i, :], lambda i: xn[:, i, :],
                          st, mv, var, std, rstd, var_ready, std_ready, b * 2 + 1)
                chain.close()
                dve.sem_inc(xn_ready, 1)
                wait_past(dve, lo_ready, NQ * b)
                for n in range(NQ):
                    i, ch = n // NC, n % NC
                    sl = slice(ch * HALF, (ch + 1) * HALF)
                    wait_past(dve, q_made, NQ * b + n + 1)
                    dve.scalar_tensor_tensor(out=turn_a[:, n % 2, :], in0=ps_q[:, n % 2, :], scalar=bqk[:, i, 0:1],
                                             in1=rope[:, 0, sl], op0=ALU.add, op1=ALU.mult).then_inc(turned_by, 1)
                    dve.scalar_tensor_tensor(out=turn_b[:, n % 2, :], in0=ps_t[:, n % 2, :], scalar=bqk[:, i, 1:2],
                                             in1=rope[:, 1, sl], op0=ALU.add, op1=ALU.mult).then_inc(turned_by, 1)
                    wait_past(dve, turned_by, (NQ * b + n + 1) * 2)
                    dve.tensor_tensor(qk[:, i, sl], turn_a[:, n % 2, :], turn_b[:, n % 2, :],
                                      ALU.add).then_inc(roped, 1)
                wait_past(dve, roped, NQ * b + NQ)
                wait_past(dve, v_out, 16 * NG * b)
                for i in range(NT):
                    wait_past(dve, v_made, 2 * b + i // 4 + 1)
                    dve.tensor_tensor(v_ext[:, :, i, :, 0:HD2],
                                      ps_v[:, i // 4, (i % 4) * D:(i % 4 + 1) * D].rearrange(
                                          "p (g j r) -> p g j r", g=NG, j=GH),
                                      bv[:, :].rearrange("p (g j r) -> p g j r", g=NG, j=GH),
                                      ALU.add).then_inc(v_ready, 1)

        @block.scalar
        def _(act):
            act.wait_ge(given, 1)
            act.wait_ge(weights_in, 16 * NWT)
            with act.Fori(0, B) as b:
                for i in range(2):
                    wait_past(act, var_ready, 2 * b + i + 1)
                    nc.scalar.activation(std[:, :], var[:, :], ACT.Sqrt).then_inc(std_ready, 1)
                for i in range(2):
                    wait_past(act, turned, 2 * b + i + 1)
                    if i == 0:
                        wait_past(act, v_made, 2 * b)
                    nc.scalar.copy(x_t[:, i * HALF:(i + 1) * HALF], ps_t[:, i, :]).then_inc(xt_ready, 1)
                wait_past(act, qk_out, 16 * 4 * NG * b)
                for n in range(NQ):
                    i, ch = n // NC, n % NC
                    wait_past(act, roped, NQ * b + n + 1)
                    sl = slice(ch * HALF, (ch + 1) * HALF)
                    nc.scalar.copy(hi[:, i, sl], qk[:, i, sl]).then_inc(hi_ready, 1)

        @block.gpsimd
        def _(pool):
            for count in (y_in, x_in, a_made, var_ready, std_ready, xmid_ready, xn_ready, turned, xt_ready,
                          q_made, turned_by, roped, hi_ready, lo_ready, v_made,
                          v_ready, mid_out, qk_out, v_out):
                pool.sem_inc(count, 1)
            pool.sem_inc(given, 1)
            pool.wait_ge(given, 1)
            with pool.Fori(0, B) as b:
                wait_past(pool, qk_out, 16 * 4 * NG * b)
                for n in range(NQ):
                    i, ch = n // NC, n % NC
                    sl = slice(ch * HALF, (ch + 1) * HALF)
                    wait_past(pool, hi_ready, NQ * b + n + 1)
                    pool.tensor_tensor(lo[:, i, sl], qk[:, i, sl], hi[:, i, sl].bitcast(F32),
                                       ALU.subtract).then_inc(lo_ready, 1)

        @block.tensor
        def _(pe):
            pe.wait_ge(given, 1)
            pe.wait_ge(weights_in, 16 * NWT)
            with pe.Fori(0, B) as b:
                wait_past(pe, y_in, 16 * NG * (b + 1))
                wait_past(pe, xmid_ready, b)
                for i in range(NT):
                    for g in range(NG):
                        last = pe.matmul(ps_a[:, i // 4, (i % 4) * D:(i % 4 + 1) * D], y[:, g, i * P:(i + 1) * P],
                                         c["wy1"][:, g, :], start=g == 0, stop=g == NG - 1)
                    if i % 4 == 3:
                        last.then_inc(a_made, 1)
                wait_past(pe, xn_ready, b + 1)
                wait_past(pe, turned_by, NQ * b * 2)
                for i in range(NT):
                    tr = pe.transpose(ps_t[:, i // 4, (i % 4) * P:(i % 4 + 1) * P], xn[:, i, :], c["ident"][:, :])
                    if i % 4 == 3:
                        tr.then_inc(turned, 1)
                wait_past(pe, xt_ready, 2 * b + 2)
                for n in range(NQ):
                    if n >= 2:
                        wait_past(pe, turned_by, (NQ * b + n - 1) * 2)
                    else:
                        wait_past(pe, turned_by, NQ * b * 2)
                    ch = n % NC
                    moving = x_t[:, ch * HALF:(ch + 1) * HALF]
                    pe.matmul(ps_q[:, n % 2, :], (wq, wk)[n // NC][:, :], moving, start=True, stop=True)
                    pe.matmul(ps_t[:, n % 2, :], (wqs, wks)[n // NC][:, :], moving,
                              start=True, stop=True).then_inc(q_made, 1)
                wait_past(pe, v_ready, NT * b)
                for i in range(NT):
                    last = pe.matmul(ps_v[:, i // 4, (i % 4) * D:(i % 4 + 1) * D], x_t[:, i * P:(i + 1) * P],
                                     wv[:, :], start=True, stop=True)
                    if i % 4 == 3:
                        last.then_inc(v_made, 1)


def experts(nc, t, s, c):
    with ExitStack() as ctx:
        def sb(name, shape, dt=F32):
            return ctx.enter_context(nc.sbuf_tensor(f"e_{name}", shape, dt))

        def sem(name):
            return ctx.enter_context(nc.semaphore(f"e_{name}"))

        def bank(name, n=2):
            return ctx.enter_context(nc.psum_tensor(f"e_{name}", [P, n, HALF], F32))

        wo = sb("wo", [P, NG, D])
        wg = sb("wg", [D, E])
        w1 = sb("w1", [D, E, NF, P])
        w2 = sb("w2", [P, E, NF, D])
        b1 = sb("b1", [P, E, NF])
        b2 = sb("b2", [E, D])
        vecs = sb("vecs", [P, 5, D])
        bg = sb("bg", [P, E])
        y = sb("y", [P, NG, L])
        xmid = sb("xmid", [P, NT, D])
        xn = sb("xn", [P, NT, D])
        x1 = sb("x1", [P, NT, D])
        acc = sb("acc", [P, NT, D])
        x_t = sb("x_t", [D, L])
        st, mv = sb("st", [P, NT, 6]), sb("mv", [P, NT, 2])
        var, std, rstd = sb("var", [P, NT]), sb("std", [P, NT]), sb("rstd", [P, NT])
        logit = sb("logit", [P, NT, E])
        gmax = sb("gmax", [P, NT])
        gexp = sb("gexp", [P, NT, E])
        gsum = sb("gsum", [P, NT])
        prob = sb("prob", [P, NT, 2 * E])
        left = sb("left", [P, NT, 2 * E])
        top = sb("top", [P, NT, 8])
        strike = sb("strike", [P, NT, 8])
        comb = sb("comb", [P, NT, E])
        comb_t = sb("comb_t", [E, L])
        hid = sb("hid", [P, 2, NF, HALF])
        ps_a, ps_t, ps_h, ps_y = bank("ps_a"), bank("ps_t"), bank("ps_h"), bank("ps_y")

        weights_in = sem("weights_in")
        filled = sem("filled")
        y_in = sem("y_in")
        xn_in = sem("xn_in")
        xmid_in = sem("xmid_in")
        a_made = sem("a_made")
        steps = sem("steps")
        var_ready = sem("var_ready")
        std_ready = sem("std_ready")
        x1_ready = sem("x1_ready")
        turned = sem("turned")
        xt_ready = sem("xt_ready")
        logits_made = sem("logits_made")
        shifted = sem("shifted")
        gexp_ready = sem("gexp_ready")
        comb_ready = sem("comb_ready")
        comb_turned = sem("comb_turned")
        comb_t_ready = sem("comb_t_ready")
        bias_made = sem("bias_made")
        acc_ready = sem("acc_ready")
        h_made = sem("h_made")
        h_ready = sem("h_ready")
        y_made = sem("y_made")
        y_added = sem("y_added")
        res_ready = sem("res_ready")
        out_done = sem("out_done")
        given = sem("given")
        block = ctx.enter_context(nc.Block())
        NWT = 8
        NE = NC * E

        @block.sync
        def _(sp):
            sp.wait_ge(given, 1)
            for dst, name in ((wo[:, :, :], "wo"), (wg[:, :], "wg"), (w1[:, :, :, :], "w1"), (w2[:, :, :, :], "w2"),
                              (b1[:, :, :], "b1"), (b2[:, :], "b2"), (vecs[:, :, :], "vecs"), (bg[:, :], "bg")):
                sp.dma_start(dst, t[name]).then_inc(weights_in, 16)
            with sp.Fori(0, B) as b:
                hold(sp, a_made, 2 * b, weights_in, 16 * NWT)
                for g in range(NG):
                    sp.dma_start(y[:, g, :], s["y2"][b * NG + g]).then_inc(y_in, 16)
                hold(sp, x1_ready, b, weights_in, 16 * NWT)
                sp.dma_start(xn[:, :, :], s["xn2"][b]).then_inc(xn_in, 16)
                hold(sp, out_done, 16 * b, weights_in, 16 * NWT)
                sp.dma_start(xmid[:, :, :], s["xmid"][b]).then_inc(xmid_in, 16)
                hold(sp, res_ready, b + 1, weights_in, 16 * NWT)
                sp.dma_start(t["out"][b].rearrange("(t p) d -> p t d", p=P), xmid[:, :, :]).then_inc(out_done, 16)
            hold(sp, out_done, 16 * B, weights_in, 16 * NWT)

        STEPS = 3 * LN_STEPS + 2 * NT + 17

        @block.vector
        def _(dve):
            dve.wait_ge(given, 1)
            dve.memset(prob[:, :, :], -1.0).then_inc(filled, 1)
            dve.memset(strike[:, :, :], -1.0).then_inc(filled, 1)
            dve.wait_ge(weights_in, 16 * NWT)
            dve.wait_ge(filled, 2)

            def per_row(v_ap):
                return v_ap.unsqueeze(1).to_broadcast([P, NT, D])

            def gain(chain, buf, g_at, b_at):
                chain.did(dve.tensor_tensor(buf[:, :, :], buf[:, :, :], per_row(vecs[:, g_at, :]), ALU.mult))
                chain.settle()
                chain.did(dve.tensor_tensor(buf[:, :, :], buf[:, :, :], per_row(vecs[:, b_at, :]), ALU.add))
                chain.settle()

            with dve.Fori(0, B) as b:
                chain = Chain(dve, steps, b * STEPS, STEPS)
                wait_past(dve, a_made, 2 * b + 2)
                for i in range(2):
                    half = acc[:, 4 * i:4 * i + 4, :]
                    chain.did(dve.tensor_tensor(half, ps_a[:, i, :].rearrange("p (t d) -> p t d", t=4),
                                                vecs[:, 0, :].unsqueeze(1).to_broadcast([P, 4, D]), ALU.add))
                chain.settle()
                wait_past(dve, xn_in, 16 * b + 16)
                chain.did(dve.tensor_tensor(acc[:, :, :], acc[:, :, :], xn[:, :, :], ALU.add))
                chain.settle()
                wait_past(dve, turned, 2 * b)
                normalise(dve, chain, lambda i: acc[:, i, :], lambda i: x1[:, i, :],
                          st, mv, var, std, rstd, var_ready, std_ready, b * 3)
                gain(chain, x1, 1, 2)
                dve.sem_inc(x1_ready, 1)
                wait_past(dve, logits_made, b + 1)
                chain.did(dve.tensor_tensor(logit[:, :, :], ps_t[:, 0, 0:NT * E].rearrange("p (t e) -> p t e", t=NT),
                                            bg[:, :].unsqueeze(1).to_broadcast([P, NT, E]), ALU.add))
                chain.settle()
                chain.did(dve.reduce_max(gmax[:, :], logit[:, :, :], AX.X))
                chain.settle()
                dve.tensor_tensor(logit[:, :, :], logit[:, :, :], gmax[:, :].unsqueeze(2).to_broadcast([P, NT, E]),
                                  ALU.subtract).then_inc(shifted, 1)
                wait_past(dve, gexp_ready, b + 1)
                chain.did(dve.reduce_sum(gsum[:, :], gexp[:, :, :], AX.X))
                chain.settle()
                chain.did(dve.reciprocal(gmax[:, :], gsum[:, :]))
                chain.settle()
                chain.did(dve.tensor_tensor(prob[:, :, 0:E], gexp[:, :, :],
                                            gmax[:, :].unsqueeze(2).to_broadcast([P, NT, E]), ALU.mult))
                chain.settle()
                dve.memset(gmax[:, :], 0.0)
                for i in range(NT):
                    chain.did(dve.max(top[:, i, :], prob[:, i, :]))
                chain.settle()
                chain.did(dve.tensor_copy(strike[:, :, 0:2], top[:, :, 0:2]))
                chain.settle()
                dve.memset(gmax[:, :], 0.0)
                for i in range(NT):
                    chain.did(dve.match_replace(left[:, i, :], strike[:, i, :], prob[:, i, :], -2.0))
                chain.did(dve.reduce_sum(gsum[:, :], top[:, :, 0:2], AX.X))
                chain.settle()
                chain.did(dve.tensor_tensor(left[:, :, 0:E], left[:, :, 0:E], prob[:, :, 0:E], ALU.not_equal))
                chain.did(dve.reciprocal(gmax[:, :], gsum[:, :]))
                chain.settle()
                chain.did(dve.tensor_tensor(gexp[:, :, :], left[:, :, 0:E], prob[:, :, 0:E], ALU.mult))
                chain.settle()
                dve.tensor_tensor(comb[:, :, :], gexp[:, :, :], gmax[:, :].unsqueeze(2).to_broadcast([P, NT, E]),
                                  ALU.mult).then_inc(comb_ready, 1)
                wait_past(dve, bias_made, b + 1)
                for i in range(2):
                    dve.tensor_tensor(acc[:, 4 * i:4 * i + 4, :], ps_a[:, i, :].rearrange("p (t d) -> p t d", t=4),
                                      x1[:, 4 * i:4 * i + 4, :], ALU.add).then_inc(acc_ready, 1)
                wait_past(dve, acc_ready, 2 * b + 2)
                wait_past(dve, comb_ready, b + 1)
                for n in range(NE):
                    ch, e = n // E, n % E
                    wait_past(dve, y_made, NE * b + n + 1)
                    if e > 0:
                        wait_past(dve, y_added, (NE * b + n) * 4)
                    for i in range(4):
                        tile = acc[:, 4 * ch + i, :]
                        dve.scalar_tensor_tensor(out=tile, in0=ps_y[:, n % 2, i * D:(i + 1) * D],
                                                 scalar=comb[:, 4 * ch + i, e:e + 1], in1=tile,
                                                 op0=ALU.mult, op1=ALU.add).then_inc(y_added, 1)
                wait_past(dve, y_added, (b + 1) * NE * 4)
                normalise(dve, chain, lambda i: acc[:, i, :], lambda i: x1[:, i, :],
                          st, mv, var, std, rstd, var_ready, std_ready, b * 3 + 1)
                gain(chain, x1, 3, 4)
                normalise(dve, chain, lambda i: x1[:, i, :], lambda i: acc[:, i, :],
                          st, mv, var, std, rstd, var_ready, std_ready, b * 3 + 2)
                chain.close()
                wait_past(dve, xmid_in, 16 * b + 16)
                dve.tensor_tensor(xmid[:, :, :], acc[:, :, :], xmid[:, :, :], ALU.add).then_inc(res_ready, 1)
                wait_past(dve, res_ready, b + 1)

        @block.gpsimd
        def _(pool):
            for count in (y_in, xn_in, xmid_in, a_made, var_ready, std_ready, x1_ready, turned, xt_ready,
                          logits_made, shifted, gexp_ready, comb_ready, comb_turned,
                          comb_t_ready, bias_made, acc_ready, h_made, h_ready,
                          y_made, y_added, res_ready, out_done):
                pool.sem_inc(count, 1)
            pool.sem_inc(given, 1)
            pool.wait_ge(given, 1)

        @block.scalar
        def _(act):
            act.wait_ge(given, 1)
            act.wait_ge(weights_in, 16 * NWT)
            with act.Fori(0, B) as b:
                wait_past(act, var_ready, 3 * b + 1)
                nc.scalar.activation(std[:, :], var[:, :], ACT.Sqrt).then_inc(std_ready, 1)
                for i in range(2):
                    wait_past(act, turned, 2 * b + i + 1)
                    if i == 0:
                        wait_past(act, h_made, NE * NF * b)
                    nc.scalar.copy(x_t[:, i * HALF:(i + 1) * HALF], ps_t[:, i, :]).then_inc(xt_ready, 1)
                wait_past(act, shifted, b + 1)
                nc.scalar.activation(gexp[:, :, :], logit[:, :, :], ACT.Exp).then_inc(gexp_ready, 1)
                for i in range(2):
                    wait_past(act, comb_turned, 2 * b + i + 1)
                    nc.scalar.copy(comb_t[:, i * HALF:(i + 1) * HALF], ps_t[0:E, i, :]).then_inc(comb_t_ready, 1)
                for n in range(NE):
                    for f in range(NF):
                        m = n * NF + f
                        wait_past(act, h_made, NE * NF * b + m + 1)
                        if f == 0:
                            if n >= 2:
                                wait_past(act, y_made, NE * b + n - 1)
                            else:
                                wait_past(act, y_made, NE * b)
                        nc.scalar.activation(hid[:, n % 2, f, :], ps_h[:, m % 2, :], ACT.Gelu,
                                             bias=b1[:, n % E, f:f + 1]).then_inc(h_ready, 1)
                for i in range(2):
                    wait_past(act, var_ready, 3 * b + 2 + i)
                    nc.scalar.activation(std[:, :], var[:, :], ACT.Sqrt).then_inc(std_ready, 1)

        @block.tensor
        def _(pe):
            pe.wait_ge(given, 1)
            pe.wait_ge(weights_in, 16 * NWT)
            with pe.Fori(0, B) as b:
                wait_past(pe, y_in, 16 * NG * (b + 1))
                wait_past(pe, acc_ready, 2 * b)
                for i in range(NT):
                    for g in range(NG):
                        last = pe.matmul(ps_a[:, i // 4, (i % 4) * D:(i % 4 + 1) * D], y[:, g, i * P:(i + 1) * P],
                                         wo[:, g, :], start=g == 0, stop=g == NG - 1)
                    if i % 4 == 3:
                        last.then_inc(a_made, 1)
                wait_past(pe, x1_ready, b + 1)
                for i in range(NT):
                    tr = pe.transpose(ps_t[:, i // 4, (i % 4) * P:(i % 4 + 1) * P], x1[:, i, :], c["ident"][:, :])
                    if i % 4 == 3:
                        tr.then_inc(turned, 1)
                wait_past(pe, xt_ready, 2 * b + 2)
                for i in range(NT):
                    last = pe.matmul(ps_t[:, 0, i * E:(i + 1) * E], x_t[:, i * P:(i + 1) * P], wg[:, :],
                                     start=True, stop=True)
                last.then_inc(logits_made, 1)
                wait_past(pe, comb_ready, b + 1)
                for i in range(NT):
                    tr = pe.transpose(ps_t[0:E, i // 4, (i % 4) * P:(i % 4 + 1) * P], comb[:, i, :], c["ident"][:, :])
                    if i % 4 == 3:
                        tr.then_inc(comb_turned, 1)
                wait_past(pe, comb_t_ready, 2 * b + 2)
                for i in range(NT):
                    last = pe.matmul(ps_a[:, i // 4, (i % 4) * D:(i % 4 + 1) * D], comb_t[:, i * P:(i + 1) * P],
                                     b2[:, :], start=True, stop=True)
                last.then_inc(bias_made, 1)

                def hidden(n):
                    for f in range(NF):
                        m = n * NF + f
                        if m >= 2:
                            wait_past(pe, h_ready, NE * NF * b + m - 1)
                        else:
                            wait_past(pe, h_ready, NE * NF * b)
                        ch, e = n // E, n % E
                        pe.matmul(ps_h[:, m % 2, :], w1[:, e, f, :], x_t[:, ch * HALF:(ch + 1) * HALF],
                                  start=True, stop=True).then_inc(h_made, 1)

                def project(n):
                    wait_past(pe, h_ready, NE * NF * b + (n + 1) * NF)
                    if n >= 2:
                        wait_past(pe, y_added, (NE * b + n - 1) * 4)
                    else:
                        wait_past(pe, y_added, NE * b * 4)
                    for i in range(4):
                        for f in range(NF):
                            last = pe.matmul(ps_y[:, n % 2, i * D:(i + 1) * D], hid[:, n % 2, f, i * P:(i + 1) * P],
                                             w2[:, n % E, f, :], start=f == 0, stop=f == NF - 1)
                    last.then_inc(y_made, 1)

                hidden(0)
                for n in range(NE):
                    if n + 1 < NE:
                        hidden(n + 1)
                    project(n)


_OUT = ((B, L, D), "float32")


def kernel(L0_attn_x_bld, L0_attn_Wq, L0_attn_Wkv_down, L0_attn_Wk_up, L0_attn_Wv_up, L0_attn_Wout,
           L0_ffn_Wq, L0_ffn_bq, L0_ffn_Wk, L0_ffn_bk, L0_ffn_Wv, L0_ffn_bv, L0_ffn_Wo, L0_ffn_bo,
           L0_ffn_Wg, L0_ffn_bg, L0_ffn_W1, L0_ffn_b1, L0_ffn_W2, L0_ffn_b2,
           L0_ffn_g1, L0_ffn_be1, L0_ffn_g2, L0_ffn_be2):
    import concourse.bacc as _bacc
    from concourse.bass_utils import run_bass_kernel_spmd as _run

    def every_partition(*vectors):
        return np.stack([np.broadcast_to(np.asarray(v), (P, v.shape[-1])) for v in vectors], axis=1)

    k, m = np.meshgrid(np.arange(P), np.arange(P), indexing="ij")
    swap = (np.arange(D) + HD2 // 2) % HD2 + np.arange(D) // HD2 * HD2
    freq = (np.float32(1.0) / np.float32(10000.0) ** (np.arange(0, HD2, 2, dtype=np.float32) / HD2)).astype(np.float32)
    angle = (np.arange(L, dtype=np.float32)[None, :] * freq[np.arange(D) % (HD2 // 2), None]).astype(np.float32)
    sign = np.where(np.arange(D) % HD2 < HD2 // 2, -1, 1).astype(np.float32)[:, None]
    rope = np.stack([np.cos(angle), np.sin(angle) * sign], axis=1).astype(np.float32)
    wo = np.asarray(L0_ffn_Wo).reshape(NG, GH, HD2, D)
    wo = np.pad(wo, ((0, 0), (0, 0), (0, R - HD2), (0, 0)))
    laid = {
        "x": np.asarray(L0_attn_x_bld),
        "wq_t": np.asarray(L0_attn_Wq).transpose(2, 1, 0),
        "wk_t": np.asarray(L0_attn_Wk_up).transpose(2, 1, 0),
        "wv_t": np.asarray(L0_attn_Wv_up).transpose(2, 1, 0),
        "wout": np.asarray(L0_attn_Wout).transpose(1, 0, 2),
        "wkv": np.asarray(L0_attn_Wkv_down),
        "wq": np.asarray(L0_ffn_Wq), "wk": np.asarray(L0_ffn_Wk), "wv": np.asarray(L0_ffn_Wv),
        "wqs": np.asarray(L0_ffn_Wq)[:, swap], "wks": np.asarray(L0_ffn_Wk)[:, swap],
        "bqk": np.stack([np.stack([v, v[swap]], axis=1) for v in (np.asarray(L0_ffn_bq), np.asarray(L0_ffn_bk))],
                        axis=1),
        "rope": rope,
        "bv": every_partition(L0_ffn_bv)[:, 0],
        "wo": wo.transpose(1, 2, 0, 3).reshape(P, NG, D),
        "wg": np.asarray(L0_ffn_Wg),
        "w1": np.asarray(L0_ffn_W1).reshape(E, D, NF, P).transpose(1, 0, 2, 3),
        "w2": np.asarray(L0_ffn_W2).reshape(E, NF, P, D).transpose(2, 0, 1, 3),
        "b1": np.asarray(L0_ffn_b1).reshape(E, NF, P).transpose(2, 0, 1),
        "b2": np.asarray(L0_ffn_b2),
        "vecs": every_partition(L0_ffn_bo, L0_ffn_g1, L0_ffn_be1, L0_ffn_g2, L0_ffn_be2),
        "bg": every_partition(L0_ffn_bg)[:, 0],
        "ident": np.eye(P, dtype=np.float32),
        "mask_q": np.where(m > k, MASKED, 0).astype(np.float32),
        "mask_k": np.where(k > m, MASKED, 0).astype(np.float32),
        "sel": (k == m // R * R + HD2).astype(np.float32),
        "head_rows": np.repeat(np.eye(GH, dtype=np.float32), L, axis=1),
    }
    nc = _bacc.Bacc("TRN2", target_bir_lowering=False, num_devices=1)
    arrays, t = {}, {}
    for name, a in laid.items():
        arrays[f"in_{name}"] = a = np.ascontiguousarray(a)
        t[name] = nc.dram_tensor(f"in_{name}", a.shape, mybir.dt.from_np(a.dtype), kind="ExternalInput").ap()
    t["out"] = nc.dram_tensor("out_0", _OUT[0], F32, kind="ExternalOutput").ap()
    build(nc, t)
    r = _run(nc, [arrays], core_ids=[0])
    return r.results[0]["out_0"]
```

```python
from contextlib import ExitStack

import numpy as np

import concourse.bass as bass
from concourse import mybir

F32 = mybir.dt.float32
F32R = mybir.dt.float32r
BF16 = mybir.dt.bfloat16
ALU = mybir.AluOpType
ACT = mybir.ActivationFunctionType
AX = mybir.AxisListType

P = 128
B, L, D = 4, 1024, 128
NT = L // P
HALF = 512
NC = L // HALF
H = 16
HD1 = 64
LAT = 32
HD2 = D // H
GH = 4
NG = H // GH
GROUPS = B * NG
R = 32
E, FF = 8, 512
NF = FF // P
EPS = 1e-5
MASKED = -1e30
ROW_H0, ROW_H1, ROW_L, ROW_M = 0, 32, 64, 96


class Chain:

    def __init__(self, eng, sem, base, per_body):
        self.eng, self.sem, self.base, self.n, self.per_body = eng, sem, base, 0, per_body

    def did(self, instruction):
        instruction.then_inc(self.sem, 1)
        self.n += 1

    def settle(self):
        self.eng.wait_ge(self.sem, self.base + self.n)

    def close(self):
        assert self.n == self.per_body, (self.n, self.per_body)


def wait_from(eng, sem, value):
    if isinstance(value, int) and value <= 0:
        return
    eng.wait_ge(sem, value)


def wait_past(eng, sem, value):
    eng.wait_ge(sem, value + 1)


def hold(sp, sem, value, steady, steady_value, given=1):
    wait_from(sp, sem, value + given)
    sp.wait_ge(steady, steady_value)


LN_STEPS = 3 * NT + 1


def normalise(dve, chain, tiles, out_tiles, st, mv, var, std, rstd, var_ready, std_ready, nth):
    for t in range(NT):
        chain.did(dve.bn_stats(st[:, t, :], tiles(t)))
    chain.settle()
    dve.memset(rstd[:, :], 1.0)
    for t in range(NT):
        chain.did(dve.bn_aggr(mv[:, t, :], st[:, t, :]))
    chain.settle()
    dve.tensor_scalar(var[:, :], mv[:, :, 1], EPS, None, ALU.add).then_inc(var_ready, 1)
    wait_past(dve, std_ready, nth + 1)
    chain.did(dve.reciprocal(rstd[:, :], std[:, :]))
    chain.settle()
    for t in range(NT):
        chain.did(dve.tensor_scalar(out_tiles(t), tiles(t), mv[:, t, 0:1], rstd[:, t:t + 1],
                                    ALU.subtract, ALU.mult))
    chain.settle()


def build(nc, t):
    with ExitStack() as outer:
        def sb(ctx, name, shape, dt=F32):
            return ctx.enter_context(nc.sbuf_tensor(name, shape, dt))

        def dram(name, shape):
            return nc.dram_tensor(name, shape, F32, kind="Internal").ap()

        s = {
            "q1h": dram("q1h", (GROUPS, P, L)), "q1l": dram("q1l", (GROUPS, P, L)),
            "k1h": dram("k1h", (GROUPS, LAT, L)), "k1l": dram("k1l", (GROUPS, LAT, L)),
            "v1": dram("v1", (GROUPS, P, NT, LAT)),
            "y1": dram("y1", (GROUPS, P, L)),
            "q2h": dram("q2h", (GROUPS, R, L)), "q2l": dram("q2l", (GROUPS, R, L)),
            "k2h": dram("k2h", (GROUPS, R, L)), "k2l": dram("k2l", (GROUPS, R, L)),
            "v2": dram("v2", (GROUPS, P, NT, GH, R)),
            "y2": dram("y2", (GROUPS, P, L)),
            "xmid": dram("xmid", (B, P, NT, D)), "xn2": dram("xn2", (B, P, NT, D)),
        }
        c = {
            "ident": sb(outer, "ident", [P, P]), "sel": sb(outer, "sel", [P, P]),
            "ident_b": sb(outer, "ident_b", [P, P], BF16),
            "mask_q": sb(outer, "mask_q", [P, P], BF16), "mask_k": sb(outer, "mask_k", [P, P], BF16),
            "wy1": sb(outer, "wy1", [P, NG, D]),
            "ones": sb(outer, "ones", [P, R]),
        }
        prepare_first(nc, t, s, c)
        attend(nc, "a", True, s["q1h"], s["q1l"], s["k1h"], s["k1l"], s["v1"], s["y1"],
               float(HD1) ** -0.5, t, c)
        prepare_second(nc, t, s, c)
        attend(nc, "f", False, s["q2h"], s["q2l"], s["k2h"], s["k2l"], s["v2"], s["y2"],
               float(HD2) ** -0.5, t, c)
        experts(nc, t, s, c)


def prepare_first(nc, t, s, c):
    with ExitStack() as ctx:
        def sb(name, shape, dt=F32):
            return ctx.enter_context(nc.sbuf_tensor(name, shape, dt))

        def sem(name):
            return ctx.enter_context(nc.semaphore(name))

        wq_t = sb("wq_t", [HD1, H, D])
        wk_t = sb("wk_t", [HD1, H, LAT])
        wv_t = sb("wv_t", [HD1, H, LAT])
        wout = sb("wout", [HD1, H, D])
        wkv = sb("wkv", [D, LAT])
        masks = sb("masks", [P, 2, P])
        wqk = sb("wqk", [D, H, LAT])
        x = sb("x1_in", [P, NT, D])
        xn = sb("x1_n", [P, NT, D])
        x_t = sb("x1_t", [D, L])
        st = sb("st1", [P, NT, 6])
        mv = sb("mv1", [P, NT, 2])
        var = sb("var1", [P, NT])
        std = sb("std1", [P, NT])
        rstd = sb("rstd1", [P, NT])
        q_hi = sb("q1_hi", [P, 2, L], F32R)
        q_lo = sb("q1_lo", [P, 2, L], F32R)
        k_hi = sb("k1_hi", [LAT, L], F32R)
        k_lo = sb("k1_lo", [LAT, L], F32R)
        lat = sb("lat1", [P, NT, LAT])
        ps_t = ctx.enter_context(nc.psum_tensor("ps1_t", [P, 2, HALF], F32))
        ps_q = ctx.enter_context(nc.psum_tensor("ps1_q", [P, 2, HALF], F32))
        ps_k = ctx.enter_context(nc.psum_tensor("ps1_k", [P, 2, HALF], F32))
        ps_v = ctx.enter_context(nc.psum_tensor("ps1_v", [P, HALF], F32))
        ps_w = ctx.enter_context(nc.psum_tensor("ps1_w", [P, HALF], F32))

        weights_in = sem("a1_weights_in")
        consts_made = sem("a1_consts_made")
        wqk_made = sem("a1_wqk_made")
        wqk_copied = sem("a1_wqk_copied")
        wy_made = sem("a1_wy_made")
        wy_copied = sem("a1_wy_copied")
        x_in = sem("a1_x_in")
        steps = sem("a1_steps")
        var_ready = sem("a1_var_ready")
        std_ready = sem("a1_std_ready")
        xn_ready = sem("a1_xn_ready")
        turned = sem("a1_turned")
        xt_ready = sem("a1_xt_ready")
        q_made = sem("a1_q_made")
        q_hi_ready = sem("a1_q_hi_ready")
        q_lo_ready = sem("a1_q_lo_ready")
        k_made = sem("a1_k_made")
        k_hi_ready = sem("a1_k_hi_ready")
        k_lo_ready = sem("a1_k_lo_ready")
        v_made = sem("a1_v_made")
        lat_ready = sem("a1_lat_ready")
        q_out = [sem(f"a1_q_out{i}") for i in range(2)]
        kv_out = sem("a1_kv_out")
        given = sem("a1_given")
        block = ctx.enter_context(nc.Block())
        NW = 9
        NQ = NG * NC

        @block.sync
        def _(sp):
            sp.wait_ge(given, 1)
            sp.dma_start(wq_t[:, :, :], t["wq_t"]).then_inc(weights_in, 16)
            sp.dma_start(wk_t[:, :, :], t["wk_t"]).then_inc(weights_in, 16)
            sp.dma_start(wv_t[:, :, :], t["wv_t"]).then_inc(weights_in, 16)
            sp.dma_start(wout[:, :, :], t["wout"]).then_inc(weights_in, 16)
            sp.dma_start(wkv[:, :], t["wkv"]).then_inc(weights_in, 16)
            sp.dma_start(c["ident"][:, :], t["ident"]).then_inc(weights_in, 16)
            sp.dma_start(c["sel"][:, :], t["sel"]).then_inc(weights_in, 16)
            sp.dma_start(masks[:, 0, :], t["mask_q"]).then_inc(weights_in, 16)
            sp.dma_start(masks[:, 1, :], t["mask_k"]).then_inc(weights_in, 16)
            with sp.Fori(0, B) as b:
                hold(sp, xn_ready, b, weights_in, 16 * NW)
                sp.dma_start(x[:, :, :], t["x"][b].rearrange("(t p) d -> p t d", p=P)).then_inc(x_in, 16)
                hold(sp, k_lo_ready, NC * b + NC, weights_in, 16 * NW)
                for g in range(NG):
                    sp.dma_start(s["k1h"][b * NG + g], k_hi[:, :].bitcast(F32)).then_inc(kv_out, 16)
                    sp.dma_start(s["k1l"][b * NG + g], k_lo[:, :].bitcast(F32)).then_inc(kv_out, 16)
                hold(sp, lat_ready, b + 1, weights_in, 16 * NW)
                for g in range(NG):
                    sp.dma_start(s["v1"][b * NG + g], lat[:, :, :]).then_inc(kv_out, 16)
                for g in range(NG):
                    hold(sp, q_lo_ready, NQ * b + NC * (g + 1), weights_in, 16 * NW)
                    sp.dma_start(s["q1h"][b * NG + g], q_hi[:, g % 2, :].bitcast(F32)).then_inc(q_out[g % 2], 16)
                    sp.dma_start(s["q1l"][b * NG + g], q_lo[:, g % 2, :].bitcast(F32)).then_inc(q_out[g % 2], 16)
            hold(sp, kv_out, 16 * 3 * GROUPS, weights_in, 16 * NW)
            for i in range(2):
                hold(sp, q_out[i], 16 * GROUPS, weights_in, 16 * NW)

        @block.vector
        def _(dve):
            dve.wait_ge(given, 1)
            dve.memset(c["ones"][:, :], 1.0).then_inc(consts_made, 1)
            dve.wait_ge(weights_in, 16 * NW)
            dve.tensor_copy(c["ident_b"][:, :], c["ident"][:, :]).then_inc(consts_made, 1)
            dve.tensor_copy(c["mask_q"][:, :], masks[:, 0, :]).then_inc(consts_made, 1)
            dve.tensor_copy(c["mask_k"][:, :], masks[:, 1, :]).then_inc(consts_made, 1)
            dve.wait_ge(consts_made, 4)
            with dve.Fori(0, B) as b:
                chain = Chain(dve, steps, b * LN_STEPS, LN_STEPS)
                wait_past(dve, x_in, 16 * b + 16)
                wait_past(dve, turned, 2 * b)
                normalise(dve, chain, lambda i: x[:, i, :], lambda i: xn[:, i, :],
                          st, mv, var, std, rstd, var_ready, std_ready, b)
                chain.close()
                dve.sem_inc(xn_ready, 1)
                wait_past(dve, kv_out, 16 * 3 * NG * b)
                for i in range(NC):
                    wait_past(dve, k_hi_ready, NC * b + i + 1)
                    sl = slice(i * HALF, (i + 1) * HALF)
                    dve.tensor_tensor(k_lo[:, sl], ps_k[0:LAT, i, :], k_hi[:, sl].bitcast(F32),
                                      ALU.subtract).then_inc(k_lo_ready, 1)
                for n in range(NQ):
                    g, i = n // NC, n % NC
                    wait_past(dve, q_hi_ready, NQ * b + n + 1)
                    sl = slice(i * HALF, (i + 1) * HALF)
                    dve.tensor_tensor(q_lo[:, g % 2, sl], ps_q[:, i, :], q_hi[:, g % 2, sl].bitcast(F32),
                                      ALU.subtract).then_inc(q_lo_ready, 1)

        @block.gpsimd
        def _(pool):
            for count in (x_in, var_ready, std_ready, xn_ready, turned, xt_ready, q_made, q_hi_ready,
                          q_lo_ready, k_made, k_hi_ready, k_lo_ready, v_made,
                          lat_ready, kv_out, *q_out):
                pool.sem_inc(count, 1)
            pool.sem_inc(given, 1)
            pool.wait_ge(given, 1)

        @block.scalar
        def _(act):
            act.wait_ge(given, 1)
            act.wait_ge(wqk_made, 1)
            nc.scalar.copy(wqk[:, :, :], ps_w[:, :].rearrange("d (h c) -> d h c", h=H)).then_inc(wqk_copied, 1)
            act.wait_ge(wy_made, 1)
            nc.scalar.copy(c["wy1"][:, :, :], ps_w[:, :].rearrange("r (g d) -> r g d", g=NG)).then_inc(wy_copied, 1)
            with act.Fori(0, B) as b:
                wait_past(act, var_ready, b + 1)
                nc.scalar.activation(std[:, :], var[:, :], ACT.Sqrt).then_inc(std_ready, 1)
                for i in range(2):
                    wait_past(act, turned, 2 * b + i + 1)
                    if i == 0:
                        wait_past(act, q_made, NQ * b)
                    nc.scalar.copy(x_t[:, i * HALF:(i + 1) * HALF], ps_t[:, i, :]).then_inc(xt_ready, 1)
                wait_past(act, kv_out, 16 * 3 * NG * b)
                for i in range(NC):
                    wait_past(act, k_made, NC * b + i + 1)
                    nc.scalar.copy(k_hi[:, i * HALF:(i + 1) * HALF], ps_k[0:LAT, i, :]).then_inc(k_hi_ready, 1)
                wait_past(act, v_made, b + 1)
                nc.scalar.copy(lat[:, :, :], ps_v[:, 0:NT * LAT].rearrange("p (t c) -> p t c", t=NT))\
                    .then_inc(lat_ready, 1)
                for n in range(NQ):
                    g, i = n // NC, n % NC
                    if i == 0:
                        wait_past(act, q_out[g % 2], 16 * 2 * (2 * b + g // 2))
                    wait_past(act, q_made, NQ * b + n + 1)
                    nc.scalar.copy(q_hi[:, g % 2, i * HALF:(i + 1) * HALF], ps_q[:, i, :]).then_inc(q_hi_ready, 1)

        @block.tensor
        def _(pe):
            pe.wait_ge(given, 1)
            pe.wait_ge(weights_in, 16 * NW)
            for h in range(H):
                last = pe.matmul(ps_w[:, h * LAT:(h + 1) * LAT], wq_t[:, h, :], wk_t[:, h, :],
                                 start=True, stop=True)
            last.then_inc(wqk_made, 1)
            pe.wait_ge(wqk_copied, 1)
            for h in range(H):
                j, g = h % GH, h // GH
                last = pe.matmul(ps_w[R * j:R * j + R, g * D:(g + 1) * D], wv_t[:, h, :], wout[:, h, :],
                                 start=True, stop=True)
            last.then_inc(wy_made, 1)
            with pe.Fori(0, B) as b:
                wait_past(pe, xn_ready, b + 1)
                wait_past(pe, xt_ready, 2 * b)
                for i in range(NT):
                    tr = pe.transpose(ps_t[:, i // 4, (i % 4) * P:(i % 4 + 1) * P], xn[:, i, :], c["ident"][:, :])
                    if i % 4 == 3:
                        tr.then_inc(turned, 1)
                wait_past(pe, xt_ready, 2 * b + 2)
                wait_past(pe, k_lo_ready, NC * b)
                for i in range(NC):
                    pe.matmul(ps_k[0:LAT, i, :], wkv[:, :], x_t[:, i * HALF:(i + 1) * HALF],
                              start=True, stop=True).then_inc(k_made, 1)
                wait_past(pe, lat_ready, b)
                for i in range(NT):
                    last = pe.matmul(ps_v[:, i * LAT:(i + 1) * LAT], x_t[:, i * P:(i + 1) * P], wkv[:, :],
                                     start=True, stop=True)
                last.then_inc(v_made, 1)
                for n in range(NQ):
                    g, i = n // NC, n % NC
                    if n >= 2:
                        wait_past(pe, q_lo_ready, NQ * b + n - 1)
                    else:
                        wait_past(pe, q_lo_ready, NQ * b)
                    pe.matmul(ps_q[:, i, :], wqk[:, g * GH:(g + 1) * GH, :], x_t[:, i * HALF:(i + 1) * HALF],
                              start=True, stop=True).then_inc(q_made, 1)
            pe.wait_ge(wy_copied, 1)


def attend(nc, tag, causal, q_hi_d, q_lo_d, k_hi_d, k_lo_d, v_d, y_d, scale, t, c):
    TILES = [(ch, k) for ch in range(NC) for k in range((ch + 1) * NT // NC if causal else NT)]
    NCT = len(TILES)
    ENDS = [max(n for n, x in enumerate(TILES) if x[0] == ch) for ch in range(NC)]
    UNITS = [(i, j, kk) for i in range(NT) for kk in range(i // 4 + 1 if causal else NC) for j in range(GH)]
    NU = len(UNITS)
    SPAN = NCT - 2
    NB = 3
    NP = 4
    NS = 3 if causal else 4
    NW = 3
    NLOAD = 6 if causal else 3 + 3 * GH
    KROWS = ROW_M + (1 if causal else GH)
    DEN_COL = 0 if causal else HD2

    def work_at(k, has_prev, has_next):
        work = []
        if has_next:
            work += [("unit", n) for n in range(k * NU // SPAN, min((k + 1) * NU // SPAN, NU))]
            if k == SPAN:
                work += [("turned", 0), ("turned", 1)]
        for ch, first in ((1, 0), (0, ENDS[0] + 1)):
            if ch == 0 or has_prev:
                if k == first + 1:
                    work.append(("den", ch))
                if k == first + 3:
                    work.append(("rec", ch))
        return work

    def plan(has_prev, has_next):
        n, out = 0, []
        for k in range(NCT):
            here = work_at(k, has_prev, has_next)
            out.append([(n + i, *w) for i, w in enumerate(here)])
            n += len(here)
        return out, n

    NWK = plan(True, True)[1]
    HEAD = NU + 2
    SHORT = NWK - plan(False, True)[1]
    assert NCT % NP == 0 and NCT * GH % NS == 0 and NB == NW

    def work_base(s):
        return HEAD if isinstance(s, int) and s == 0 else s * NWK + HEAD - SHORT

    def work_bank(s_is_0, buf, n):
        return (HEAD + n) % NW if s_is_0 else (buf * NWK + HEAD - SHORT + n) % NW

    with ExitStack() as ctx:
        def sb(name, shape, dt=F32):
            return ctx.enter_context(nc.sbuf_tensor(f"{tag}_{name}", shape, dt))

        def sem(name):
            return ctx.enter_context(nc.semaphore(f"{tag}_{name}"))

        many = [sb(f"many{i}", [P, GH, L], F32R) for i in range(NB)]
        one = [sb(f"one{i}", [P, L], F32R) for i in range(NB)]
        v = [sb(f"v{i}", [P, NT, R if causal else GH * R]) for i in range(NB)]
        rows = sb("rows", [P, L if causal else GH * L])
        probs = sb("probs", [P, NP, GH, HALF])
        y = sb("y", [P, NC, HALF])
        raw = sb("raw", [P, HALF])
        den = sb("den", [P, HALF]) if causal else raw
        rec = sb("rec", [P, 4, GH])
        wide = sb("wide", [P, 4, GH, R])
        part_max = sb("part_max", [P, NT, GH, NC])
        neg_max = sb("neg_max", [P, NT, ROW_M + GH])
        ps_s = ctx.enter_context(nc.psum_tensor(f"{tag}_ps_s", [P, NS, HALF], F32))
        ps_w = ctx.enter_context(nc.psum_tensor(f"{tag}_ps_w", [P, NW, HALF], F32))
        ps_o = ctx.enter_context(nc.psum_tensor(f"{tag}_ps_o", [P, HALF], F32))
        ps_d = ctx.enter_context(nc.psum_tensor(f"{tag}_ps_d", [P, HALF], F32)) if causal else None

        filled = sem("filled")
        rows_in = sem("rows_in")
        operands_in = [sem(f"operands_in{i}") for i in range(NB)]
        v_in = [sem(f"v_in{i}") for i in range(NB)]
        work_full = sem("work_full")
        work_free = sem("work_free")
        neg_ready = sem("neg_ready")
        max_in = sem("max_in")
        scores_ready = sem("scores_ready")
        exp_done = sem("exp_done")
        pv_done = sem("pv_done")
        raw_ready = sem("raw_ready")
        den_ready = sem("den_ready")
        rec_ready = sem("rec_ready")
        wide_ready = sem("wide_ready")
        y_ready = sem("y_ready")
        y_out = [sem(f"y_out{i}") for i in range(NC)]
        block = ctx.enter_context(nc.Block())
        NFILL = 2 + NB * (1 if causal else 2)

        def first_col(ch, k):
            return max(0, (k - ch * 4) * P) if causal else 0

        def run_steps(eng, step):
            step(0, 0, 0, False, True)
            step(1, 1, 0, True, True)
            with eng.Fori(0, (GROUPS - 4) // NB) as it:
                step(it * NB + 2, 2, it, True, True)
                step(it * NB + 3, 0, it + 1, True, True)
                step(it * NB + 4, 1, it + 1, True, True)
            for s in range(GROUPS - 2, GROUPS):
                step(s, s % NB, s // NB, True, s < GROUPS - 1)

        def after(buf, rnd, n=1):
            return (buf + n) % NB, rnd + (buf + n) // NB

        @block.sync
        def _(sp):
            def load_operands(g, buf):
                if causal:
                    heads = q_hi_d[g].rearrange("(j r) n -> r j n", j=GH)
                    lows = q_lo_d[g].rearrange("(j r) n -> r j n", j=GH)
                    pairs = [(many[buf][ROW_H0:ROW_H0 + R, :, :], heads), (many[buf][ROW_H1:ROW_H1 + R, :, :], heads),
                             (many[buf][ROW_L:ROW_L + R, :, :], lows),
                             (one[buf][ROW_H0:ROW_H0 + R, :], k_hi_d[g]), (one[buf][ROW_H1:ROW_H1 + R, :], k_lo_d[g]),
                             (one[buf][ROW_L:ROW_L + R, :], k_hi_d[g])]
                else:
                    pairs = [(one[buf][ROW_H0:ROW_H0 + R, :], q_hi_d[g]), (one[buf][ROW_H1:ROW_H1 + R, :], q_hi_d[g]),
                             (one[buf][ROW_L:ROW_L + R, :], q_lo_d[g])]
                    for j in range(GH):
                        own = slice(j * HD2, (j + 1) * HD2)
                        for row, src in ((ROW_H0, k_hi_d), (ROW_H1, k_lo_d), (ROW_L, k_hi_d)):
                            pairs.append((many[buf][row + j * HD2:row + (j + 1) * HD2, j, :], src[g, own, :]))
                assert len(pairs) == NLOAD
                for dst, src in pairs:
                    sp.dma_start(dst.bitcast(F32), src).then_inc(operands_in[buf], 16)

            def load_v(g, buf):
                src = v_d[g] if causal else v_d[g].rearrange("p t j r -> p t (j r)")
                sp.dma_start(v[buf][:, :, :], src).then_inc(v_in[buf], 16)

            def place_max(g, buf, turned_at):
                hold(sp, work_free, turned_at, filled, NFILL, 0)
                for j in range(GH):
                    sp.dma_start(many[buf][ROW_M:ROW_M + 1, j, :].bitcast(F32),
                                 rows[ROW_M + j:ROW_M + j + 1, :]).then_inc(max_in, 16)

            def store(s, ch):
                hold(sp, y_ready, s * NC + ch + 1, filled, NFILL, 0)
                sp.dma_start(y_d[s][:, ch * HALF:(ch + 1) * HALF], y[:, ch, :]).then_inc(y_out[ch], 16)

            def step(s, buf, rnd, has_prev, has_next):
                if not (isinstance(s, int) and s >= GROUPS - 2):
                    if has_prev:
                        hold(sp, scores_ready, s * GH * NCT, filled, NFILL, 0)
                    load_operands(s + 2, (buf + 2) % NB)
                    if has_prev:
                        hold(sp, pv_done, s * NCT, filled, NFILL, 0)
                    load_v(s + 2, (buf + 2) % NB)
                if has_prev:
                    store(s - 1, 1)
                store(s, 0)
                if has_next and causal:
                    listed = plan(has_prev, has_next)[0]
                    last = max(n for here in listed for n, kind, _ in here if kind == "turned")
                    place_max(s + 1, (buf + 1) % NB, work_base(s) + last + 1)

            if not causal:
                sp.dma_start(rows[ROW_M:ROW_M + GH, :], t["head_rows"]).then_inc(rows_in, 16)
            sp.wait_ge(filled, NFILL)
            for g in range(2):
                load_operands(g, g)
                load_v(g, g)
            if causal:
                place_max(0, 0, HEAD)
            run_steps(sp, step)
            store(GROUPS - 1, 1)
            for ch in range(NC):
                sp.wait_ge(y_out[ch], 16 * GROUPS)

        @block.tensor
        def _(pe):
            def max_unit(w, bank, buf, n):
                i, j, kk = UNITS[n]
                diag = causal and kk == i // 4
                off = (i % 4) * P
                width = off + P if diag else HALF
                wait_from(pe, work_free, w - NW + 1)
                q = many[buf][0:ROW_M, j, i * P:(i + 1) * P] if causal else one[buf][0:ROW_M, i * P:(i + 1) * P]
                k = one[buf][0:ROW_M, kk * HALF:kk * HALF + width] if causal \
                    else many[buf][0:ROW_M, j, kk * HALF:kk * HALF + width]
                last = pe.matmul(ps_w[:, bank, 0:width], q, k, start=True, stop=not diag)
                if diag:
                    last = pe.matmul(ps_w[:, bank, off:width], c["ident_b"][:, :], c["mask_q"][:, :],
                                     start=False, stop=True)
                last.then_inc(work_full, 1)

            def turn_max(w, bank, g, hb):
                pe.wait_ge(neg_ready, g + 1)
                wait_from(pe, work_free, w - NW + 1)
                for ii in range(4):
                    last = pe.transpose(ps_w[0:ROW_M + GH, bank, ii * P:(ii + 1) * P],
                                        neg_max[:, hb * 4 + ii, :], c["ident"][:, :])
                last.then_inc(work_full, 1)

            def turn_den(w, bank, s, ch):
                pe.wait_ge(den_ready if causal else raw_ready, s * NC + ch + 1)
                wait_from(pe, work_free, w - NW + 1)
                for i in range(4):
                    last = pe.transpose(ps_w[:, bank, i * P:(i + 1) * P], den[:, i * P:(i + 1) * P],
                                        c["ident"][:, :])
                last.then_inc(work_full, 1)

            def turn_rec(w, bank, s, ch):
                pe.wait_ge(wide_ready, s * NC + ch + 1)
                wait_from(pe, work_free, w - NW + 1)
                for i in range(4):
                    last = pe.transpose(ps_w[:, bank, i * P:(i + 1) * P],
                                        wide[:, i, :, :].rearrange("p j r -> p (j r)"), c["ident"][:, :])
                last.then_inc(work_full, 1)

            def scores(s, buf, k, j):
                ch, kt = TILES[k]
                lo = first_col(ch, kt)
                diag = causal and kt >= 4 * ch
                slot = (GH * k + j) % NS
                wait_from(pe, exp_done, s * GH * NCT + GH * k + j - NS + 1)
                cols = slice(ch * HALF + lo, (ch + 1) * HALF)
                keys = slice(kt * P, (kt + 1) * P)
                lhs = one[buf][0:KROWS, keys] if causal else many[buf][0:KROWS, j, keys]
                rhs = many[buf][0:KROWS, j, cols] if causal else one[buf][0:KROWS, cols]
                last = pe.matmul(ps_s[:, slot, lo:HALF], lhs, rhs, start=True, stop=not diag)
                if diag:
                    last = pe.matmul(ps_s[:, slot, lo:lo + P], c["ident_b"][:, :], c["mask_k"][:, :],
                                     start=False, stop=True)
                last.then_inc(scores_ready, 1)

            def value_waits(s, buf, rnd, k):
                pe.wait_ge(exp_done, s * GH * NCT + GH * (k + 1))
                if k == 0:
                    pe.wait_ge(v_in[buf], (rnd + 1) * 16)
                if TILES[k][1] == 0:
                    wait_from(pe, raw_ready, s * NC + TILES[k][0])
                    if causal:
                        wait_from(pe, den_ready, s * NC + TILES[k][0])

            def values(buf, k, done):
                ch, kt = TILES[k]
                lo = first_col(ch, kt)
                for j in range(GH):
                    lhs = v[buf][:, kt, :] if causal else v[buf][:, kt, j * R:(j + 1) * R]
                    last = pe.matmul(ps_o[R * j:R * j + R, lo:HALF], lhs, probs[:, k % NP, j, lo:HALF],
                                     start=kt == 0, stop=k in ENDS)
                if done:
                    last.then_inc(pv_done, 1)

            def denominators(k):
                ch, kt = TILES[k]
                lo = first_col(ch, kt)
                for j in range(GH):
                    last = pe.matmul(ps_d[R * j:R * j + R, lo:HALF], c["ones"][:, :],
                                     probs[:, k % NP, j, lo:HALF], start=kt == 0, stop=k in ENDS)
                last.then_inc(pv_done, 1)

            def step(s, buf, rnd, has_prev, has_next):
                uses, _ = plan(has_prev, has_next)
                base = work_base(s)
                nbuf, nrnd = after(buf, rnd)

                def work(k, quarter):
                    here = uses[k]
                    for n, kind, what in here[len(here) * quarter // 4:len(here) * (quarter + 1) // 4]:
                        bank = work_bank(not has_prev, buf, n)
                        if kind == "unit":
                            if what == 0:
                                pe.wait_ge(operands_in[nbuf], (nrnd + 1) * 16 * NLOAD)
                            max_unit(base + n, bank, nbuf, what)
                        elif kind == "turned":
                            turn_max(base + n, bank, s + 1, what)
                        elif kind == "den":
                            turn_den(base + n, bank, s - what, what)
                        else:
                            turn_rec(base + n, bank, s - what, what)

                if causal:
                    pe.wait_ge(max_in, (s + 1) * 16 * GH)
                elif has_prev:
                    listed = plan(True, True)[0]
                    last = max(n for here in listed for n, kind, _ in here if kind == "turned")
                    pe.wait_ge(work_free, work_base(s) - NWK + last + 1)
                else:
                    pe.wait_ge(work_free, HEAD)
                for k in range(NCT):
                    here = (s, buf, rnd, k - 1) if k > 0 else (s - 1, (buf - 1) % NB, after(buf, rnd, -1)[1], NCT - 1)
                    late = k > 0 or has_prev
                    for j in range(GH):
                        scores(s, buf, k, j)
                        work(k, j)
                    if late:
                        value_waits(*here)
                        values(here[1], here[3], not causal)
                        if causal:
                            denominators(here[3])

            pe.wait_ge(filled, NFILL)
            pe.wait_ge(operands_in[0], 16 * NLOAD)
            for n in range(NU):
                max_unit(n, n % NW, 0, n)
            for hb in range(2):
                turn_max(NU + hb, (NU + hb) % NW, 0, hb)
            run_steps(pe, step)
            s, base = GROUPS - 1, work_base(GROUPS - 1) + plan(True, False)[1]
            value_waits(s, s % NB, s // NB, NCT - 1)
            values(s % NB, NCT - 1, not causal)
            if causal:
                denominators(NCT - 1)
            turn_den(base, base % NW, s, 1)
            turn_rec(base + 1, (base + 1) % NW, s, 1)
        @block.gpsimd
        def _(pool):
            def spread(n):
                pool.wait_ge(rec_ready, n + 1)
                pool.tensor_tensor(wide[:, :, :, :], rec[:, :, :].unsqueeze(3).to_broadcast([P, 4, GH, R]),
                                   c["ones"][:, :].unsqueeze(1).unsqueeze(1).to_broadcast([P, 4, GH, R]),
                                   ALU.mult).then_inc(wide_ready, 1)

            spread(0)
            with pool.Fori(1, GROUPS * NC) as n:
                pool.wait_ge(y_ready, n)
                spread(n)

        @block.scalar
        def _(act):
            def take_den(s, ch):
                act.wait_ge(pv_done, s * NCT + ENDS[ch] + 1)
                wait_from(act, rec_ready, s * NC + ch)
                nc.scalar.copy(den[:, :], ps_d[:, :]).then_inc(den_ready, 1)

            def step(s, buf, rnd, has_prev, has_next):
                for k in range(NCT):
                    ch, kt = TILES[k]
                    lo = first_col(ch, kt)
                    wait_from(act, pv_done, s * NCT + k - NP + 1)
                    for j in range(GH):
                        act.wait_ge(scores_ready, s * GH * NCT + GH * k + j + 1)
                        nc.scalar.activation(probs[:, k % NP, j, lo:HALF], ps_s[:, (GH * k + j) % NS, lo:HALF],
                                             ACT.Exp, scale=scale).then_inc(exp_done, 1)
                    if causal and k == 0 and has_prev:
                        take_den(s - 1, 1)
                    if causal and k == ENDS[0] + 1:
                        take_den(s, 0)

            run_steps(act, step)
            if causal:
                take_den(GROUPS - 1, 1)

        @block.vector
        def _(dve):
            def max_unit(w, bank, n):
                i, j, kk = UNITS[n]
                width = (i % 4) * P + P if causal and kk == i // 4 else HALF
                dve.wait_ge(work_full, w + 1)
                dve.reduce_max(part_max[:, i, j, kk:kk + 1], ps_w[:, bank, 0:width], AX.X).then_inc(work_free, 1)

            def negate_max(w):
                dve.wait_ge(work_free, w)
                dve.tensor_reduce(neg_max[:, :, ROW_M:ROW_M + GH], part_max[:, :, :, :], AX.X, ALU.max,
                                  negate=True).then_inc(neg_ready, 1)

            def take_turned(w, bank, g, buf, hb):
                if causal and hb == 0:
                    wait_from(dve, max_in, g * 16 * GH)
                dve.wait_ge(work_full, w + 1)
                sl = slice(hb * HALF, (hb + 1) * HALF)
                dst = rows[ROW_M:ROW_M + GH, sl].bitcast(F32R) if causal else one[buf][ROW_M:ROW_M + GH, sl]
                dve.tensor_copy(dst, ps_w[ROW_M:ROW_M + GH, bank, :]).then_inc(work_free, 1)

            def take_raw(s, ch):
                dve.wait_ge(pv_done, s * NCT + ENDS[ch] + 1)
                wait_from(dve, y_ready, s * NC + ch)
                dve.tensor_copy(raw[:, :], ps_o[:, :]).then_inc(raw_ready, 1)

            def invert(w, bank, s, ch):
                dve.wait_ge(work_full, w + 1)
                wait_from(dve, wide_ready, s * NC + ch)
                dve.reciprocal(rec[:, :, :], ps_w[:, bank, :].rearrange("p (i j r) -> p i j r", i=4, j=GH)[
                    :, :, :, DEN_COL]).then_inc(work_free, 1)
                dve.wait_ge(work_free, w + 1)
                dve.sem_inc(rec_ready, 1)

            def divide(w, bank, s, rnd, ch):
                dve.wait_ge(work_full, w + 1)
                dve.wait_ge(raw_ready, s * NC + ch + 1)
                wait_from(dve, y_out[ch], s * 16)
                dve.tensor_tensor(y[:, ch, :], raw[:, :], ps_w[:, bank, :], ALU.mult).then_inc(work_free, 1)
                dve.wait_ge(work_free, w + 1)
                dve.sem_inc(y_ready, 1)

            def step(s, buf, rnd, has_prev, has_next):
                uses, _ = plan(has_prev, has_next)
                base = work_base(s)
                nbuf, _ = after(buf, rnd)
                for k in range(NCT):
                    for n, kind, what in uses[k]:
                        bank = work_bank(not has_prev, buf, n)
                        if kind == "unit":
                            max_unit(base + n, bank, what)
                            if what == NU - 1:
                                negate_max(base + n + 1)
                        elif kind == "turned":
                            take_turned(base + n, bank, s + 1, nbuf, what)
                        elif kind == "den":
                            invert(base + n, bank, s - what, what)
                        else:
                            divide(base + n, bank, s - what, rnd, what)
                    if k == 0 and has_prev:
                        take_raw(s - 1, 1)
                    if k == ENDS[0] + 1:
                        take_raw(s, 0)

            dve.memset(part_max[:, :, :, :], -3e38).then_inc(filled, 1)
            dve.memset(neg_max[:, :, :], 0.0).then_inc(filled, 1)
            for i in range(NB):
                if causal:
                    dve.memset(one[i][ROW_M:ROW_M + 1, :].bitcast(F32), 1.0).then_inc(filled, 1)
                else:
                    dve.memset(many[i][0:ROW_M, :, :].bitcast(F32), 0.0).then_inc(filled, 1)
                    if i == 0:
                        dve.wait_ge(rows_in, 16)
                    dve.tensor_copy(many[i][ROW_M:ROW_M + GH, :, :],
                                    rows[ROW_M:ROW_M + GH, :].rearrange("r (j n) -> r j n", j=GH)).then_inc(filled, 1)
            dve.wait_ge(filled, NFILL)
            for n in range(NU):
                max_unit(n, n % NW, n)
            negate_max(NU)
            for hb in range(2):
                take_turned(NU + hb, (NU + hb) % NW, 0, 0, hb)
            run_steps(dve, step)
            s, base = GROUPS - 1, work_base(GROUPS - 1) + plan(True, False)[1]
            take_raw(s, 1)
            invert(base, base % NW, s, 1)
            divide(base + 1, (base + 1) % NW, s, s // NB, 1)


def prepare_second(nc, t, s, c):
    with ExitStack() as ctx:
        def sb(name, shape, dt=F32):
            return ctx.enter_context(nc.sbuf_tensor(f"m_{name}", shape, dt))

        def sem(name):
            return ctx.enter_context(nc.semaphore(f"m_{name}"))

        def bank(name, n=2):
            return ctx.enter_context(nc.psum_tensor(f"m_{name}", [P, n, HALF], F32))

        wq, wk, wv = (sb(n, [D, D]) for n in ("wq", "wk", "wv"))
        wqs, wks = (sb(n, [D, D]) for n in ("wqs", "wks"))
        bqk = sb("bqk", [D, 2, 2])
        rope = sb("rope", [D, 2, L])
        turn_a, turn_b = sb("turn_a", [D, 2, HALF]), sb("turn_b", [D, 2, HALF])
        qk = sb("qk", [D, 2, L])
        bv = sb("bv", [P, D])
        y = sb("y", [P, NG, L])
        x = sb("x", [P, NT, D])
        an = sb("an", [P, NT, D])
        xmid = sb("xmid", [P, NT, D])
        xn = sb("xn", [P, NT, D])
        x_t = sb("x_t", [D, L])
        st, mv = sb("st", [P, NT, 6]), sb("mv", [P, NT, 2])
        var, std, rstd = sb("var", [P, NT]), sb("std", [P, NT]), sb("rstd", [P, NT])
        hi = sb("hi", [P, 2, L], F32R)
        lo = sb("lo", [P, 2, L], F32R)
        v_ext = sb("v_ext", [P, NG, NT, GH, R])
        ps_a, ps_t, ps_q, ps_v = bank("ps_a"), bank("ps_t"), bank("ps_q"), bank("ps_v")

        weights_in = sem("weights_in")
        v_filled = sem("v_filled")
        y_in = sem("y_in")
        x_in = sem("x_in")
        a_made = sem("a_made")
        steps = sem("steps")
        var_ready = sem("var_ready")
        std_ready = sem("std_ready")
        xmid_ready = sem("xmid_ready")
        xn_ready = sem("xn_ready")
        turned = sem("turned")
        xt_ready = sem("xt_ready")
        q_made = sem("q_made")
        turned_by = sem("turned_by")
        roped = sem("roped")
        hi_ready = sem("hi_ready")
        lo_ready = sem("lo_ready")
        v_made = sem("v_made")
        v_ready = sem("v_ready")
        mid_out = sem("mid_out")
        qk_out = sem("qk_out")
        v_out = sem("v_out")
        given = sem("given")
        block = ctx.enter_context(nc.Block())
        NQ = 2 * NC
        NWT = 8
        STEPS = 2 * LN_STEPS + 1

        @block.sync
        def _(sp):
            sp.wait_ge(given, 1)
            sp.dma_start(wq[:, :], t["wq"]).then_inc(weights_in, 16)
            sp.dma_start(wk[:, :], t["wk"]).then_inc(weights_in, 16)
            sp.dma_start(wv[:, :], t["wv"]).then_inc(weights_in, 16)
            sp.dma_start(wqs[:, :], t["wqs"]).then_inc(weights_in, 16)
            sp.dma_start(wks[:, :], t["wks"]).then_inc(weights_in, 16)
            sp.dma_start(rope[:, :, :], t["rope"]).then_inc(weights_in, 16)
            sp.dma_start(bqk[:, :, :], t["bqk"]).then_inc(weights_in, 16)
            sp.dma_start(bv[:, :], t["bv"]).then_inc(weights_in, 16)
            with sp.Fori(0, B) as b:
                hold(sp, a_made, 2 * b, weights_in, 16 * NWT)
                for g in range(NG):
                    sp.dma_start(y[:, g, :], s["y1"][b * NG + g]).then_inc(y_in, 16)
                hold(sp, xmid_ready, b, weights_in, 16 * NWT)
                sp.dma_start(x[:, :, :], t["x"][b].rearrange("(t p) d -> p t d", p=P)).then_inc(x_in, 16)
                hold(sp, xmid_ready, b + 1, weights_in, 16 * NWT)
                sp.dma_start(s["xmid"][b], xmid[:, :, :]).then_inc(mid_out, 16)
                hold(sp, xn_ready, b + 1, weights_in, 16 * NWT)
                sp.dma_start(s["xn2"][b], xn[:, :, :]).then_inc(mid_out, 16)
                for i, (dh, dl) in enumerate((("q2h", "q2l"), ("k2h", "k2l"))):
                    hold(sp, lo_ready, NQ * b + NC * (i + 1), weights_in, 16 * NWT)
                    for g in range(NG):
                        sp.dma_start(s[dh][b * NG + g], hi[g * R:(g + 1) * R, i, :].bitcast(F32)).then_inc(qk_out, 16)
                        sp.dma_start(s[dl][b * NG + g], lo[g * R:(g + 1) * R, i, :].bitcast(F32)).then_inc(qk_out, 16)
                hold(sp, v_ready, NT * (b + 1), weights_in, 16 * NWT)
                for g in range(NG):
                    sp.dma_start(s["v2"][b * NG + g], v_ext[:, g, :, :, :]).then_inc(v_out, 16)
            hold(sp, mid_out, 16 * 2 * B, weights_in, 16 * NWT)
            hold(sp, qk_out, 16 * 4 * GROUPS, weights_in, 16 * NWT)
            hold(sp, v_out, 16 * GROUPS, weights_in, 16 * NWT)

        @block.vector
        def _(dve):
            dve.wait_ge(given, 1)
            dve.memset(v_ext[:, :, :, :, :], 0.0).then_inc(v_filled, 1)
            dve.wait_ge(v_filled, 1)
            for g in range(NG):
                dve.memset(v_ext[:, g, :, :, HD2:HD2 + 1], 1.0).then_inc(v_filled, 1)
            dve.wait_ge(v_filled, 1 + NG)
            dve.wait_ge(weights_in, 16 * NWT)
            with dve.Fori(0, B) as b:
                chain = Chain(dve, steps, b * STEPS, STEPS)
                wait_past(dve, a_made, 2 * b + 2)
                normalise(dve, chain, lambda i: ps_a[:, i // 4, (i % 4) * D:(i % 4 + 1) * D], lambda i: an[:, i, :],
                          st, mv, var, std, rstd, var_ready, std_ready, b * 2)
                wait_past(dve, x_in, 16 * b + 16)
                wait_past(dve, mid_out, 32 * b)
                chain.did(dve.tensor_tensor(xmid[:, :, :], an[:, :, :], x[:, :, :], ALU.add))
                chain.settle()
                dve.sem_inc(xmid_ready, 1)
                wait_past(dve, turned, 2 * b)
                normalise(dve, chain, lambda i: xmid[:, i, :], lambda i: xn[:, i, :],
                          st, mv, var, std, rstd, var_ready, std_ready, b * 2 + 1)
                chain.close()
                dve.sem_inc(xn_ready, 1)
                wait_past(dve, lo_ready, NQ * b)
                for n in range(NQ):
                    i, ch = n // NC, n % NC
                    sl = slice(ch * HALF, (ch + 1) * HALF)
                    wait_past(dve, q_made, NQ * b + n + 1)
                    dve.scalar_tensor_tensor(out=turn_a[:, n % 2, :], in0=ps_q[:, n % 2, :], scalar=bqk[:, i, 0:1],
                                             in1=rope[:, 0, sl], op0=ALU.add, op1=ALU.mult).then_inc(turned_by, 1)
                    dve.scalar_tensor_tensor(out=turn_b[:, n % 2, :], in0=ps_t[:, n % 2, :], scalar=bqk[:, i, 1:2],
                                             in1=rope[:, 1, sl], op0=ALU.add, op1=ALU.mult).then_inc(turned_by, 1)
                    wait_past(dve, turned_by, (NQ * b + n + 1) * 2)
                    dve.tensor_tensor(qk[:, i, sl], turn_a[:, n % 2, :], turn_b[:, n % 2, :],
                                      ALU.add).then_inc(roped, 1)
                wait_past(dve, roped, NQ * b + NQ)
                wait_past(dve, v_out, 16 * NG * b)
                for i in range(NT):
                    wait_past(dve, v_made, 2 * b + i // 4 + 1)
                    dve.tensor_tensor(v_ext[:, :, i, :, 0:HD2],
                                      ps_v[:, i // 4, (i % 4) * D:(i % 4 + 1) * D].rearrange(
                                          "p (g j r) -> p g j r", g=NG, j=GH),
                                      bv[:, :].rearrange("p (g j r) -> p g j r", g=NG, j=GH),
                                      ALU.add).then_inc(v_ready, 1)

        @block.scalar
        def _(act):
            act.wait_ge(given, 1)
            act.wait_ge(weights_in, 16 * NWT)
            with act.Fori(0, B) as b:
                for i in range(2):
                    wait_past(act, var_ready, 2 * b + i + 1)
                    nc.scalar.activation(std[:, :], var[:, :], ACT.Sqrt).then_inc(std_ready, 1)
                for i in range(2):
                    wait_past(act, turned, 2 * b + i + 1)
                    if i == 0:
                        wait_past(act, v_made, 2 * b)
                    nc.scalar.copy(x_t[:, i * HALF:(i + 1) * HALF], ps_t[:, i, :]).then_inc(xt_ready, 1)
                wait_past(act, qk_out, 16 * 4 * NG * b)
                for n in range(NQ):
                    i, ch = n // NC, n % NC
                    wait_past(act, roped, NQ * b + n + 1)
                    sl = slice(ch * HALF, (ch + 1) * HALF)
                    nc.scalar.copy(hi[:, i, sl], qk[:, i, sl]).then_inc(hi_ready, 1)

        @block.gpsimd
        def _(pool):
            for count in (y_in, x_in, a_made, var_ready, std_ready, xmid_ready, xn_ready, turned, xt_ready,
                          q_made, turned_by, roped, hi_ready, lo_ready, v_made,
                          v_ready, mid_out, qk_out, v_out):
                pool.sem_inc(count, 1)
            pool.sem_inc(given, 1)
            pool.wait_ge(given, 1)
            with pool.Fori(0, B) as b:
                wait_past(pool, qk_out, 16 * 4 * NG * b)
                for n in range(NQ):
                    i, ch = n // NC, n % NC
                    sl = slice(ch * HALF, (ch + 1) * HALF)
                    wait_past(pool, hi_ready, NQ * b + n + 1)
                    pool.tensor_tensor(lo[:, i, sl], qk[:, i, sl], hi[:, i, sl].bitcast(F32),
                                       ALU.subtract).then_inc(lo_ready, 1)

        @block.tensor
        def _(pe):
            pe.wait_ge(given, 1)
            pe.wait_ge(weights_in, 16 * NWT)
            with pe.Fori(0, B) as b:
                wait_past(pe, y_in, 16 * NG * (b + 1))
                wait_past(pe, xmid_ready, b)
                for i in range(NT):
                    for g in range(NG):
                        last = pe.matmul(ps_a[:, i // 4, (i % 4) * D:(i % 4 + 1) * D], y[:, g, i * P:(i + 1) * P],
                                         c["wy1"][:, g, :], start=g == 0, stop=g == NG - 1)
                    if i % 4 == 3:
                        last.then_inc(a_made, 1)
                wait_past(pe, xn_ready, b + 1)
                wait_past(pe, turned_by, NQ * b * 2)
                for i in range(NT):
                    tr = pe.transpose(ps_t[:, i // 4, (i % 4) * P:(i % 4 + 1) * P], xn[:, i, :], c["ident"][:, :])
                    if i % 4 == 3:
                        tr.then_inc(turned, 1)
                wait_past(pe, xt_ready, 2 * b + 2)
                for n in range(NQ):
                    if n >= 2:
                        wait_past(pe, turned_by, (NQ * b + n - 1) * 2)
                    else:
                        wait_past(pe, turned_by, NQ * b * 2)
                    ch = n % NC
                    moving = x_t[:, ch * HALF:(ch + 1) * HALF]
                    pe.matmul(ps_q[:, n % 2, :], (wq, wk)[n // NC][:, :], moving, start=True, stop=True)
                    pe.matmul(ps_t[:, n % 2, :], (wqs, wks)[n // NC][:, :], moving,
                              start=True, stop=True).then_inc(q_made, 1)
                wait_past(pe, v_ready, NT * b)
                for i in range(NT):
                    last = pe.matmul(ps_v[:, i // 4, (i % 4) * D:(i % 4 + 1) * D], x_t[:, i * P:(i + 1) * P],
                                     wv[:, :], start=True, stop=True)
                    if i % 4 == 3:
                        last.then_inc(v_made, 1)


def experts(nc, t, s, c):
    with ExitStack() as ctx:
        def sb(name, shape, dt=F32):
            return ctx.enter_context(nc.sbuf_tensor(f"e_{name}", shape, dt))

        def sem(name):
            return ctx.enter_context(nc.semaphore(f"e_{name}"))

        def bank(name, n=2):
            return ctx.enter_context(nc.psum_tensor(f"e_{name}", [P, n, HALF], F32))

        wo = sb("wo", [P, NG, D])
        wg = sb("wg", [D, E])
        w1 = sb("w1", [D, E, NF, P])
        w2 = sb("w2", [P, E, NF, D])
        b1 = sb("b1", [P, E, NF])
        b2 = sb("b2", [E, D])
        vecs = sb("vecs", [P, 5, D])
        bg = sb("bg", [P, E])
        y = sb("y", [P, NG, L])
        xmid = sb("xmid", [P, NT, D])
        xn = sb("xn", [P, NT, D])
        x1 = sb("x1", [P, NT, D])
        acc = sb("acc", [P, NT, D])
        x_t = sb("x_t", [D, L])
        st, mv = sb("st", [P, NT, 6]), sb("mv", [P, NT, 2])
        var, std, rstd = sb("var", [P, NT]), sb("std", [P, NT]), sb("rstd", [P, NT])
        logit = sb("logit", [P, NT, E])
        gmax = sb("gmax", [P, NT])
        gexp = sb("gexp", [P, NT, E])
        gsum = sb("gsum", [P, NT])
        prob = sb("prob", [P, NT, 2 * E])
        left = sb("left", [P, NT, 2 * E])
        top = sb("top", [P, NT, 8])
        strike = sb("strike", [P, NT, 8])
        comb = sb("comb", [P, NT, E])
        comb_t = sb("comb_t", [E, L])
        hid = sb("hid", [P, 2, NF, HALF])
        ps_a, ps_t, ps_h, ps_y = bank("ps_a"), bank("ps_t"), bank("ps_h"), bank("ps_y")

        weights_in = sem("weights_in")
        filled = sem("filled")
        y_in = sem("y_in")
        xn_in = sem("xn_in")
        xmid_in = sem("xmid_in")
        a_made = sem("a_made")
        steps = sem("steps")
        var_ready = sem("var_ready")
        std_ready = sem("std_ready")
        x1_ready = sem("x1_ready")
        turned = sem("turned")
        xt_ready = sem("xt_ready")
        logits_made = sem("logits_made")
        shifted = sem("shifted")
        gexp_ready = sem("gexp_ready")
        comb_ready = sem("comb_ready")
        comb_turned = sem("comb_turned")
        comb_t_ready = sem("comb_t_ready")
        bias_made = sem("bias_made")
        acc_ready = sem("acc_ready")
        h_made = sem("h_made")
        h_ready = sem("h_ready")
        y_made = sem("y_made")
        y_added = sem("y_added")
        res_ready = sem("res_ready")
        out_done = sem("out_done")
        given = sem("given")
        block = ctx.enter_context(nc.Block())
        NWT = 8
        NE = NC * E

        @block.sync
        def _(sp):
            sp.wait_ge(given, 1)
            for dst, name in ((wo[:, :, :], "wo"), (wg[:, :], "wg"), (w1[:, :, :, :], "w1"), (w2[:, :, :, :], "w2"),
                              (b1[:, :, :], "b1"), (b2[:, :], "b2"), (vecs[:, :, :], "vecs"), (bg[:, :], "bg")):
                sp.dma_start(dst, t[name]).then_inc(weights_in, 16)
            with sp.Fori(0, B) as b:
                hold(sp, a_made, 2 * b, weights_in, 16 * NWT)
                for g in range(NG):
                    sp.dma_start(y[:, g, :], s["y2"][b * NG + g]).then_inc(y_in, 16)
                hold(sp, x1_ready, b, weights_in, 16 * NWT)
                sp.dma_start(xn[:, :, :], s["xn2"][b]).then_inc(xn_in, 16)
                hold(sp, out_done, 16 * b, weights_in, 16 * NWT)
                sp.dma_start(xmid[:, :, :], s["xmid"][b]).then_inc(xmid_in, 16)
                hold(sp, res_ready, b + 1, weights_in, 16 * NWT)
                sp.dma_start(t["out"][b].rearrange("(t p) d -> p t d", p=P), xmid[:, :, :]).then_inc(out_done, 16)
            hold(sp, out_done, 16 * B, weights_in, 16 * NWT)

        STEPS = 3 * LN_STEPS + 2 * NT + 17

        @block.vector
        def _(dve):
            dve.wait_ge(given, 1)
            dve.memset(prob[:, :, :], -1.0).then_inc(filled, 1)
            dve.memset(strike[:, :, :], -1.0).then_inc(filled, 1)
            dve.wait_ge(weights_in, 16 * NWT)
            dve.wait_ge(filled, 2)

            def per_row(v_ap):
                return v_ap.unsqueeze(1).to_broadcast([P, NT, D])

            def gain(chain, buf, g_at, b_at):
                chain.did(dve.tensor_tensor(buf[:, :, :], buf[:, :, :], per_row(vecs[:, g_at, :]), ALU.mult))
                chain.settle()
                chain.did(dve.tensor_tensor(buf[:, :, :], buf[:, :, :], per_row(vecs[:, b_at, :]), ALU.add))
                chain.settle()

            with dve.Fori(0, B) as b:
                chain = Chain(dve, steps, b * STEPS, STEPS)
                wait_past(dve, a_made, 2 * b + 2)
                for i in range(2):
                    half = acc[:, 4 * i:4 * i + 4, :]
                    chain.did(dve.tensor_tensor(half, ps_a[:, i, :].rearrange("p (t d) -> p t d", t=4),
                                                vecs[:, 0, :].unsqueeze(1).to_broadcast([P, 4, D]), ALU.add))
                chain.settle()
                wait_past(dve, xn_in, 16 * b + 16)
                chain.did(dve.tensor_tensor(acc[:, :, :], acc[:, :, :], xn[:, :, :], ALU.add))
                chain.settle()
                wait_past(dve, turned, 2 * b)
                normalise(dve, chain, lambda i: acc[:, i, :], lambda i: x1[:, i, :],
                          st, mv, var, std, rstd, var_ready, std_ready, b * 3)
                gain(chain, x1, 1, 2)
                dve.sem_inc(x1_ready, 1)
                wait_past(dve, logits_made, b + 1)
                chain.did(dve.tensor_tensor(logit[:, :, :], ps_t[:, 0, 0:NT * E].rearrange("p (t e) -> p t e", t=NT),
                                            bg[:, :].unsqueeze(1).to_broadcast([P, NT, E]), ALU.add))
                chain.settle()
                chain.did(dve.reduce_max(gmax[:, :], logit[:, :, :], AX.X))
                chain.settle()
                dve.tensor_tensor(logit[:, :, :], logit[:, :, :], gmax[:, :].unsqueeze(2).to_broadcast([P, NT, E]),
                                  ALU.subtract).then_inc(shifted, 1)
                wait_past(dve, gexp_ready, b + 1)
                chain.did(dve.reduce_sum(gsum[:, :], gexp[:, :, :], AX.X))
                chain.settle()
                chain.did(dve.reciprocal(gmax[:, :], gsum[:, :]))
                chain.settle()
                chain.did(dve.tensor_tensor(prob[:, :, 0:E], gexp[:, :, :],
                                            gmax[:, :].unsqueeze(2).to_broadcast([P, NT, E]), ALU.mult))
                chain.settle()
                dve.memset(gmax[:, :], 0.0)
                for i in range(NT):
                    chain.did(dve.max(top[:, i, :], prob[:, i, :]))
                chain.settle()
                chain.did(dve.tensor_copy(strike[:, :, 0:2], top[:, :, 0:2]))
                chain.settle()
                dve.memset(gmax[:, :], 0.0)
                for i in range(NT):
                    chain.did(dve.match_replace(left[:, i, :], strike[:, i, :], prob[:, i, :], -2.0))
                chain.did(dve.reduce_sum(gsum[:, :], top[:, :, 0:2], AX.X))
                chain.settle()
                chain.did(dve.tensor_tensor(left[:, :, 0:E], left[:, :, 0:E], prob[:, :, 0:E], ALU.not_equal))
                chain.did(dve.reciprocal(gmax[:, :], gsum[:, :]))
                chain.settle()
                chain.did(dve.tensor_tensor(gexp[:, :, :], left[:, :, 0:E], prob[:, :, 0:E], ALU.mult))
                chain.settle()
                dve.tensor_tensor(comb[:, :, :], gexp[:, :, :], gmax[:, :].unsqueeze(2).to_broadcast([P, NT, E]),
                                  ALU.mult).then_inc(comb_ready, 1)
                wait_past(dve, bias_made, b + 1)
                for i in range(2):
                    dve.tensor_tensor(acc[:, 4 * i:4 * i + 4, :], ps_a[:, i, :].rearrange("p (t d) -> p t d", t=4),
                                      x1[:, 4 * i:4 * i + 4, :], ALU.add).then_inc(acc_ready, 1)
                wait_past(dve, acc_ready, 2 * b + 2)
                wait_past(dve, comb_ready, b + 1)
                for n in range(NE):
                    ch, e = n // E, n % E
                    wait_past(dve, y_made, NE * b + n + 1)
                    if e > 0:
                        wait_past(dve, y_added, (NE * b + n) * 4)
                    for i in range(4):
                        tile = acc[:, 4 * ch + i, :]
                        dve.scalar_tensor_tensor(out=tile, in0=ps_y[:, n % 2, i * D:(i + 1) * D],
                                                 scalar=comb[:, 4 * ch + i, e:e + 1], in1=tile,
                                                 op0=ALU.mult, op1=ALU.add).then_inc(y_added, 1)
                wait_past(dve, y_added, (b + 1) * NE * 4)
                normalise(dve, chain, lambda i: acc[:, i, :], lambda i: x1[:, i, :],
                          st, mv, var, std, rstd, var_ready, std_ready, b * 3 + 1)
                gain(chain, x1, 3, 4)
                normalise(dve, chain, lambda i: x1[:, i, :], lambda i: acc[:, i, :],
                          st, mv, var, std, rstd, var_ready, std_ready, b * 3 + 2)
                chain.close()
                wait_past(dve, xmid_in, 16 * b + 16)
                dve.tensor_tensor(xmid[:, :, :], acc[:, :, :], xmid[:, :, :], ALU.add).then_inc(res_ready, 1)
                wait_past(dve, res_ready, b + 1)

        @block.gpsimd
        def _(pool):
            for count in (y_in, xn_in, xmid_in, a_made, var_ready, std_ready, x1_ready, turned, xt_ready,
                          logits_made, shifted, gexp_ready, comb_ready, comb_turned,
                          comb_t_ready, bias_made, acc_ready, h_made, h_ready,
                          y_made, y_added, res_ready, out_done):
                pool.sem_inc(count, 1)
            pool.sem_inc(given, 1)
            pool.wait_ge(given, 1)

        @block.scalar
        def _(act):
            act.wait_ge(given, 1)
            act.wait_ge(weights_in, 16 * NWT)
            with act.Fori(0, B) as b:
                wait_past(act, var_ready, 3 * b + 1)
                nc.scalar.activation(std[:, :], var[:, :], ACT.Sqrt).then_inc(std_ready, 1)
                for i in range(2):
                    wait_past(act, turned, 2 * b + i + 1)
                    if i == 0:
                        wait_past(act, h_made, NE * NF * b)
                    nc.scalar.copy(x_t[:, i * HALF:(i + 1) * HALF], ps_t[:, i, :]).then_inc(xt_ready, 1)
                wait_past(act, shifted, b + 1)
                nc.scalar.activation(gexp[:, :, :], logit[:, :, :], ACT.Exp).then_inc(gexp_ready, 1)
                for i in range(2):
                    wait_past(act, comb_turned, 2 * b + i + 1)
                    nc.scalar.copy(comb_t[:, i * HALF:(i + 1) * HALF], ps_t[0:E, i, :]).then_inc(comb_t_ready, 1)
                for n in range(NE):
                    for f in range(NF):
                        m = n * NF + f
                        wait_past(act, h_made, NE * NF * b + m + 1)
                        if f == 0:
                            if n >= 2:
                                wait_past(act, y_made, NE * b + n - 1)
                            else:
                                wait_past(act, y_made, NE * b)
                        nc.scalar.activation(hid[:, n % 2, f, :], ps_h[:, m % 2, :], ACT.Gelu,
                                             bias=b1[:, n % E, f:f + 1]).then_inc(h_ready, 1)
                for i in range(2):
                    wait_past(act, var_ready, 3 * b + 2 + i)
                    nc.scalar.activation(std[:, :], var[:, :], ACT.Sqrt).then_inc(std_ready, 1)

        @block.tensor
        def _(pe):
            pe.wait_ge(given, 1)
            pe.wait_ge(weights_in, 16 * NWT)
            with pe.Fori(0, B) as b:
                wait_past(pe, y_in, 16 * NG * (b + 1))
                wait_past(pe, acc_ready, 2 * b)
                for i in range(NT):
                    for g in range(NG):
                        last = pe.matmul(ps_a[:, i // 4, (i % 4) * D:(i % 4 + 1) * D], y[:, g, i * P:(i + 1) * P],
                                         wo[:, g, :], start=g == 0, stop=g == NG - 1)
                    if i % 4 == 3:
                        last.then_inc(a_made, 1)
                wait_past(pe, x1_ready, b + 1)
                for i in range(NT):
                    tr = pe.transpose(ps_t[:, i // 4, (i % 4) * P:(i % 4 + 1) * P], x1[:, i, :], c["ident"][:, :])
                    if i % 4 == 3:
                        tr.then_inc(turned, 1)
                wait_past(pe, xt_ready, 2 * b + 2)
                for i in range(NT):
                    last = pe.matmul(ps_t[:, 0, i * E:(i + 1) * E], x_t[:, i * P:(i + 1) * P], wg[:, :],
                                     start=True, stop=True)
                last.then_inc(logits_made, 1)
                wait_past(pe, comb_ready, b + 1)
                for i in range(NT):
                    tr = pe.transpose(ps_t[0:E, i // 4, (i % 4) * P:(i % 4 + 1) * P], comb[:, i, :], c["ident"][:, :])
                    if i % 4 == 3:
                        tr.then_inc(comb_turned, 1)
                wait_past(pe, comb_t_ready, 2 * b + 2)
                for i in range(NT):
                    last = pe.matmul(ps_a[:, i // 4, (i % 4) * D:(i % 4 + 1) * D], comb_t[:, i * P:(i + 1) * P],
                                     b2[:, :], start=True, stop=True)
                last.then_inc(bias_made, 1)

                def hidden(n):
                    for f in range(NF):
                        m = n * NF + f
                        if m >= 2:
                            wait_past(pe, h_ready, NE * NF * b + m - 1)
                        else:
                            wait_past(pe, h_ready, NE * NF * b)
                        ch, e = n // E, n % E
                        pe.matmul(ps_h[:, m % 2, :], w1[:, e, f, :], x_t[:, ch * HALF:(ch + 1) * HALF],
                                  start=True, stop=True).then_inc(h_made, 1)

                def project(n):
                    wait_past(pe, h_ready, NE * NF * b + (n + 1) * NF)
                    if n >= 2:
                        wait_past(pe, y_added, (NE * b + n - 1) * 4)
                    else:
                        wait_past(pe, y_added, NE * b * 4)
                    for i in range(4):
                        for f in range(NF):
                            last = pe.matmul(ps_y[:, n % 2, i * D:(i + 1) * D], hid[:, n % 2, f, i * P:(i + 1) * P],
                                             w2[:, n % E, f, :], start=f == 0, stop=f == NF - 1)
                    last.then_inc(y_made, 1)

                hidden(0)
                for n in range(NE):
                    if n + 1 < NE:
                        hidden(n + 1)
                    project(n)


_OUT = ((B, L, D), "float32")


def kernel(L0_attn_x_bld, L0_attn_Wq, L0_attn_Wkv_down, L0_attn_Wk_up, L0_attn_Wv_up, L0_attn_Wout,
           L0_ffn_Wq, L0_ffn_bq, L0_ffn_Wk, L0_ffn_bk, L0_ffn_Wv, L0_ffn_bv, L0_ffn_Wo, L0_ffn_bo,
           L0_ffn_Wg, L0_ffn_bg, L0_ffn_W1, L0_ffn_b1, L0_ffn_W2, L0_ffn_b2,
           L0_ffn_g1, L0_ffn_be1, L0_ffn_g2, L0_ffn_be2):
    import concourse.bacc as _bacc
    from concourse.bass_utils import run_bass_kernel_spmd as _run

    def every_partition(*vectors):
        return np.stack([np.broadcast_to(np.asarray(v), (P, v.shape[-1])) for v in vectors], axis=1)

    k, m = np.meshgrid(np.arange(P), np.arange(P), indexing="ij")
    swap = (np.arange(D) + HD2 // 2) % HD2 + np.arange(D) // HD2 * HD2
    freq = (np.float32(1.0) / np.float32(10000.0) ** (np.arange(0, HD2, 2, dtype=np.float32) / HD2)).astype(np.float32)
    angle = (np.arange(L, dtype=np.float32)[None, :] * freq[np.arange(D) % (HD2 // 2), None]).astype(np.float32)
    sign = np.where(np.arange(D) % HD2 < HD2 // 2, -1, 1).astype(np.float32)[:, None]
    rope = np.stack([np.cos(angle), np.sin(angle) * sign], axis=1).astype(np.float32)
    wo = np.asarray(L0_ffn_Wo).reshape(NG, GH, HD2, D)
    wo = np.pad(wo, ((0, 0), (0, 0), (0, R - HD2), (0, 0)))
    laid = {
        "x": np.asarray(L0_attn_x_bld),
        "wq_t": np.asarray(L0_attn_Wq).transpose(2, 1, 0),
        "wk_t": np.asarray(L0_attn_Wk_up).transpose(2, 1, 0),
        "wv_t": np.asarray(L0_attn_Wv_up).transpose(2, 1, 0),
        "wout": np.asarray(L0_attn_Wout).transpose(1, 0, 2),
        "wkv": np.asarray(L0_attn_Wkv_down),
        "wq": np.asarray(L0_ffn_Wq), "wk": np.asarray(L0_ffn_Wk), "wv": np.asarray(L0_ffn_Wv),
        "wqs": np.asarray(L0_ffn_Wq)[:, swap], "wks": np.asarray(L0_ffn_Wk)[:, swap],
        "bqk": np.stack([np.stack([v, v[swap]], axis=1) for v in (np.asarray(L0_ffn_bq), np.asarray(L0_ffn_bk))],
                        axis=1),
        "rope": rope,
        "bv": every_partition(L0_ffn_bv)[:, 0],
        "wo": wo.transpose(1, 2, 0, 3).reshape(P, NG, D),
        "wg": np.asarray(L0_ffn_Wg),
        "w1": np.asarray(L0_ffn_W1).reshape(E, D, NF, P).transpose(1, 0, 2, 3),
        "w2": np.asarray(L0_ffn_W2).reshape(E, NF, P, D).transpose(2, 0, 1, 3),
        "b1": np.asarray(L0_ffn_b1).reshape(E, NF, P).transpose(2, 0, 1),
        "b2": np.asarray(L0_ffn_b2),
        "vecs": every_partition(L0_ffn_bo, L0_ffn_g1, L0_ffn_be1, L0_ffn_g2, L0_ffn_be2),
        "bg": every_partition(L0_ffn_bg)[:, 0],
        "ident": np.eye(P, dtype=np.float32),
        "mask_q": np.where(m > k, MASKED, 0).astype(np.float32),
        "mask_k": np.where(k > m, MASKED, 0).astype(np.float32),
        "sel": (k == m // R * R + HD2).astype(np.float32),
        "head_rows": np.repeat(np.eye(GH, dtype=np.float32), L, axis=1),
    }
    nc = _bacc.Bacc("TRN2", target_bir_lowering=False, num_devices=1)
    arrays, t = {}, {}
    for name, a in laid.items():
        arrays[f"in_{name}"] = a = np.ascontiguousarray(a)
        t[name] = nc.dram_tensor(f"in_{name}", a.shape, mybir.dt.from_np(a.dtype), kind="ExternalInput").ap()
    t["out"] = nc.dram_tensor("out_0", _OUT[0], F32, kind="ExternalOutput").ap()
    build(nc, t)
    r = _run(nc, [arrays], core_ids=[0])
    return r.results[0]["out_0"]
```

```python
from contextlib import ExitStack

import numpy as np

import concourse.bass as bass
from concourse import mybir

F32 = mybir.dt.float32
F32R = mybir.dt.float32r
BF16 = mybir.dt.bfloat16
ALU = mybir.AluOpType
ACT = mybir.ActivationFunctionType
AX = mybir.AxisListType

P = 128
B, L, D = 4, 1024, 128
NT = L // P
HALF = 512
NC = L // HALF
H = 16
HD1 = 64
LAT = 32
HD2 = D // H
GH = 4
NG = H // GH
GROUPS = B * NG
R = 32
E, FF = 8, 512
NF = FF // P
EPS = 1e-5
MASKED = -1e30
ROW_H0, ROW_H1, ROW_L, ROW_M = 0, 32, 64, 96


class Chain:

    def __init__(self, eng, sem, base, per_body):
        self.eng, self.sem, self.base, self.n, self.per_body = eng, sem, base, 0, per_body

    def did(self, instruction):
        instruction.then_inc(self.sem, 1)
        self.n += 1

    def settle(self):
        self.eng.wait_ge(self.sem, self.base + self.n)

    def close(self):
        assert self.n == self.per_body, (self.n, self.per_body)


def wait_from(eng, sem, value):
    if isinstance(value, int) and value <= 0:
        return
    eng.wait_ge(sem, value)


def wait_past(eng, sem, value):
    eng.wait_ge(sem, value + 1)


def hold(sp, sem, value, steady, steady_value, given=1):
    wait_from(sp, sem, value + given)
    sp.wait_ge(steady, steady_value)


LN_STEPS = 3 * NT + 1


def measure(dve, chain, tiles, count, st):
    for t in count:
        chain.did(dve.bn_stats(st[:, t, :], tiles(t)))


def conclude(dve, chain, st, mv, var, rstd, var_ready):
    chain.settle()
    dve.memset(rstd[:, :], 1.0)
    for t in range(NT):
        chain.did(dve.bn_aggr(mv[:, t, :], st[:, t, :]))
    chain.settle()
    dve.tensor_scalar(var[:, :], mv[:, :, 1], EPS, None, ALU.add).then_inc(var_ready, 1)


def invert_roots(dve, chain, std, rstd, std_ready, nth):
    wait_past(dve, std_ready, nth + 1)
    chain.did(dve.reciprocal(rstd[:, :], std[:, :]))
    chain.settle()


def scale_rows(dve, chain, tiles, out_tiles, count, mv, rstd):
    for t in count:
        chain.did(dve.tensor_scalar(out_tiles(t), tiles(t), mv[:, t, 0:1], rstd[:, t:t + 1],
                                    ALU.subtract, ALU.mult))


def build(nc, t):
    with ExitStack() as outer:
        def sb(ctx, name, shape, dt=F32):
            return ctx.enter_context(nc.sbuf_tensor(name, shape, dt))

        def dram(name, shape):
            return nc.dram_tensor(name, shape, F32, kind="Internal").ap()

        s = {
            "q1h": dram("q1h", (GROUPS, P, L)), "q1l": dram("q1l", (GROUPS, P, L)),
            "k1h": dram("k1h", (GROUPS, LAT, L)), "k1l": dram("k1l", (GROUPS, LAT, L)),
            "v1": dram("v1", (GROUPS, P, NT, LAT)),
            "y1": dram("y1", (GROUPS, P, L)),
            "q2h": dram("q2h", (GROUPS, R, L)), "q2l": dram("q2l", (GROUPS, R, L)),
            "k2h": dram("k2h", (GROUPS, R, L)), "k2l": dram("k2l", (GROUPS, R, L)),
            "v2": dram("v2", (GROUPS, P, NT, GH, R)),
            "y2": dram("y2", (GROUPS, P, L)),
            "xmid": dram("xmid", (B, P, NT, D)), "xn2": dram("xn2", (B, P, NT, D)),
        }
        c = {
            "ident": sb(outer, "ident", [P, P]),
            "ident_b": sb(outer, "ident_b", [P, P], BF16),
            "mask_q": sb(outer, "mask_q", [P, P], BF16), "mask_k": sb(outer, "mask_k", [P, P], BF16),
            "wy1": sb(outer, "wy1", [P, NG, D]),
            "ones": sb(outer, "ones", [P, R]),
            "w1_hi": sb(outer, "w1_hi", [D, E, NF, P], F32R), "w1_lo": sb(outer, "w1_lo", [D, E, NF, P], F32R),
        }
        prepare_first(nc, t, s, c)
        attend(nc, "a", True, s["q1h"], s["q1l"], s["k1h"], s["k1l"], s["v1"], s["y1"],
               float(HD1) ** -0.5, t, c)
        prepare_second(nc, t, s, c)
        attend(nc, "f", False, s["q2h"], s["q2l"], s["k2h"], s["k2l"], s["v2"], s["y2"],
               float(HD2) ** -0.5, t, c)
        experts(nc, t, s, c)


def prepare_first(nc, t, s, c):
    with ExitStack() as ctx:
        def sb(name, shape, dt=F32):
            return ctx.enter_context(nc.sbuf_tensor(name, shape, dt))

        def sem(name):
            return ctx.enter_context(nc.semaphore(name))

        wq_t = sb("wq_t", [HD1, H, D])
        wk_t = sb("wk_t", [HD1, H, LAT])
        wv_t = sb("wv_t", [HD1, H, LAT])
        wout = sb("wout", [HD1, H, D])
        wkv = sb("wkv", [D, LAT])
        masks = sb("masks", [P, 2, P])
        w1 = sb("w1", [D, E, NF, P])
        wqk = sb("wqk", [D, H, LAT])
        x = sb("x1_in", [P, NT, D])
        xn = sb("x1_n", [P, NT, D])
        x_t = sb("x1_t", [D, L])
        st = sb("st1", [P, NT, 6])
        mv = sb("mv1", [P, NT, 2])
        var = sb("var1", [P, NT])
        std = sb("std1", [P, NT])
        rstd = sb("rstd1", [P, NT])
        q_hi = sb("q1_hi", [P, 2, L], F32R)
        q_lo = sb("q1_lo", [P, 2, L], F32R)
        k_hi = sb("k1_hi", [LAT, L], F32R)
        k_lo = sb("k1_lo", [LAT, L], F32R)
        lat = sb("lat1", [P, NT, LAT])
        ps_t = ctx.enter_context(nc.psum_tensor("ps1_t", [P, 2, HALF], F32))
        ps_q = ctx.enter_context(nc.psum_tensor("ps1_q", [P, 2, HALF], F32))
        ps_k = ctx.enter_context(nc.psum_tensor("ps1_k", [P, 2, HALF], F32))
        ps_v = ctx.enter_context(nc.psum_tensor("ps1_v", [P, HALF], F32))
        ps_w = ctx.enter_context(nc.psum_tensor("ps1_w", [P, HALF], F32))

        weights_in = sem("a1_weights_in")
        w1_in = sem("a1_w1_in")
        w1_hi_ready = sem("a1_w1_hi_ready")
        w1_lo_ready = sem("a1_w1_lo_ready")
        consts_made = sem("a1_consts_made")
        wqk_made = sem("a1_wqk_made")
        wqk_copied = sem("a1_wqk_copied")
        wy_made = sem("a1_wy_made")
        wy_copied = sem("a1_wy_copied")
        x_in = sem("a1_x_in")
        steps = sem("a1_steps")
        var_ready = sem("a1_var_ready")
        std_ready = sem("a1_std_ready")
        xn_ready = sem("a1_xn_ready")
        turned = sem("a1_turned")
        xt_ready = sem("a1_xt_ready")
        q_made = sem("a1_q_made")
        q_hi_ready = sem("a1_q_hi_ready")
        q_lo_ready = sem("a1_q_lo_ready")
        k_made = sem("a1_k_made")
        k_hi_ready = sem("a1_k_hi_ready")
        k_lo_ready = sem("a1_k_lo_ready")
        v_made = sem("a1_v_made")
        lat_ready = sem("a1_lat_ready")
        q_out = [sem(f"a1_q_out{i}") for i in range(2)]
        kv_out = sem("a1_kv_out")
        given = sem("a1_given")
        block = ctx.enter_context(nc.Block())
        NW = 8
        NQ = NG * NC

        @block.sync
        def _(sp):
            sp.wait_ge(given, 1)
            sp.dma_start(x[:, :, :], t["x"][0].rearrange("(t p) d -> p t d", p=P)).then_inc(x_in, 16)
            sp.dma_start(wq_t[:, :, :], t["wq_t"]).then_inc(weights_in, 16)
            sp.dma_start(wk_t[:, :, :], t["wk_t"]).then_inc(weights_in, 16)
            sp.dma_start(wv_t[:, :, :], t["wv_t"]).then_inc(weights_in, 16)
            sp.dma_start(wout[:, :, :], t["wout"]).then_inc(weights_in, 16)
            sp.dma_start(wkv[:, :], t["wkv"]).then_inc(weights_in, 16)
            sp.dma_start(c["ident"][:, :], t["ident"]).then_inc(weights_in, 16)
            sp.dma_start(masks[:, 0, :], t["mask_q"]).then_inc(weights_in, 16)
            sp.dma_start(masks[:, 1, :], t["mask_k"]).then_inc(weights_in, 16)

            def load_x(b):
                sp.dma_start(x[:, :, :], t["x"][b].rearrange("(t p) d -> p t d", p=P)).then_inc(x_in, 16)

            def store(b, has_next):
                hold(sp, k_lo_ready, NC * b + NC, weights_in, 16 * NW)
                for dst, src in (("k1h", k_hi), ("k1l", k_lo)):
                    sp.dma_start(s[dst].rearrange("(b g) r l -> b r g l", g=NG)[b],
                                 src[:, :].bitcast(F32).unsqueeze(1).to_broadcast([LAT, NG, L])).then_inc(kv_out, 16)
                hold(sp, lat_ready, b + 1, weights_in, 16 * NW)
                for g in range(NG):
                    sp.dma_start(s["v1"][b * NG + g], lat[:, :, :]).then_inc(kv_out, 16)
                for g in range(NG):
                    hold(sp, q_lo_ready, NQ * b + NC * (g + 1), weights_in, 16 * NW)
                    sp.dma_start(s["q1h"][b * NG + g], q_hi[:, g % 2, :].bitcast(F32)).then_inc(q_out[g % 2], 16)
                    sp.dma_start(s["q1l"][b * NG + g], q_lo[:, g % 2, :].bitcast(F32)).then_inc(q_out[g % 2], 16)
                if has_next:
                    hold(sp, xn_ready, b + 2, weights_in, 16 * NW)
                    load_x(b + 2)

            sp.wait_ge(xn_ready, 2)
            load_x(1)
            sp.dma_start(w1[:, :, :, :], t["w1"]).then_inc(w1_in, 16)
            with sp.Fori(0, B - 2) as b:
                store(b, True)
            for b in range(B - 2, B):
                store(b, False)
            hold(sp, kv_out, 16 * (2 + NG) * B, weights_in, 16 * NW)
            for i in range(2):
                hold(sp, q_out[i], 16 * GROUPS, weights_in, 16 * NW)

        @block.vector
        def _(dve):
            dve.wait_ge(given, 1)
            dve.memset(c["ones"][:, :], 1.0).then_inc(consts_made, 1)

            def rows_of(b):
                return Chain(dve, steps, b * LN_STEPS, LN_STEPS)

            def measure_x(b, chain, count):
                wait_past(dve, x_in, 16 * b + 16)
                measure(dve, chain, lambda i: x[:, i, :], count, st)

            def conclude_x(chain):
                conclude(dve, chain, st, mv, var, rstd, var_ready)

            def scale_x(b, chain, count):
                if count[0] == 0:
                    wait_past(dve, turned, 2 * b)
                    invert_roots(dve, chain, std, rstd, std_ready, b)
                scale_rows(dve, chain, lambda i: x[:, i, :], lambda i: xn[:, i, :], count, mv, rstd)
                if count[-1] == NT - 1:
                    chain.settle()
                    chain.close()
                    dve.sem_inc(xn_ready, 1)

            def split(b, has_next):
                chain = rows_of(b + 1)
                wait_past(dve, kv_out, 16 * (2 + NG) * b)
                for i in range(NC):
                    wait_past(dve, k_hi_ready, NC * b + i + 1)
                    sl = slice(i * HALF, (i + 1) * HALF)
                    dve.tensor_tensor(k_lo[:, sl], ps_k[0:LAT, i, :], k_hi[:, sl].bitcast(F32),
                                      ALU.subtract).then_inc(k_lo_ready, 1)
                for n in range(NQ):
                    g, i = n // NC, n % NC
                    wait_past(dve, q_hi_ready, NQ * b + n + 1)
                    sl = slice(i * HALF, (i + 1) * HALF)
                    dve.tensor_tensor(q_lo[:, g % 2, sl], ps_q[:, i, :], q_hi[:, g % 2, sl].bitcast(F32),
                                      ALU.subtract).then_inc(q_lo_ready, 1)
                    if has_next:
                        if n < 4:
                            measure_x(b + 1, chain, range(2 * n, 2 * n + 2))
                        if n == 3:
                            conclude_x(chain)
                        if n == 5:
                            scale_x(b + 1, chain, range(NT // 2))
                        if n == 7:
                            scale_x(b + 1, chain, range(NT // 2, NT))

            first = rows_of(0)
            measure_x(0, first, range(NT))
            conclude_x(first)
            scale_x(0, first, range(NT))
            with dve.Fori(0, B - 1) as b:
                split(b, True)
            split(B - 1, False)
            dve.wait_ge(weights_in, 16 * NW)
            dve.tensor_copy(c["ident_b"][:, :], c["ident"][:, :]).then_inc(consts_made, 1)
            dve.tensor_copy(c["mask_q"][:, :], masks[:, 0, :]).then_inc(consts_made, 1)
            dve.tensor_copy(c["mask_k"][:, :], masks[:, 1, :]).then_inc(consts_made, 1)
            dve.wait_ge(consts_made, 4)
            dve.wait_ge(w1_in, 16)
            for e in range(E):
                dve.wait_ge(w1_hi_ready, e + 1)
                dve.tensor_tensor(c["w1_lo"][:, e, :, :], w1[:, e, :, :], c["w1_hi"][:, e, :, :].bitcast(F32),
                                  ALU.subtract).then_inc(w1_lo_ready, 1)
            dve.wait_ge(w1_lo_ready, E)

        @block.gpsimd
        def _(pool):
            for count in (x_in, var_ready, std_ready, xn_ready, turned, xt_ready, q_made, q_hi_ready,
                          q_lo_ready, k_made, k_hi_ready, k_lo_ready, v_made,
                          lat_ready, kv_out, *q_out):
                pool.sem_inc(count, 1)
            pool.sem_inc(given, 1)
            pool.wait_ge(given, 1)

        @block.scalar
        def _(act):
            act.wait_ge(given, 1)

            def root(b):
                wait_past(act, var_ready, b + 1)
                nc.scalar.activation(std[:, :], var[:, :], ACT.Sqrt).then_inc(std_ready, 1)

            def take_turned(b):
                wait_past(act, q_made, NQ * b)
                for i in range(2):
                    wait_past(act, turned, 2 * b + i + 1)
                    nc.scalar.copy(x_t[:, i * HALF:(i + 1) * HALF], ps_t[:, i, :]).then_inc(xt_ready, 1)

            def take_products(b, has_next):
                wait_past(act, kv_out, 16 * (2 + NG) * b)
                for i in range(NC):
                    wait_past(act, k_made, NC * b + i + 1)
                    nc.scalar.copy(k_hi[:, i * HALF:(i + 1) * HALF], ps_k[0:LAT, i, :]).then_inc(k_hi_ready, 1)
                wait_past(act, v_made, b + 1)
                nc.scalar.copy(lat[:, :, :], ps_v[:, 0:NT * LAT].rearrange("p (t c) -> p t c", t=NT))\
                    .then_inc(lat_ready, 1)
                for n in range(NQ):
                    g, i = n // NC, n % NC
                    if i == 0:
                        wait_past(act, q_out[g % 2], 16 * 2 * (2 * b + g // 2))
                    wait_past(act, q_made, NQ * b + n + 1)
                    nc.scalar.copy(q_hi[:, g % 2, i * HALF:(i + 1) * HALF], ps_q[:, i, :]).then_inc(q_hi_ready, 1)
                    if n == 5 and has_next:
                        root(b + 1)
                if has_next:
                    take_turned(b + 1)

            root(0)
            act.wait_ge(wqk_made, 1)
            nc.scalar.copy(wqk[:, :, :], ps_w[:, :].rearrange("d (h c) -> d h c", h=H)).then_inc(wqk_copied, 1)
            act.wait_ge(wy_made, 1)
            nc.scalar.copy(c["wy1"][:, :, :], ps_w[:, :].rearrange("r (g d) -> r g d", g=NG)).then_inc(wy_copied, 1)
            take_turned(0)
            with act.Fori(0, B - 1) as b:
                take_products(b, True)
            take_products(B - 1, False)
            act.wait_ge(w1_in, 16)
            for e in range(E):
                nc.scalar.copy(c["w1_hi"][:, e, :, :], w1[:, e, :, :]).then_inc(w1_hi_ready, 1)

        @block.tensor
        def _(pe):
            pe.wait_ge(given, 1)
            pe.wait_ge(weights_in, 16 * NW)
            for h in range(H):
                last = pe.matmul(ps_w[:, h * LAT:(h + 1) * LAT], wq_t[:, h, :], wk_t[:, h, :],
                                 start=True, stop=True)
            last.then_inc(wqk_made, 1)
            pe.wait_ge(wqk_copied, 1)
            for h in range(H):
                j, g = h % GH, h // GH
                last = pe.matmul(ps_w[R * j:R * j + R, g * D:(g + 1) * D], wv_t[:, h, :], wout[:, h, :],
                                 start=True, stop=True)
            last.then_inc(wy_made, 1)

            def turn_x(b):
                wait_past(pe, xn_ready, b + 1)
                wait_past(pe, xt_ready, 2 * b)
                for i in range(NT):
                    tr = pe.transpose(ps_t[:, i // 4, (i % 4) * P:(i % 4 + 1) * P], xn[:, i, :], c["ident"][:, :])
                    if i % 4 == 3:
                        tr.then_inc(turned, 1)

            def products(b, has_next):
                wait_past(pe, xt_ready, 2 * b + 2)
                wait_past(pe, k_lo_ready, NC * b)
                for i in range(NC):
                    pe.matmul(ps_k[0:LAT, i, :], wkv[:, :], x_t[:, i * HALF:(i + 1) * HALF],
                              start=True, stop=True).then_inc(k_made, 1)
                wait_past(pe, lat_ready, b)
                for i in range(NT):
                    last = pe.matmul(ps_v[:, i * LAT:(i + 1) * LAT], x_t[:, i * P:(i + 1) * P], wkv[:, :],
                                     start=True, stop=True)
                last.then_inc(v_made, 1)
                for n in range(NQ):
                    g, i = n // NC, n % NC
                    if n >= 2:
                        wait_past(pe, q_lo_ready, NQ * b + n - 1)
                    else:
                        wait_past(pe, q_lo_ready, NQ * b)
                    pe.matmul(ps_q[:, i, :], wqk[:, g * GH:(g + 1) * GH, :], x_t[:, i * HALF:(i + 1) * HALF],
                              start=True, stop=True).then_inc(q_made, 1)
                if has_next:
                    turn_x(b + 1)

            turn_x(0)
            with pe.Fori(0, B - 1) as b:
                products(b, True)
            products(B - 1, False)
            pe.wait_ge(wy_copied, 1)


def attend(nc, tag, causal, q_hi_d, q_lo_d, k_hi_d, k_lo_d, v_d, y_d, scale, t, c):
    TILES = [(ch, k) for ch in range(NC) for k in range((ch + 1) * NT // NC if causal else NT)]
    NCT = len(TILES)
    ENDS = [max(n for n, x in enumerate(TILES) if x[0] == ch) for ch in range(NC)]
    UNITS = [(i, j, kk) for i in range(NT) for kk in range(i // 4 + 1 if causal else NC) for j in range(GH)]
    NU = len(UNITS)
    SPAN = NCT - (4 if causal else 1)
    NB = 3
    NP = 4
    NS = 3 if causal else 4
    DEN_COL = 0 if causal else HD2
    POOL_HEADS = GH - 1
    AT_SUM, AT_DEN, AT_REC = (2, 3, 4) if causal else (None, 1, 3)
    NW = 4 if causal else 3
    NLOAD = 6 if causal else 3 + 3 * GH
    KROWS = ROW_M + (1 if causal else GH)

    ADDED = [sum(kt > 0 for _, kt in TILES[:k + 1]) for k in range(NCT)]

    def added(s, k, heads):
        return heads * (s * ADDED[-1] + (ADDED[k] if k >= 0 else ADDED[k + NCT] - ADDED[-1]))

    room = np.cumsum([0] + [2 * HALF - (max(0, (kt - 4 * ch) * P) if causal else 0) for ch, kt in TILES[:SPAN]])
    cost = np.cumsum([0] + [64 + ((i % 4) * P + P if causal and kk == i // 4 else HALF) for i, _, kk in UNITS])
    BEFORE = [int(np.searchsorted(cost, cost[-1] * room[k] / room[-1] - 1e-6)) for k in range(SPAN + 1)]

    def work_at(k, has_prev, has_next):
        work = []
        if has_next:
            if k < SPAN:
                work += [("unit", n) for n in range(BEFORE[k], BEFORE[k + 1])]
            if k == SPAN:
                work += [("turned", 0), ("turned", 1)]
        for ch, first in ((1, 0), (0, ENDS[0] + 1)):
            if ch == 0 or has_prev:
                if k == first + AT_DEN:
                    work.append(("den", ch))
                if causal and k == first + AT_SUM:
                    work.append(("sum", ch))
                if k == first + AT_REC:
                    work.append(("rec", ch))
        return work

    def plan(has_prev, has_next):
        n, out = 0, []
        for k in range(NCT):
            here = work_at(k, has_prev, has_next)
            out.append([(n + i, *w) for i, w in enumerate(here)])
            n += len(here)
        return out, n

    NWK = plan(True, True)[1]
    HEAD = NU + 2
    SHORT = NWK - plan(False, True)[1]
    assert NCT % NP == 0 and NCT * GH % NS == 0 and (NB == NW or NWK % NW == 0)

    def work_base(s):
        return HEAD if isinstance(s, int) and s == 0 else s * NWK + HEAD - SHORT

    def work_bank(s_is_0, buf, n):
        return (HEAD + n) % NW if s_is_0 else (buf * NWK + HEAD - SHORT + n) % NW

    with ExitStack() as ctx:
        def sb(name, shape, dt=F32):
            return ctx.enter_context(nc.sbuf_tensor(f"{tag}_{name}", shape, dt))

        def sem(name):
            return ctx.enter_context(nc.semaphore(f"{tag}_{name}"))

        many = [sb(f"many{i}", [P, GH, L], F32R) for i in range(NB)]
        one = [sb(f"one{i}", [P, L], F32R) for i in range(NB)]
        v = [sb(f"v{i}", [P, NT, R if causal else GH * R]) for i in range(NB)]
        rows = sb("rows", [P, L if causal else GH * L])
        probs = sb("probs", [P, NP, GH, HALF])
        y = sb("y", [P, NC, HALF])
        raw = sb("raw", [P, NC, HALF])
        den = sb("den", [P, HALF]) if causal else None
        sums = sb("sums", [P, NC, GH, HALF]) if causal else None
        rec = sb("rec", [P, 4, GH])
        wide = sb("wide", [P, 4, GH, R])
        part_max = sb("part_max", [P, NT, GH, NC])
        neg_max = sb("neg_max", [P, NT, ROW_M + GH])
        ps_s = ctx.enter_context(nc.psum_tensor(f"{tag}_ps_s", [P, NS, HALF], F32))
        ps_w = ctx.enter_context(nc.psum_tensor(f"{tag}_ps_w", [P, NW, HALF], F32))
        ps_o = ctx.enter_context(nc.psum_tensor(f"{tag}_ps_o", [P, HALF], F32))

        filled = sem("filled")
        filled_later = sem("filled_later")
        rows_in = sem("rows_in")
        rows_filled = sem("rows_filled")
        operands_in = [sem(f"operands_in{i}") for i in range(NB)]
        v_in = [sem(f"v_in{i}") for i in range(NB)]
        work_full = sem("work_full")
        work_free = sem("work_free")
        neg_ready = sem("neg_ready")
        max_in = sem("max_in")
        scores_ready = sem("scores_ready")
        exp_done = sem("exp_done")
        pv_done = sem("pv_done")
        raw_ready = sem("raw_ready")
        pool_added = sem("pool_added")
        dve_added = sem("dve_added")
        den_ready = sem("den_ready")
        rec_ready = sem("rec_ready")
        wide_ready = sem("wide_ready")
        y_ready = sem("y_ready")
        y_out = [sem(f"y_out{i}") for i in range(NC)]
        block = ctx.enter_context(nc.Block())
        NFILL = 3

        def fill(eng, i, done):
            if causal:
                eng.memset(one[i][ROW_M:ROW_M + 1, :].bitcast(F32), 1.0).then_inc(done, 1)
            else:
                eng.memset(many[i][0:ROW_M, :, :].bitcast(F32), 0.0).then_inc(done, 1)

        def add_up(eng, s, k, j):
            ch, kt = TILES[k]
            if kt == 0:
                return
            mine, done = (POOL_HEADS, pool_added) if j < POOL_HEADS else (GH - POOL_HEADS, dve_added)
            lo = first_col(ch, kt)
            eng.wait_ge(exp_done, s * GH * NCT + GH * k + j + 1)
            wait_from(eng, done, added(s, k, mine) - 2 * mine + j % mine + 1)
            so_far = sums[:, ch, j, :]
            if kt == 1:
                wait_from(eng, den_ready, (s - 1) * NC + ch + 1)
                so_far = probs[:, (k - 1) % NP, j, :]
                if lo > 0:
                    eng.tensor_tensor(sums[:, ch, j, 0:lo].rearrange("p (n r) -> p n r", r=R),
                                      so_far[:, 0:lo].rearrange("p (n r) -> p n r", r=R),
                                      c["ones"][:, :].unsqueeze(1).to_broadcast([P, lo // R, R]), ALU.mult)
            eng.tensor_tensor(sums[:, ch, j, lo:HALF], so_far[:, lo:HALF], probs[:, k % NP, j, lo:HALF],
                              ALU.add).then_inc(done, 1)

        def first_col(ch, k):
            return max(0, (k - ch * 4) * P) if causal else 0

        def run_steps(eng, step):
            step(0, 0, 0, False, True)
            step(1, 1, 0, True, True)
            with eng.Fori(0, (GROUPS - 4) // NB) as it:
                step(it * NB + 2, 2, it, True, True)
                step(it * NB + 3, 0, it + 1, True, True)
                step(it * NB + 4, 1, it + 1, True, True)
            for s in range(GROUPS - 2, GROUPS):
                step(s, s % NB, s // NB, True, s < GROUPS - 1)

        def after(buf, rnd, n=1):
            return (buf + n) % NB, rnd + (buf + n) // NB

        @block.sync
        def _(sp):
            def load_operands(g, buf, not_filled=False):
                if causal:
                    heads = q_hi_d[g].rearrange("(j r) n -> r j n", j=GH)
                    lows = q_lo_d[g].rearrange("(j r) n -> r j n", j=GH)
                    pairs = [(many[buf][ROW_H0:ROW_H0 + R, :, :], heads), (many[buf][ROW_H1:ROW_H1 + R, :, :], heads),
                             (many[buf][ROW_L:ROW_L + R, :, :], lows),
                             (one[buf][ROW_H0:ROW_H0 + R, :], k_hi_d[g]), (one[buf][ROW_H1:ROW_H1 + R, :], k_lo_d[g]),
                             (one[buf][ROW_L:ROW_L + R, :], k_hi_d[g])]
                else:
                    pairs = [(one[buf][ROW_H0:ROW_H0 + R, :], q_hi_d[g]), (one[buf][ROW_H1:ROW_H1 + R, :], q_hi_d[g]),
                             (one[buf][ROW_L:ROW_L + R, :], q_lo_d[g])]
                    for j in range(GH):
                        own = slice(j * HD2, (j + 1) * HD2)
                        for row, src in ((ROW_H0, k_hi_d), (ROW_H1, k_lo_d), (ROW_L, k_hi_d)):
                            pairs.append((many[buf][row + j * HD2:row + (j + 1) * HD2, j, :], src[g, own, :]))
                assert len(pairs) == NLOAD
                for n, (dst, src) in enumerate(pairs):
                    if not_filled and n == (0 if causal else 3):
                        sp.wait_ge(filled, NFILL)
                    sp.dma_start(dst.bitcast(F32), src).then_inc(operands_in[buf], 16)

            def load_v(g, buf):
                src = v_d[g] if causal else v_d[g].rearrange("p t j r -> p t (j r)")
                sp.dma_start(v[buf][:, :, :], src).then_inc(v_in[buf], 16)

            def place_max(g, buf, turned_at):
                hold(sp, work_free, turned_at, filled, NFILL, 0)
                sp.dma_start(many[buf][ROW_M:ROW_M + 1, :, :].bitcast(F32),
                             rows[ROW_M:ROW_M + GH, :]).then_inc(max_in, 16)

            def store(s, ch):
                hold(sp, y_ready, s * NC + ch + 1, filled, NFILL, 0)
                sp.dma_start(y_d[s][:, ch * HALF:(ch + 1) * HALF], y[:, ch, :]).then_inc(y_out[ch], 16)

            def step(s, buf, rnd, has_prev, has_next):
                if not (isinstance(s, int) and s >= GROUPS - 2):
                    if has_prev:
                        hold(sp, scores_ready, s * GH * NCT, filled, NFILL, 0)
                    load_operands(s + 2, (buf + 2) % NB)
                    if has_prev:
                        hold(sp, pv_done, s * NCT, filled, NFILL, 0)
                    load_v(s + 2, (buf + 2) % NB)
                if has_prev:
                    store(s - 1, 1)
                store(s, 0)
                if has_next and causal:
                    listed = plan(has_prev, has_next)[0]
                    last = max(n for here in listed for n, kind, _ in here if kind == "turned")
                    place_max(s + 1, (buf + 1) % NB, work_base(s) + last + 1)

            if not causal:
                sp.dma_start(rows[ROW_M:ROW_M + GH, :], t["head_rows"]).then_inc(rows_in, 16)
            load_operands(0, 0, not_filled=True)
            load_v(0, 0)
            sp.wait_ge(filled_later, NB - 1)
            load_operands(1, 1)
            load_v(1, 1)
            if causal:
                place_max(0, 0, HEAD)
            run_steps(sp, step)
            store(GROUPS - 1, 1)
            for ch in range(NC):
                sp.wait_ge(y_out[ch], 16 * GROUPS)

        @block.tensor
        def _(pe):
            def max_unit(w, bank, buf, n):
                i, j, kk = UNITS[n]
                diag = causal and kk == i // 4
                off = (i % 4) * P
                width = off + P if diag else HALF
                wait_from(pe, work_free, w - NW + 1)
                q = many[buf][0:ROW_M, j, i * P:(i + 1) * P] if causal else one[buf][0:ROW_M, i * P:(i + 1) * P]
                k = one[buf][0:ROW_M, kk * HALF:kk * HALF + width] if causal \
                    else many[buf][0:ROW_M, j, kk * HALF:kk * HALF + width]
                last = pe.matmul(ps_w[:, bank, 0:width], q, k, start=True, stop=not diag)
                if diag:
                    last = pe.matmul(ps_w[:, bank, off:width], c["ident_b"][:, :], c["mask_q"][:, :],
                                     start=False, stop=True)
                last.then_inc(work_full, 1)

            def turn_max(w, bank, g, hb):
                pe.wait_ge(neg_ready, g + 1)
                wait_from(pe, work_free, w - NW + 1)
                for ii in range(4):
                    last = pe.transpose(ps_w[0:ROW_M + GH, bank, ii * P:(ii + 1) * P],
                                        neg_max[:, hb * 4 + ii, :], c["ident"][:, :])
                last.then_inc(work_full, 1)

            def sum_up(w, bank, s, ch):
                pe.wait_ge(pool_added, added(s, ENDS[ch], POOL_HEADS))
                pe.wait_ge(dve_added, added(s, ENDS[ch], GH - POOL_HEADS))
                wait_from(pe, work_free, w - NW + 1)
                for j in range(GH):
                    last = pe.matmul(ps_w[R * j:R * j + R, bank, :], c["ones"][:, :], sums[:, ch, j, :],
                                     start=True, stop=True)
                last.then_inc(work_full, 1)

            def turn_den(w, bank, s, ch):
                pe.wait_ge(den_ready if causal else raw_ready, s * NC + ch + 1)
                wait_from(pe, work_free, w - NW + 1)
                for i in range(4):
                    cols = slice(i * P, (i + 1) * P)
                    last = pe.transpose(ps_w[:, bank, cols], den[:, cols] if causal else raw[:, ch, cols],
                                        c["ident"][:, :])
                last.then_inc(work_full, 1)

            def turn_rec(w, bank, s, ch):
                pe.wait_ge(wide_ready, s * NC + ch + 1)
                wait_from(pe, work_free, w - NW + 1)
                for i in range(4):
                    last = pe.transpose(ps_w[:, bank, i * P:(i + 1) * P],
                                        wide[:, i, :, :].rearrange("p j r -> p (j r)"), c["ident"][:, :])
                last.then_inc(work_full, 1)

            def scores(s, buf, k, j):
                ch, kt = TILES[k]
                lo = first_col(ch, kt)
                diag = causal and kt >= 4 * ch
                slot = (GH * k + j) % NS
                wait_from(pe, exp_done, s * GH * NCT + GH * k + j - NS + 1)
                cols = slice(ch * HALF + lo, (ch + 1) * HALF)
                keys = slice(kt * P, (kt + 1) * P)
                lhs = one[buf][0:KROWS, keys] if causal else many[buf][0:KROWS, j, keys]
                rhs = many[buf][0:KROWS, j, cols] if causal else one[buf][0:KROWS, cols]
                last = pe.matmul(ps_s[:, slot, lo:HALF], lhs, rhs, start=True, stop=not diag)
                if diag:
                    last = pe.matmul(ps_s[:, slot, lo:lo + P], c["ident_b"][:, :], c["mask_k"][:, :],
                                     start=False, stop=True)
                last.then_inc(scores_ready, 1)

            def value_waits(s, buf, rnd, k):
                pe.wait_ge(exp_done, s * GH * NCT + GH * (k + 1))
                if k == 0:
                    pe.wait_ge(v_in[buf], (rnd + 1) * 16)
                if TILES[k][1] == 0:
                    wait_from(pe, raw_ready, s * NC + TILES[k][0])

            def values(buf, k):
                ch, kt = TILES[k]
                lo = first_col(ch, kt)
                for j in range(GH):
                    lhs = v[buf][:, kt, :] if causal else v[buf][:, kt, j * R:(j + 1) * R]
                    last = pe.matmul(ps_o[R * j:R * j + R, lo:HALF], lhs, probs[:, k % NP, j, lo:HALF],
                                     start=kt == 0, stop=k in ENDS)
                last.then_inc(pv_done, 1)

            def step(s, buf, rnd, has_prev, has_next):
                uses, _ = plan(has_prev, has_next)
                base = work_base(s)
                nbuf, nrnd = after(buf, rnd)

                def work(k, quarter):
                    here = uses[k]
                    for n, kind, what in here[len(here) * quarter // 4:len(here) * (quarter + 1) // 4]:
                        bank = work_bank(not has_prev, buf, n)
                        if kind == "unit":
                            if what == 0:
                                pe.wait_ge(operands_in[nbuf], (nrnd + 1) * 16 * NLOAD)
                            max_unit(base + n, bank, nbuf, what)
                        elif kind == "turned":
                            turn_max(base + n, bank, s + 1, what)
                        elif kind == "sum":
                            sum_up(base + n, bank, s - what, what)
                        elif kind == "den":
                            turn_den(base + n, bank, s - what, what)
                        else:
                            turn_rec(base + n, bank, s - what, what)

                if causal:
                    pe.wait_ge(max_in, (s + 1) * 16)
                elif has_prev:
                    listed = plan(True, True)[0]
                    last = max(n for here in listed for n, kind, _ in here if kind == "turned")
                    pe.wait_ge(work_free, work_base(s) - NWK + last + 1)
                else:
                    pe.wait_ge(rows_filled, NB)
                    pe.wait_ge(work_free, HEAD)
                for k in range(NCT):
                    here = (s, buf, rnd, k - 1) if k > 0 else (s - 1, (buf - 1) % NB, after(buf, rnd, -1)[1], NCT - 1)
                    late = k > 0 or has_prev
                    for j in range(GH):
                        scores(s, buf, k, j)
                        work(k, j)
                    if late:
                        value_waits(*here)
                        values(here[1], here[3])

            pe.wait_ge(filled, NFILL)
            pe.wait_ge(operands_in[0], 16 * NLOAD)
            for n in range(NU):
                max_unit(n, n % NW, 0, n)
            for hb in range(2):
                turn_max(NU + hb, (NU + hb) % NW, 0, hb)
            run_steps(pe, step)
            s, base = GROUPS - 1, work_base(GROUPS - 1) + plan(True, False)[1]
            value_waits(s, s % NB, s // NB, NCT - 1)
            values(s % NB, NCT - 1)
            if causal:
                sum_up(base, base % NW, s, 1)
                base += 1
            turn_den(base, base % NW, s, 1)
            turn_rec(base + 1, (base + 1) % NW, s, 1)

        @block.gpsimd
        def _(pool):
            def spread(s, ch):
                pool.wait_ge(rec_ready, s * NC + ch + 1)
                wait_from(pool, y_ready, s * NC + ch)
                pool.tensor_tensor(wide[:, :, :, :], rec[:, :, :].unsqueeze(3).to_broadcast([P, 4, GH, R]),
                                   c["ones"][:, :].unsqueeze(1).unsqueeze(1).to_broadcast([P, 4, GH, R]),
                                   ALU.mult).then_inc(wide_ready, 1)

            def step(s, buf, rnd, has_prev, has_next):
                for k in range(NCT):
                    for j in range(POOL_HEADS if causal else 0):
                        add_up(pool, s, k, j)
                    if k == AT_DEN and has_prev:
                        spread(s - 1, 1)
                    if k == ENDS[0] + 1 + AT_DEN:
                        spread(s, 0)

            for i in range(1, NB):
                fill(pool, i, filled_later)
            run_steps(pool, step)
            spread(GROUPS - 1, 1)

        @block.scalar
        def _(act):
            def take_raw(s, ch):
                act.wait_ge(pv_done, s * NCT + ENDS[ch] + 1)
                wait_from(act, y_ready, (s - 1) * NC + ch + 1)
                nc.scalar.copy(raw[:, ch, :], ps_o[:, :]).then_inc(raw_ready, 1)

            def step(s, buf, rnd, has_prev, has_next):
                for k in range(NCT):
                    ch, kt = TILES[k]
                    lo = first_col(ch, kt)
                    wait_from(act, pv_done, s * NCT + k - NP + 1)
                    if causal:
                        last = k - NP + (TILES[k - NP][1] == 0)
                        wait_from(act, pool_added, added(s, last, POOL_HEADS))
                        wait_from(act, dve_added, added(s, last, GH - POOL_HEADS))
                    for j in range(GH):
                        act.wait_ge(scores_ready, s * GH * NCT + GH * k + j + 1)
                        nc.scalar.activation(probs[:, k % NP, j, lo:HALF], ps_s[:, (GH * k + j) % NS, lo:HALF],
                                             ACT.Exp, scale=scale).then_inc(exp_done, 1)
                    if k == 0 and has_prev:
                        take_raw(s - 1, 1)
                    if k == ENDS[0] + 1:
                        take_raw(s, 0)

            if not causal:
                act.wait_ge(rows_in, 16)
                for i in range(NB):
                    nc.scalar.copy(many[i][ROW_M:ROW_M + GH, :, :],
                                   rows[ROW_M:ROW_M + GH, :].rearrange("r (j n) -> r j n", j=GH)).then_inc(rows_filled, 1)
            run_steps(act, step)
            take_raw(GROUPS - 1, 1)

        @block.vector
        def _(dve):
            def max_unit(w, bank, n):
                i, j, kk = UNITS[n]
                width = (i % 4) * P + P if causal and kk == i // 4 else HALF
                dve.wait_ge(work_full, w + 1)
                dve.reduce_max(part_max[:, i, j, kk:kk + 1], ps_w[:, bank, 0:width], AX.X).then_inc(work_free, 1)

            def negate_max(w):
                dve.wait_ge(work_free, w)
                dve.tensor_reduce(neg_max[:, :, ROW_M:ROW_M + GH], part_max[:, :, :, :], AX.X, ALU.max,
                                  negate=True).then_inc(neg_ready, 1)

            def take_turned(w, bank, g, buf, hb):
                if causal and hb == 0:
                    wait_from(dve, max_in, g * 16)
                dve.wait_ge(work_full, w + 1)
                sl = slice(hb * HALF, (hb + 1) * HALF)
                dst = rows[ROW_M:ROW_M + GH, sl].bitcast(F32R) if causal else one[buf][ROW_M:ROW_M + GH, sl]
                dve.tensor_copy(dst, ps_w[ROW_M:ROW_M + GH, bank, :]).then_inc(work_free, 1)

            def take_sum(w, bank, s, ch):
                dve.wait_ge(work_full, w + 1)
                dve.tensor_copy(den[:, :], ps_w[:, bank, :]).then_inc(work_free, 1)
                dve.wait_ge(work_free, w + 1)
                dve.sem_inc(den_ready, 1)

            def invert(w, bank, s, ch):
                dve.wait_ge(work_full, w + 1)
                wait_from(dve, wide_ready, s * NC + ch)
                dve.reciprocal(rec[:, :, :], ps_w[:, bank, :].rearrange("p (i j r) -> p i j r", i=4, j=GH)[
                    :, :, :, DEN_COL]).then_inc(work_free, 1)
                dve.wait_ge(work_free, w + 1)
                dve.sem_inc(rec_ready, 1)

            def divide(w, bank, s, rnd, ch):
                dve.wait_ge(work_full, w + 1)
                dve.wait_ge(raw_ready, s * NC + ch + 1)
                wait_from(dve, y_out[ch], s * 16)
                dve.tensor_tensor(y[:, ch, :], raw[:, ch, :], ps_w[:, bank, :], ALU.mult).then_inc(work_free, 1)
                dve.wait_ge(work_free, w + 1)
                dve.sem_inc(y_ready, 1)

            def add_before(s, k, has_prev):
                for j in range(POOL_HEADS, GH):
                    if k > 0:
                        add_up(dve, s, k - 1, j)
                    elif has_prev:
                        add_up(dve, s - 1, NCT - 1, j)

            def step(s, buf, rnd, has_prev, has_next):
                uses, _ = plan(has_prev, has_next)
                base = work_base(s)
                nbuf, _ = after(buf, rnd)
                for k in range(NCT):
                    for at, (n, kind, what) in enumerate(uses[k]):
                        if causal and at == len(uses[k]) // 2:
                            add_before(s, k, has_prev)
                        bank = work_bank(not has_prev, buf, n)
                        if kind == "unit":
                            max_unit(base + n, bank, what)
                            if what == NU - 1:
                                negate_max(base + n + 1)
                        elif kind == "turned":
                            take_turned(base + n, bank, s + 1, nbuf, what)
                        elif kind == "sum":
                            take_sum(base + n, bank, s - what, what)
                        elif kind == "den":
                            invert(base + n, bank, s - what, what)
                        else:
                            divide(base + n, bank, s - what, rnd, what)
                    if causal and not uses[k]:
                        add_before(s, k, has_prev)

            dve.memset(part_max[:, :, :, :], -3e38).then_inc(filled, 1)
            dve.memset(neg_max[:, :, :], 0.0).then_inc(filled, 1)
            fill(dve, 0, filled)
            dve.wait_ge(filled, NFILL)
            for n in range(NU):
                max_unit(n, n % NW, n)
            negate_max(NU)
            for hb in range(2):
                take_turned(NU + hb, (NU + hb) % NW, 0, 0, hb)
            run_steps(dve, step)
            s, base = GROUPS - 1, work_base(GROUPS - 1) + plan(True, False)[1]
            if causal:
                for j in range(POOL_HEADS, GH):
                    add_up(dve, s, NCT - 1, j)
                take_sum(base, base % NW, s, 1)
                base += 1
            invert(base, base % NW, s, 1)
            divide(base + 1, (base + 1) % NW, s, s // NB, 1)


def prepare_second(nc, t, s, c):
    with ExitStack() as ctx:
        def sb(name, shape, dt=F32):
            return ctx.enter_context(nc.sbuf_tensor(f"m_{name}", shape, dt))

        def sem(name):
            return ctx.enter_context(nc.semaphore(f"m_{name}"))

        def bank(name, n=2):
            return ctx.enter_context(nc.psum_tensor(f"m_{name}", [P, n, HALF], F32))

        wq, wk, wv = (sb(n, [D, D]) for n in ("wq", "wk", "wv"))
        wqs, wks = (sb(n, [D, D]) for n in ("wqs", "wks"))
        bqk = sb("bqk", [D, 2, 2])
        rope = sb("rope", [D, 2, L])
        turn_a, turn_b = sb("turn_a", [D, 2, HALF]), sb("turn_b", [D, 2, HALF])
        qk = sb("qk", [D, 2, L])
        bv = sb("bv", [P, D])
        y = sb("y", [P, NG, L])
        x = sb("x", [P, NT, D])
        an = sb("an", [P, NT, D])
        xmid = sb("xmid", [P, NT, D])
        xn = sb("xn", [P, NT, D])
        x_t = sb("x_t", [D, L])
        st, mv = sb("st", [P, NT, 6]), sb("mv", [P, NT, 2])
        var, std, rstd = sb("var", [P, NT]), sb("std", [P, NT]), sb("rstd", [P, NT])
        hi = sb("hi", [P, 2, L], F32R)
        lo = sb("lo", [P, 2, L], F32R)
        v_ext = sb("v_ext", [P, NG, NT, GH, R])
        ps_a, ps_t, ps_q, ps_v = bank("ps_a"), bank("ps_t"), bank("ps_q"), bank("ps_v")

        weights_in = sem("weights_in")
        v_filled = sem("v_filled")
        y_in = sem("y_in")
        x_in = sem("x_in")
        a_made = sem("a_made")
        steps = sem("steps")
        var_ready = sem("var_ready")
        std_ready = sem("std_ready")
        xmid_ready = sem("xmid_ready")
        xn_ready = sem("xn_ready")
        turned = sem("turned")
        xt_ready = sem("xt_ready")
        q_made = sem("q_made")
        turned_by = sem("turned_by")
        roped = sem("roped")
        hi_ready = sem("hi_ready")
        lo_ready = sem("lo_ready")
        v_made = sem("v_made")
        v_ready = sem("v_ready")
        mid_out = sem("mid_out")
        qk_out = sem("qk_out")
        v_out = sem("v_out")
        given = sem("given")
        block = ctx.enter_context(nc.Block())
        NQ = 2 * NC
        NWT = 8
        STEPS = 2 * LN_STEPS + 1

        @block.sync
        def _(sp):
            sp.wait_ge(given, 1)
            y1 = s["y1"].rearrange("(b g) p l -> b p g l", g=NG)
            sp.dma_start(y[:, :, :], y1[0]).then_inc(y_in, 16)
            sp.dma_start(x[:, :, :], t["x"][0].rearrange("(t p) d -> p t d", p=P)).then_inc(x_in, 16)
            sp.dma_start(wq[:, :], t["wq"]).then_inc(weights_in, 16)
            sp.dma_start(wk[:, :], t["wk"]).then_inc(weights_in, 16)
            sp.dma_start(wv[:, :], t["wv"]).then_inc(weights_in, 16)
            sp.dma_start(wqs[:, :], t["wqs"]).then_inc(weights_in, 16)
            sp.dma_start(wks[:, :], t["wks"]).then_inc(weights_in, 16)
            sp.dma_start(rope[:, :, :], t["rope"]).then_inc(weights_in, 16)
            sp.dma_start(bqk[:, :, :], t["bqk"]).then_inc(weights_in, 16)
            sp.dma_start(bv[:, :], t["bv"]).then_inc(weights_in, 16)

            def load_attended(b):
                hold(sp, a_made, 2 * b, weights_in, 16 * NWT)
                sp.dma_start(y[:, :, :], y1[b]).then_inc(y_in, 16)

            def load_x(b):
                hold(sp, xmid_ready, b, weights_in, 16 * NWT)
                sp.dma_start(x[:, :, :], t["x"][b].rearrange("(t p) d -> p t d", p=P)).then_inc(x_in, 16)

            def store_rows(b):
                hold(sp, xmid_ready, b + 1, weights_in, 16 * NWT)
                sp.dma_start(s["xmid"][b], xmid[:, :, :]).then_inc(mid_out, 16)
                hold(sp, xn_ready, b + 1, weights_in, 16 * NWT)
                sp.dma_start(s["xn2"][b], xn[:, :, :]).then_inc(mid_out, 16)

            def store_operands(b):
                for i, (dh, dl) in enumerate((("q2h", "q2l"), ("k2h", "k2l"))):
                    hold(sp, lo_ready, NQ * b + NC * (i + 1), weights_in, 16 * NWT)
                    for dst, src in ((dh, hi), (dl, lo)):
                        sp.dma_start(s[dst].rearrange("(b g) r l -> b (g r) l", g=NG)[b],
                                     src[:, i, :].bitcast(F32)).then_inc(qk_out, 16)
                hold(sp, v_ready, NT * (b + 1), weights_in, 16 * NWT)
                sp.dma_start(s["v2"].rearrange("(b g) p t j r -> b p g (t j r)", g=NG)[b],
                             v_ext[:, :, :, :, :].rearrange("p g t j r -> p g (t j r)")).then_inc(v_out, 16)

            load_attended(1)
            store_rows(0)
            load_x(1)
            with sp.Fori(0, B - 2) as b:
                load_attended(b + 2)
                store_operands(b)
                store_rows(b + 1)
                load_x(b + 2)
            store_operands(B - 2)
            store_rows(B - 1)
            store_operands(B - 1)
            hold(sp, mid_out, 16 * 2 * B, weights_in, 16 * NWT)
            hold(sp, qk_out, 16 * 4 * B, weights_in, 16 * NWT)
            hold(sp, v_out, 16 * B, weights_in, 16 * NWT)

        @block.vector
        def _(dve):
            dve.wait_ge(given, 1)
            dve.memset(v_ext[:, :, :, :, :], 0.0).then_inc(v_filled, 1)
            dve.wait_ge(v_filled, 1)
            for g in range(NG):
                dve.memset(v_ext[:, g, :, :, HD2:HD2 + 1], 1.0).then_inc(v_filled, 1)
            dve.wait_ge(v_filled, 1 + NG)
            dve.wait_ge(weights_in, 16 * NWT)

            def attended(i):
                return ps_a[:, i // 4, (i % 4) * D:(i % 4 + 1) * D]

            def rows_of(b):
                return Chain(dve, steps, b * STEPS, STEPS)

            def measure_attended(b, chain):
                wait_past(dve, a_made, 2 * b + 2)
                measure(dve, chain, attended, range(NT), st)
                conclude(dve, chain, st, mv, var, rstd, var_ready)

            def add_residual(b, chain):
                invert_roots(dve, chain, std, rstd, std_ready, b * 2)
                scale_rows(dve, chain, attended, lambda i: an[:, i, :], range(NT), mv, rstd)
                chain.settle()
                wait_past(dve, x_in, 16 * b + 16)
                wait_past(dve, mid_out, 32 * b)
                chain.did(dve.tensor_tensor(xmid[:, :, :], an[:, :, :], x[:, :, :], ALU.add))
                chain.settle()
                dve.sem_inc(xmid_ready, 1)
                measure(dve, chain, lambda i: xmid[:, i, :], range(NT), st)
                conclude(dve, chain, st, mv, var, rstd, var_ready)

            def scale_sum(b, chain):
                wait_past(dve, turned, 2 * b)
                invert_roots(dve, chain, std, rstd, std_ready, b * 2 + 1)
                scale_rows(dve, chain, lambda i: xmid[:, i, :], lambda i: xn[:, i, :], range(NT), mv, rstd)
                chain.settle()
                chain.close()
                dve.sem_inc(xn_ready, 1)

            def rotate(b, n):
                i, ch = n // NC, n % NC
                sl = slice(ch * HALF, (ch + 1) * HALF)
                if n == 0:
                    wait_past(dve, lo_ready, NQ * b)
                wait_past(dve, q_made, NQ * b + n + 1)
                dve.scalar_tensor_tensor(out=turn_a[:, n % 2, :], in0=ps_q[:, n % 2, :], scalar=bqk[:, i, 0:1],
                                         in1=rope[:, 0, sl], op0=ALU.add, op1=ALU.mult).then_inc(turned_by, 1)
                dve.scalar_tensor_tensor(out=turn_b[:, n % 2, :], in0=ps_t[:, n % 2, :], scalar=bqk[:, i, 1:2],
                                         in1=rope[:, 1, sl], op0=ALU.add, op1=ALU.mult).then_inc(turned_by, 1)
                wait_past(dve, turned_by, (NQ * b + n + 1) * 2)
                dve.tensor_tensor(qk[:, i, sl], turn_a[:, n % 2, :], turn_b[:, n % 2, :],
                                  ALU.add).then_inc(roped, 1)

            def take_values(b):
                wait_past(dve, roped, NQ * b + NQ)
                wait_past(dve, v_out, 16 * b)
                for i in range(NT):
                    wait_past(dve, v_made, 2 * b + i // 4 + 1)
                    dve.tensor_tensor(v_ext[:, :, i, :, 0:HD2],
                                      ps_v[:, i // 4, (i % 4) * D:(i % 4 + 1) * D].rearrange(
                                          "p (g j r) -> p g j r", g=NG, j=GH),
                                      bv[:, :].rearrange("p (g j r) -> p g j r", g=NG, j=GH),
                                      ALU.add).then_inc(v_ready, 1)

            first = rows_of(0)
            measure_attended(0, first)
            add_residual(0, first)
            scale_sum(0, first)
            with dve.Fori(0, B - 1) as b:
                chain = rows_of(b + 1)
                measure_attended(b + 1, chain)
                rotate(b, 0)
                rotate(b, 1)
                add_residual(b + 1, chain)
                rotate(b, 2)
                rotate(b, 3)
                take_values(b)
                scale_sum(b + 1, chain)
            for n in range(NQ):
                rotate(B - 1, n)
            take_values(B - 1)

        @block.scalar
        def _(act):
            act.wait_ge(given, 1)
            act.wait_ge(weights_in, 16 * NWT)

            def root(nth):
                wait_past(act, var_ready, nth + 1)
                nc.scalar.activation(std[:, :], var[:, :], ACT.Sqrt).then_inc(std_ready, 1)

            def take_turned(b):
                for i in range(2):
                    wait_past(act, turned, 2 * b + i + 1)
                    if i == 0:
                        wait_past(act, v_made, 2 * b)
                    nc.scalar.copy(x_t[:, i * HALF:(i + 1) * HALF], ps_t[:, i, :]).then_inc(xt_ready, 1)

            def take_hi(b, n):
                i, ch = n // NC, n % NC
                if n == 0:
                    wait_past(act, qk_out, 16 * 4 * b)
                wait_past(act, roped, NQ * b + n + 1)
                sl = slice(ch * HALF, (ch + 1) * HALF)
                nc.scalar.copy(hi[:, i, sl], qk[:, i, sl]).then_inc(hi_ready, 1)

            root(0)
            root(1)
            take_turned(0)
            with act.Fori(0, B - 1) as b:
                root(2 * b + 2)
                take_hi(b, 0)
                take_hi(b, 1)
                root(2 * b + 3)
                take_hi(b, 2)
                take_hi(b, 3)
                take_turned(b + 1)
            for n in range(NQ):
                take_hi(B - 1, n)

        @block.gpsimd
        def _(pool):
            for count in (y_in, x_in, a_made, var_ready, std_ready, xmid_ready, xn_ready, turned, xt_ready,
                          q_made, turned_by, roped, hi_ready, lo_ready, v_made,
                          v_ready, mid_out, qk_out, v_out):
                pool.sem_inc(count, 1)
            pool.sem_inc(given, 1)
            pool.wait_ge(given, 1)
            with pool.Fori(0, B) as b:
                wait_past(pool, qk_out, 16 * 4 * b)
                for n in range(NQ):
                    i, ch = n // NC, n % NC
                    sl = slice(ch * HALF, (ch + 1) * HALF)
                    wait_past(pool, hi_ready, NQ * b + n + 1)
                    pool.tensor_tensor(lo[:, i, sl], qk[:, i, sl], hi[:, i, sl].bitcast(F32),
                                       ALU.subtract).then_inc(lo_ready, 1)

        @block.tensor
        def _(pe):
            pe.wait_ge(given, 1)
            pe.wait_ge(weights_in, 16 * NWT)

            def out_product(b):
                wait_past(pe, y_in, 16 * (b + 1))
                wait_past(pe, xmid_ready, b)
                for i in range(NT):
                    for g in range(NG):
                        last = pe.matmul(ps_a[:, i // 4, (i % 4) * D:(i % 4 + 1) * D], y[:, g, i * P:(i + 1) * P],
                                         c["wy1"][:, g, :], start=g == 0, stop=g == NG - 1)
                    if i % 4 == 3:
                        last.then_inc(a_made, 1)

            def turn_x(b):
                wait_past(pe, xn_ready, b + 1)
                wait_past(pe, turned_by, NQ * b * 2)
                for i in range(NT):
                    tr = pe.transpose(ps_t[:, i // 4, (i % 4) * P:(i % 4 + 1) * P], xn[:, i, :], c["ident"][:, :])
                    if i % 4 == 3:
                        tr.then_inc(turned, 1)

            def queries_keys(b, n):
                if n == 0:
                    wait_past(pe, xt_ready, 2 * b + 2)
                wait_past(pe, turned_by, (NQ * b + max(n - 1, 0)) * 2)
                ch = n % NC
                moving = x_t[:, ch * HALF:(ch + 1) * HALF]
                pe.matmul(ps_q[:, n % 2, :], (wq, wk)[n // NC][:, :], moving, start=True, stop=True)
                pe.matmul(ps_t[:, n % 2, :], (wqs, wks)[n // NC][:, :], moving,
                          start=True, stop=True).then_inc(q_made, 1)

            def values(b):
                wait_past(pe, v_ready, NT * b)
                for i in range(NT):
                    last = pe.matmul(ps_v[:, i // 4, (i % 4) * D:(i % 4 + 1) * D], x_t[:, i * P:(i + 1) * P],
                                     wv[:, :], start=True, stop=True)
                    if i % 4 == 3:
                        last.then_inc(v_made, 1)

            def batch(b, has_next, has_second):
                for n in range(NQ):
                    queries_keys(b, n)
                values(b)
                if has_second:
                    out_product(b + 2)
                if has_next:
                    turn_x(b + 1)

            out_product(0)
            out_product(1)
            turn_x(0)
            with pe.Fori(0, B - 2) as b:
                batch(b, True, True)
            batch(B - 2, True, False)
            batch(B - 1, False, False)


def experts(nc, t, s, c):
    with ExitStack() as ctx:
        def sb(name, shape, dt=F32):
            return ctx.enter_context(nc.sbuf_tensor(f"e_{name}", shape, dt))

        def sem(name):
            return ctx.enter_context(nc.semaphore(f"e_{name}"))

        def bank(name, n=1):
            return ctx.enter_context(nc.psum_tensor(f"e_{name}", [P, n, HALF], F32))

        T = HALF // P
        U = B * NC
        wo = sb("wo", [P, NG, D])
        wg = sb("wg", [D, E])
        w1_hi, w1_lo = c["w1_hi"], c["w1_lo"]
        w2 = sb("w2", [P, E, NF, D])
        b1 = sb("b1", [P, E, NF])
        b2 = sb("b2", [E, D])
        vecs = sb("vecs", [P, 5, D])
        bg = sb("bg", [P, E])
        y = sb("y", [P, NG, HALF])
        xn = sb("xn", [P, T, D])
        pre = sb("pre", [P, T, D])
        x1 = sb("x1", [P, T, D])
        x_t = sb("x_t", [D, HALF])
        x_hi = [sb(f"x_hi{i}", [D, HALF], F32R) for i in range(2)]
        x_lo = [sb(f"x_lo{i}", [D, HALF], F32R) for i in range(2)]
        acc = [sb(f"acc{i}", [P, T, D]) for i in range(2)]
        comb = [sb(f"comb{i}", [P, T, E]) for i in range(2)]
        fin = sb("fin", [P, T, D])
        xmid = sb("xmid", [P, T, D])

        def stats(name):
            return {"st": sb(f"st_{name}", [P, T, 6]), "mv": sb(f"mv_{name}", [P, T, 2]),
                    "var": sb(f"var_{name}", [P, T]), "std": sb(f"std_{name}", [P, T]),
                    "rstd": sb(f"rstd_{name}", [P, T]),
                    "var_ready": sem(f"var_ready_{name}"), "std_ready": sem(f"std_ready_{name}")}

        front_stats, back_stats = stats("front"), stats("back")
        logit = sb("logit", [P, T, E])
        gmax = sb("gmax", [P, T])
        gexp = sb("gexp", [P, T, E])
        gsum = sb("gsum", [P, T])
        prob = sb("prob", [P, T, 2 * E])
        left = sb("left", [P, T, 2 * E])
        top = sb("top", [P, T, 8])
        strike = sb("strike", [P, T, 8])
        comb_t = sb("comb_t", [E, HALF])
        hid = sb("hid", [P, 2, NF, HALF])
        NH = 4
        ps_a, ps_t, ps_h, ps_y = bank("ps_a"), bank("ps_t"), bank("ps_h", NH), bank("ps_y", 2)

        weights_in = sem("weights_in")
        w2_in = sem("w2_in")
        filled = sem("filled")
        y_in = sem("y_in")
        xn_in = sem("xn_in")
        xmid_in = sem("xmid_in")
        a_made = sem("a_made")
        pre_ready = sem("pre_ready")
        front_steps = sem("front_steps")
        back_steps = sem("back_steps")
        x1_ready = sem("x1_ready")
        turned = sem("turned")
        xhi_ready = sem("xhi_ready")
        xlo_ready = sem("xlo_ready")
        logits_made = sem("logits_made")
        shifted = sem("shifted")
        gexp_ready = sem("gexp_ready")
        comb_ready = sem("comb_ready")
        comb_turned = sem("comb_turned")
        comb_t_ready = sem("comb_t_ready")
        bias_made = sem("bias_made")
        acc_ready = sem("acc_ready")
        h_made = sem("h_made")
        h_ready = sem("h_ready")
        y_made = sem("y_made")
        y_added = sem("y_added")
        res_ready = sem("res_ready")
        out_done = sem("out_done")
        block = ctx.enter_context(nc.Block())
        NWT = 6
        ADDS = E * T
        HIDS = E * NF

        y2 = s["y2"].rearrange("(b g) p (c l) -> b c p g l", g=NG, c=NC)
        xn2 = s["xn2"].rearrange("b p (c t) d -> b c p t d", c=NC)
        xmid_d = s["xmid"].rearrange("b p (c t) d -> b c p t d", c=NC)
        out_d = t["out"].rearrange("b (c t p) d -> b c p t d", c=NC, p=P)

        def following(b, i):
            return (b, i + 1) if i + 1 < NC else (b + 1, 0)

        def preceding(b, i):
            return (b, i - 1) if i > 0 else (b - 1, NC - 1)

        def chunk_windows(eng, window):
            for i in range(NC):
                window(0, i, i > 0, True)
            with eng.Fori(1, B - 1) as b:
                for i in range(NC):
                    window(b, i, True, True)
            for i in range(NC):
                window(B - 1, i, True, i < NC - 1)

        def held(sp, sem_, value):
            hold(sp, sem_, value, weights_in, 16 * NWT, given=0)

        @block.sync
        def _(sp):
            sp.dma_start(y[:, :, :], y2[0, 0]).then_inc(y_in, 16)
            sp.dma_start(xn[:, :, :], xn2[0, 0]).then_inc(xn_in, 16)
            for dst, name in ((wo[:, :, :], "wo"), (vecs[:, :, :], "vecs"), (wg[:, :], "wg"), (bg[:, :], "bg"),
                              (b2[:, :], "b2"), (b1[:, :, :], "b1")):
                sp.dma_start(dst, t[name]).then_inc(weights_in, 16)

            def load(b, i):
                v = NC * b + i
                held(sp, a_made, v)
                sp.dma_start(y[:, :, :], y2[b, i]).then_inc(y_in, 16)
                held(sp, pre_ready, v)
                sp.dma_start(xn[:, :, :], xn2[b, i]).then_inc(xn_in, 16)

            def store(b, i):
                held(sp, res_ready, NC * b + i + 1)
                sp.dma_start(out_d[b, i], xmid[:, :, :]).then_inc(out_done, 16)

            def window(b, i, has_back, has_front):
                v = NC * b + i
                if has_front and not (isinstance(b, int) and b == B - 1):
                    load(b + 1, i)
                if has_back:
                    store(*preceding(b, i))
                held(sp, out_done, 16 * v)
                sp.dma_start(xmid[:, :, :], xmid_d[b, i]).then_inc(xmid_in, 16)

            sp.dma_start(w2[:, :, :, :], t["w2"]).then_inc(w2_in, 16)
            load(0, 1)
            chunk_windows(sp, window)
            store(B - 1, NC - 1)
            sp.wait_ge(out_done, 16 * U)

        FRONT = 15 + 5 * T
        BACK = 2 * (3 * T + 1) + 2

        @block.vector
        def _(dve):
            dve.memset(prob[:, :, :], -1.0).then_inc(filled, 1)
            dve.memset(strike[:, :, :], -1.0).then_inc(filled, 1)
            dve.wait_ge(weights_in, 16 * NWT)
            dve.wait_ge(filled, 2)

            def per_row(v_ap):
                return v_ap.unsqueeze(1).to_broadcast([P, T, D])

            def measure(chain, buf, k):
                for j in range(T):
                    chain.did(dve.bn_stats(k["st"][:, j, :], buf[:, j, :]))
                chain.settle()
                dve.memset(k["rstd"][:, :], 1.0)
                for j in range(T):
                    chain.did(dve.bn_aggr(k["mv"][:, j, :], k["st"][:, j, :]))
                chain.settle()
                dve.tensor_scalar(k["var"][:, :], k["mv"][:, :, 1], EPS, None, ALU.add).then_inc(k["var_ready"], 1)

            def scale(chain, buf, out, k, nth):
                wait_from(dve, k["std_ready"], nth)
                chain.did(dve.reciprocal(k["rstd"][:, :], k["std"][:, :]))
                chain.settle()
                for j in range(T):
                    chain.did(dve.tensor_scalar(out[:, j, :], buf[:, j, :], k["mv"][:, j, 0:1],
                                                k["rstd"][:, j:j + 1], ALU.subtract, ALU.mult))
                chain.settle()

            def front_input(b, i, chain):
                v = NC * b + i
                wait_from(dve, a_made, v + 1)
                chain.did(dve.tensor_tensor(pre[:, :, :], ps_a[:, 0, :].rearrange("p (t d) -> p t d", t=T),
                                            per_row(vecs[:, 0, :]), ALU.add))
                chain.settle()
                wait_from(dve, xn_in, 16 * (v + 1))
                chain.did(dve.tensor_tensor(pre[:, :, :], pre[:, :, :], xn[:, :, :], ALU.add))
                chain.settle()
                dve.sem_inc(pre_ready, 1)
                measure(chain, pre, front_stats)

            def front_norm(b, i, chain):
                v = NC * b + i
                wait_from(dve, turned, v)
                scale(chain, pre, x1, front_stats, v + 1)
                chain.did(dve.tensor_tensor(x1[:, :, :], x1[:, :, :], per_row(vecs[:, 1, :]), ALU.mult))
                chain.settle()
                chain.did(dve.tensor_tensor(x1[:, :, :], x1[:, :, :], per_row(vecs[:, 2, :]), ALU.add))
                chain.settle()
                dve.sem_inc(x1_ready, 1)

            def front_split(b, i):
                v = NC * b + i
                wait_from(dve, xhi_ready, 2 * (v + 1))
                dve.tensor_tensor(x_lo[i][:, :], x_t[:, :], x_hi[i][:, :].bitcast(F32),
                                  ALU.subtract).then_inc(xlo_ready, 1)

            def front_logits(b, i, chain):
                v = NC * b + i
                wait_from(dve, logits_made, v + 1)
                chain.did(dve.tensor_tensor(logit[:, :, :], ps_t[:, 0, 0:T * E].rearrange("p (t e) -> p t e", t=T),
                                            bg[:, :].unsqueeze(1).to_broadcast([P, T, E]), ALU.add))
                chain.settle()
                chain.did(dve.reduce_max(gmax[:, :], logit[:, :, :], AX.X))
                chain.settle()
                dve.tensor_tensor(logit[:, :, :], logit[:, :, :], gmax[:, :].unsqueeze(2).to_broadcast([P, T, E]),
                                  ALU.subtract).then_inc(shifted, 1)

            def front_gate(b, i, chain):
                v = NC * b + i
                wait_from(dve, gexp_ready, v + 1)
                chain.did(dve.reduce_sum(gsum[:, :], gexp[:, :, :], AX.X))
                chain.settle()
                chain.did(dve.reciprocal(gmax[:, :], gsum[:, :]))
                chain.settle()
                chain.did(dve.tensor_tensor(prob[:, :, 0:E], gexp[:, :, :],
                                            gmax[:, :].unsqueeze(2).to_broadcast([P, T, E]), ALU.mult))
                chain.settle()
                dve.memset(gmax[:, :], 0.0)
                for j in range(T):
                    chain.did(dve.max(top[:, j, :], prob[:, j, :]))
                chain.settle()
                chain.did(dve.tensor_copy(strike[:, :, 0:2], top[:, :, 0:2]))
                chain.settle()
                dve.memset(gmax[:, :], 0.0)
                for j in range(T):
                    chain.did(dve.match_replace(left[:, j, :], strike[:, j, :], prob[:, j, :], -2.0))
                chain.did(dve.reduce_sum(gsum[:, :], top[:, :, 0:2], AX.X))
                chain.settle()
                chain.did(dve.tensor_tensor(left[:, :, 0:E], left[:, :, 0:E], prob[:, :, 0:E], ALU.not_equal))
                chain.did(dve.reciprocal(gmax[:, :], gsum[:, :]))
                chain.settle()
                chain.did(dve.tensor_tensor(gexp[:, :, :], left[:, :, 0:E], prob[:, :, 0:E], ALU.mult))
                chain.settle()
                wait_from(dve, y_added, ADDS * (v - 1))
                dve.tensor_tensor(comb[i][:, :, :], gexp[:, :, :], gmax[:, :].unsqueeze(2).to_broadcast([P, T, E]),
                                  ALU.mult).then_inc(comb_ready, 1)
                chain.close()

            def front_begin(b, i):
                v = NC * b + i
                wait_from(dve, bias_made, v + 1)
                wait_from(dve, res_ready, v - 1)
                dve.tensor_tensor(acc[i][:, :, :], ps_a[:, 0, :].rearrange("p (t d) -> p t d", t=T),
                                  x1[:, :, :], ALU.add).then_inc(acc_ready, 1)

            def add(b, i, e):
                v = NC * b + i
                if e == 0:
                    wait_from(dve, acc_ready, v + 1)
                    wait_from(dve, comb_ready, v + 1)
                else:
                    wait_from(dve, y_added, ADDS * v + T * e)
                wait_from(dve, y_made, E * v + e + 1)
                for j in range(T):
                    tile = acc[i][:, j, :]
                    dve.scalar_tensor_tensor(out=tile, in0=ps_y[:, e % 2, j * D:(j + 1) * D],
                                             scalar=comb[i][:, j, e:e + 1], in1=tile,
                                             op0=ALU.mult, op1=ALU.add).then_inc(y_added, 1)

            def back_measure(b, i, chain):
                wait_from(dve, y_added, ADDS * (NC * b + i + 1))
                measure(chain, acc[i], back_stats)

            def back_norm(b, i, chain):
                v = NC * b + i
                scale(chain, acc[i], fin, back_stats, 2 * v + 1)
                chain.did(dve.tensor_tensor(fin[:, :, :], fin[:, :, :], per_row(vecs[:, 3, :]), ALU.mult))
                chain.settle()
                chain.did(dve.tensor_tensor(fin[:, :, :], fin[:, :, :], per_row(vecs[:, 4, :]), ALU.add))
                chain.settle()
                measure(chain, fin, back_stats)

            def back_output(b, i, chain):
                v = NC * b + i
                scale(chain, fin, acc[i], back_stats, 2 * v + 2)
                chain.close()
                wait_from(dve, xmid_in, 16 * (v + 1))
                dve.tensor_tensor(xmid[:, :, :], acc[i][:, :, :], xmid[:, :, :], ALU.add).then_inc(res_ready, 1)

            def chains(b, i):
                v = NC * b + i
                return Chain(dve, front_steps, v * FRONT, FRONT), Chain(dve, back_steps, v * BACK, BACK)

            def window(b, i, has_back, has_front):
                nxt, prv = following(b, i), preceding(b, i)
                front, back = chains(*nxt)[0], chains(*prv)[1]
                for e in range(E):
                    if e == 0 and has_back:
                        back_measure(*prv, back)
                    if e == 1 and has_front:
                        front_input(*nxt, front)
                    if e == 2 and has_front:
                        front_norm(*nxt, front)
                    if e == 3 and has_back:
                        back_norm(*prv, back)
                    if e == 5:
                        if has_front:
                            front_split(*nxt)
                            front_logits(*nxt, front)
                        if has_back:
                            back_output(*prv, back)
                    if e == 6 and has_front:
                        front_gate(*nxt, front)
                    add(b, i, e)
                if has_front:
                    front_begin(*nxt)

            front = chains(0, 0)[0]
            front_input(0, 0, front)
            front_norm(0, 0, front)
            front_split(0, 0)
            front_logits(0, 0, front)
            front_gate(0, 0, front)
            front_begin(0, 0)
            chunk_windows(dve, window)
            last = (B - 1, NC - 1)
            back = chains(*last)[1]
            back_measure(*last, back)
            back_norm(*last, back)
            back_output(*last, back)

        @block.scalar
        def _(act):
            act.wait_ge(weights_in, 16 * NWT)

            def root(k, nth):
                wait_from(act, k["var_ready"], nth)
                nc.scalar.activation(k["std"][:, :], k["var"][:, :], ACT.Sqrt).then_inc(k["std_ready"], 1)

            def gelu(b, i, e):
                v = NC * b + i
                for f in range(NF):
                    m = e * NF + f
                    if f == 0:
                        wait_from(act, y_made, E * v + e - 1)
                    wait_from(act, h_made, HIDS * v + m + 1)
                    nc.scalar.activation(hid[:, e % 2, f, :], ps_h[:, m % NH, :], ACT.Gelu,
                                         bias=b1[:, e, f:f + 1]).then_inc(h_ready, 1)

            def copy_x(b, i):
                v = NC * b + i
                wait_from(act, logits_made, v)
                wait_from(act, xlo_ready, v)
                wait_from(act, turned, v + 1)
                nc.scalar.copy(x_t[:, :], ps_t[:, 0, :]).then_inc(xhi_ready, 1)
                wait_from(act, h_made, HIDS * (v - 1))
                nc.scalar.copy(x_hi[i][:, :], ps_t[:, 0, :]).then_inc(xhi_ready, 1)

            def gate_exp(b, i):
                wait_from(act, shifted, NC * b + i + 1)
                nc.scalar.activation(gexp[:, :, :], logit[:, :, :], ACT.Exp).then_inc(gexp_ready, 1)

            def copy_comb(b, i):
                v = NC * b + i
                wait_from(act, bias_made, v)
                wait_from(act, comb_turned, v + 1)
                nc.scalar.copy(comb_t[:, :], ps_t[0:E, 0, :]).then_inc(comb_t_ready, 1)

            def window(b, i, has_back, has_front):
                nxt, prv = following(b, i), preceding(b, i)
                for e in range(E):
                    gelu(b, i, e)
                    if e == 1 and has_back:
                        root(back_stats, 2 * (NC * prv[0] + prv[1]) + 1)
                    if e == 2 and has_front:
                        root(front_stats, NC * nxt[0] + nxt[1] + 1)
                    if e == 4 and has_back:
                        root(back_stats, 2 * (NC * prv[0] + prv[1]) + 2)
                    if e == 4 and has_front:
                        copy_x(*nxt)
                    if e == 6 and has_front:
                        gate_exp(*nxt)
                if has_front:
                    copy_comb(*nxt)

            root(front_stats, 1)
            copy_x(0, 0)
            gate_exp(0, 0)
            copy_comb(0, 0)
            chunk_windows(act, window)
            for n in (1, 2):
                root(back_stats, 2 * (U - 1) + n)

        @block.tensor
        def _(pe):
            pe.wait_ge(weights_in, 16 * NWT)

            def out_product(b, i):
                v = NC * b + i
                wait_from(pe, acc_ready, v)
                wait_from(pe, y_in, 16 * (v + 1))
                for j in range(T):
                    for g in range(NG):
                        last = pe.matmul(ps_a[:, 0, j * D:(j + 1) * D], y[:, g, j * P:(j + 1) * P],
                                         wo[:, g, :], start=g == 0, stop=g == NG - 1)
                last.then_inc(a_made, 1)

            def turn_x1(b, i):
                v = NC * b + i
                wait_from(pe, comb_t_ready, v)
                wait_from(pe, x1_ready, v + 1)
                for j in range(T):
                    last = pe.transpose(ps_t[:, 0, j * P:(j + 1) * P], x1[:, j, :], c["ident"][:, :])
                last.then_inc(turned, 1)

            def logits(b, i):
                v = NC * b + i
                wait_from(pe, xhi_ready, 2 * (v + 1))
                for j in range(T):
                    last = pe.matmul(ps_t[:, 0, j * E:(j + 1) * E], x_t[:, j * P:(j + 1) * P], wg[:, :],
                                     start=True, stop=True)
                last.then_inc(logits_made, 1)

            def turn_comb(b, i):
                v = NC * b + i
                wait_from(pe, comb_ready, v + 1)
                for j in range(T):
                    last = pe.transpose(ps_t[0:E, 0, j * P:(j + 1) * P], comb[i][:, j, :], c["ident"][:, :])
                last.then_inc(comb_turned, 1)

            def biases(b, i):
                v = NC * b + i
                wait_from(pe, comb_t_ready, v + 1)
                for j in range(T):
                    last = pe.matmul(ps_a[:, 0, j * D:(j + 1) * D], comb_t[:, j * P:(j + 1) * P], b2[:, :],
                                     start=True, stop=True)
                last.then_inc(bias_made, 1)

            def hidden(b, i, e):
                v = NC * b + i
                if e == 0:
                    wait_from(pe, xlo_ready, v + 1)
                for f in range(NF):
                    m = e * NF + f
                    wait_from(pe, h_ready, HIDS * v + m + 1 - NH)
                    for n, (w, x) in enumerate(((w1_hi, x_hi), (w1_lo, x_hi), (w1_hi, x_lo))):
                        last = pe.matmul(ps_h[:, m % NH, :], w[:, e, f, :], x[i][:, :], start=n == 0, stop=n == 2)
                    last.then_inc(h_made, 1)

            def project(b, i, e):
                v = NC * b + i
                wait_from(pe, h_ready, HIDS * v + (e + 1) * NF)
                wait_from(pe, y_added, ADDS * v + T * (e - 1))
                for j in range(T):
                    for f in range(NF):
                        last = pe.matmul(ps_y[:, e % 2, j * D:(j + 1) * D], hid[:, e % 2, f, j * P:(j + 1) * P],
                                         w2[:, e, f, :], start=f == 0, stop=f == NF - 1)
                last.then_inc(y_made, 1)

            def window(b, i, has_back, has_front):
                nxt = following(b, i)
                hidden(b, i, 0)
                for e in range(E):
                    if e + 1 < E:
                        hidden(b, i, e + 1)
                    if has_front:
                        if e == 0:
                            out_product(*nxt)
                        if e == 3:
                            turn_x1(*nxt)
                        if e == 4:
                            logits(*nxt)
                        if e == 7:
                            turn_comb(*nxt)
                    project(b, i, e)
                if has_front:
                    biases(*nxt)

            out_product(0, 0)
            turn_x1(0, 0)
            logits(0, 0)
            turn_comb(0, 0)
            biases(0, 0)
            pe.wait_ge(w2_in, 16)
            chunk_windows(pe, window)


_OUT = ((B, L, D), "float32")


def kernel(L0_attn_x_bld, L0_attn_Wq, L0_attn_Wkv_down, L0_attn_Wk_up, L0_attn_Wv_up, L0_attn_Wout,
           L0_ffn_Wq, L0_ffn_bq, L0_ffn_Wk, L0_ffn_bk, L0_ffn_Wv, L0_ffn_bv, L0_ffn_Wo, L0_ffn_bo,
           L0_ffn_Wg, L0_ffn_bg, L0_ffn_W1, L0_ffn_b1, L0_ffn_W2, L0_ffn_b2,
           L0_ffn_g1, L0_ffn_be1, L0_ffn_g2, L0_ffn_be2):
    import concourse.bacc as _bacc
    from concourse.bass_utils import run_bass_kernel_spmd as _run

    def every_partition(*vectors):
        return np.stack([np.broadcast_to(np.asarray(v), (P, v.shape[-1])) for v in vectors], axis=1)

    k, m = np.meshgrid(np.arange(P), np.arange(P), indexing="ij")
    swap = (np.arange(D) + HD2 // 2) % HD2 + np.arange(D) // HD2 * HD2
    freq = (np.float32(1.0) / np.float32(10000.0) ** (np.arange(0, HD2, 2, dtype=np.float32) / HD2)).astype(np.float32)
    angle = (np.arange(L, dtype=np.float32)[None, :] * freq[np.arange(D) % (HD2 // 2), None]).astype(np.float32)
    sign = np.where(np.arange(D) % HD2 < HD2 // 2, -1, 1).astype(np.float32)[:, None]
    rope = np.stack([np.cos(angle), np.sin(angle) * sign], axis=1).astype(np.float32)
    wo = np.asarray(L0_ffn_Wo).reshape(NG, GH, HD2, D)
    wo = np.pad(wo, ((0, 0), (0, 0), (0, R - HD2), (0, 0)))
    laid = {
        "x": np.asarray(L0_attn_x_bld),
        "wq_t": np.asarray(L0_attn_Wq).transpose(2, 1, 0),
        "wk_t": np.asarray(L0_attn_Wk_up).transpose(2, 1, 0),
        "wv_t": np.asarray(L0_attn_Wv_up).transpose(2, 1, 0),
        "wout": np.asarray(L0_attn_Wout).transpose(1, 0, 2),
        "wkv": np.asarray(L0_attn_Wkv_down),
        "wq": np.asarray(L0_ffn_Wq), "wk": np.asarray(L0_ffn_Wk), "wv": np.asarray(L0_ffn_Wv),
        "wqs": np.asarray(L0_ffn_Wq)[:, swap], "wks": np.asarray(L0_ffn_Wk)[:, swap],
        "bqk": np.stack([np.stack([v, v[swap]], axis=1) for v in (np.asarray(L0_ffn_bq), np.asarray(L0_ffn_bk))],
                        axis=1),
        "rope": rope,
        "bv": every_partition(L0_ffn_bv)[:, 0],
        "wo": wo.transpose(1, 2, 0, 3).reshape(P, NG, D),
        "wg": np.asarray(L0_ffn_Wg),
        "w1": np.asarray(L0_ffn_W1).reshape(E, D, NF, P).transpose(1, 0, 2, 3),
        "w2": np.asarray(L0_ffn_W2).reshape(E, NF, P, D).transpose(2, 0, 1, 3),
        "b1": np.asarray(L0_ffn_b1).reshape(E, NF, P).transpose(2, 0, 1),
        "b2": np.asarray(L0_ffn_b2),
        "vecs": every_partition(L0_ffn_bo, L0_ffn_g1, L0_ffn_be1, L0_ffn_g2, L0_ffn_be2),
        "bg": every_partition(L0_ffn_bg)[:, 0],
        "ident": np.eye(P, dtype=np.float32),
        "mask_q": np.where(m > k, MASKED, 0).astype(np.float32),
        "mask_k": np.where(k > m, MASKED, 0).astype(np.float32),
        "head_rows": np.repeat(np.eye(GH, dtype=np.float32), L, axis=1),
    }
    nc = _bacc.Bacc("TRN2", target_bir_lowering=False, num_devices=1)
    arrays, t = {}, {}
    for name, a in laid.items():
        arrays[f"in_{name}"] = a = np.ascontiguousarray(a)
        t[name] = nc.dram_tensor(f"in_{name}", a.shape, mybir.dt.from_np(a.dtype), kind="ExternalInput").ap()
    t["out"] = nc.dram_tensor("out_0", _OUT[0], F32, kind="ExternalOutput").ap()
    build(nc, t)
    r = _run(nc, [arrays], core_ids=[0])
    return r.results[0]["out_0"]
```
